# Optimizing a Trainium2 kernel written in Bass

```python
import numpy as np
import jax
import jax.numpy as jnp

def _softmax(x, axis=-1):
    return jax.nn.softmax(x, axis=axis)

def _gelu(x):
    return jax.nn.gelu(x, approximate=True)

def _silu(x):
    return jax.nn.silu(x)

def _sigmoid(x):
    return jax.nn.sigmoid(x)

def _layernorm(x, axis=-1, eps=1e-05):
    m = jnp.mean(x, axis=axis, keepdims=True)
    v = jnp.var(x, axis=axis, keepdims=True)
    return (x - m) / jnp.sqrt(v + eps)

def _scatter_add(tgt, idx, src, axis=0):
    return tgt.at[idx].add(src)

def _segment_sum(src, seg, n):
    return jax.ops.segment_sum(src, seg, n)
kernel_name = 'mk_perceiver_d1_seqx_r2_bfb7d6'

def setup_inputs(seed: int=0):
    np.random.seed(seed)
    _w = jnp.asarray

    def _rec_inputs():
        import jax
        import jax.numpy as jnp
        _rk = jax.random.key(seed)
        x = 7.22e-05 + 1 * jax.random.normal(jax.random.fold_in(_rk, 1), (16, 64, 512), jnp.float32)
        _lenS = 64 - jax.random.randint(jax.random.fold_in(_rk, 7), (16,), 0, max(1, 64 // 4) + 1, jnp.int32)
        _lenS2 = 512 - jax.random.randint(jax.random.fold_in(_rk, 8), (16,), 0, max(1, 512 // 4) + 1, jnp.int32)
        _ctx_768P = jax.random.normal(jax.random.fold_in(_rk, 11), (16, 16, 384), jnp.float32)
        _ctx_768c = jax.random.dirichlet(jax.random.fold_in(_rk, 511), 0.3 * jnp.ones((16,), jnp.float32), (16, 512))
        _ctx_768t = jnp.einsum('bsk,bkd->bsd', _ctx_768c, _ctx_768P)
        _ctx_768t = _ctx_768t * jax.lax.rsqrt(jnp.mean(jnp.square(_ctx_768t)) + 1e-12) * 0.953939
        ctx_768 = -0.000191848 + 0.999787 * (_ctx_768t + 0.3 * jax.random.normal(jax.random.fold_in(_rk, 611), (16, 512, 384), jnp.float32))
        return (x, ctx_768)
    x, ctx_768 = _rec_inputs()

    def _L0_xattn_setup():
        import jax, jax.numpy as jnp
        import numpy as np
        NUM_HEADS = 16
        CLAMP = 10000.0
        key = jax.random.key(seed)
        ks = jax.random.split(key, 8)
        B, Nq, Nkv, Cq, Ckv = (4, 1024, 1024, 512, 384)
        s_q = 1.0 / np.sqrt(Cq)
        s_kv = 1.0 / np.sqrt(Ckv)
        return {'query': jax.random.normal(ks[0], (B, Nq, Cq), jnp.float32), 'key_value': jax.random.normal(ks[1], (B, Nkv, Ckv), jnp.float32), 'Wq': jax.random.normal(ks[2], (Cq, Cq), jnp.float32) * s_q, 'bq': jnp.zeros((Cq,), jnp.float32), 'Wk': jax.random.normal(ks[3], (Ckv, Cq), jnp.float32) * s_kv, 'bk': jnp.zeros((Cq,), jnp.float32), 'Wv': jax.random.normal(ks[4], (Ckv, Cq), jnp.float32) * s_kv, 'bv': jnp.zeros((Cq,), jnp.float32), 'Wo': jax.random.normal(ks[5], (Cq, Cq), jnp.float32) * s_q, 'bo': jnp.zeros((Cq,), jnp.float32)}
    _L0_xattn_all = _L0_xattn_setup()
    _L0_xattn_in = {k: v for k, v in _L0_xattn_all.items() if k in ('Wq', 'bq', 'Wk', 'bk', 'Wv', 'bv', 'Wo', 'bo')}
    del _L0_xattn_all

    def _L0_attn_setup():
        import jax, jax.numpy as jnp
        import numpy as np
        HEADS = 32
        DIM_HEAD = 32
        EPS = 1e-06
        key = jax.random.key(seed)
        k1, k2, k3 = jax.random.split(key, 3)
        b, n, dim = (2, 1024, 512)
        x = jax.random.normal(k1, (b, n, dim), dtype=jnp.float32)
        w_qkv = jax.random.normal(k2, (dim, 3 * HEADS * DIM_HEAD), dtype=jnp.float32) * dim ** (-0.5)
        w_out = jax.random.normal(k3, (HEADS * DIM_HEAD, dim), dtype=jnp.float32) * dim ** (-0.5)
        b_out = jnp.zeros((dim,), dtype=jnp.float32)
        ln_gamma = jnp.ones((dim,), dtype=jnp.float32)
        ln_beta = jnp.zeros((dim,), dtype=jnp.float32)
        return {'x': x, 'w_qkv': w_qkv, 'w_out': w_out, 'b_out': b_out, 'ln_gamma': ln_gamma, 'ln_beta': ln_beta}
    _L0_attn_all = _L0_attn_setup()
    _L0_attn_in = {k: v for k, v in _L0_attn_all.items() if k in ('w_qkv', 'w_out', 'b_out', 'ln_gamma', 'ln_beta')}
    del _L0_attn_all

    def _L0_ffn_setup():
        import jax, jax.numpy as jnp
        import numpy as np
        BITS = 8
        LORA_RANK = 16
        LORA_ALPHA = 32
        SCALING = LORA_ALPHA / LORA_RANK

        def fake_quant_weight(w, bits=BITS):
            qmax = 2.0 ** (bits - 1) - 1
            scale = jnp.max(jnp.abs(w)) / qmax
            wq = jnp.clip(jnp.round(w / scale), -qmax - 1, qmax) * scale
            return w + jax.lax.stop_gradient(wq - w)

        def qat_lora_linear(x, W, b, A, B):
            Wq = fake_quant_weight(W)
            base = jnp.einsum('bsi,oi->bso', x, Wq) + b
            lora = jnp.einsum('bsr,or->bso', jnp.einsum('bsi,ri->bsr', x, A), B)
            return base + SCALING * lora
        key = jax.random.key(seed)
        ks = jax.random.split(key, 9)
        d, f = (512, 2048)
        s_in = 1.0 / np.sqrt(d)
        s_ff = 1.0 / np.sqrt(f)
        return {'hidden_states': jax.random.normal(ks[0], (4, 1024, d), jnp.float32), 'W_fc': jax.random.normal(ks[1], (f, d), jnp.float32) * s_in, 'b_fc': jnp.zeros((f,), jnp.float32), 'A_fc': jax.random.normal(ks[2], (LORA_RANK, d), jnp.float32) * s_in, 'B_fc': jnp.zeros((f, LORA_RANK), jnp.float32), 'W_proj': jax.random.normal(ks[3], (d, f), jnp.float32) * s_ff, 'b_proj': jnp.zeros((d,), jnp.float32), 'A_proj': jax.random.normal(ks[4], (LORA_RANK, f), jnp.float32) * s_ff, 'B_proj': jnp.zeros((d, LORA_RANK), jnp.float32)}
    _L0_ffn_all = _L0_ffn_setup()
    _L0_ffn_in = {k: v for k, v in _L0_ffn_all.items() if k in ('W_fc', 'b_fc', 'A_fc', 'B_fc', 'W_proj', 'b_proj', 'A_proj', 'B_proj')}
    del _L0_ffn_all
    return {'x': x, 'ctx_768': ctx_768, 'L0_xattn_Wq': _L0_xattn_in['Wq'], 'L0_xattn_bq': _L0_xattn_in['bq'], 'L0_xattn_Wk': _L0_xattn_in['Wk'], 'L0_xattn_bk': _L0_xattn_in['bk'], 'L0_xattn_Wv': _L0_xattn_in['Wv'], 'L0_xattn_bv': _L0_xattn_in['bv'], 'L0_xattn_Wo': _L0_xattn_in['Wo'], 'L0_xattn_bo': _L0_xattn_in['bo'], 'L0_attn_w_qkv': _L0_attn_in['w_qkv'], 'L0_attn_w_out': _L0_attn_in['w_out'], 'L0_attn_b_out': _L0_attn_in['b_out'], 'L0_attn_ln_gamma': _L0_attn_in['ln_gamma'], 'L0_attn_ln_beta': _L0_attn_in['ln_beta'], 'L0_ffn_W_fc': _L0_ffn_in['W_fc'], 'L0_ffn_b_fc': _L0_ffn_in['b_fc'], 'L0_ffn_A_fc': _L0_ffn_in['A_fc'], 'L0_ffn_B_fc': _L0_ffn_in['B_fc'], 'L0_ffn_W_proj': _L0_ffn_in['W_proj'], 'L0_ffn_b_proj': _L0_ffn_in['b_proj'], 'L0_ffn_A_proj': _L0_ffn_in['A_proj'], 'L0_ffn_B_proj': _L0_ffn_in['B_proj']}

def reference(x, ctx_768, L0_xattn_Wq, L0_xattn_bq, L0_xattn_Wk, L0_xattn_bk, L0_xattn_Wv, L0_xattn_bv, L0_xattn_Wo, L0_xattn_bo, L0_attn_w_qkv, L0_attn_w_out, L0_attn_b_out, L0_attn_ln_gamma, L0_attn_ln_beta, L0_ffn_W_fc, L0_ffn_b_fc, L0_ffn_A_fc, L0_ffn_B_fc, L0_ffn_W_proj, L0_ffn_b_proj, L0_ffn_A_proj, L0_ffn_B_proj):
    import jax
    import jax.numpy as jnp

    def _L0_xattn_ref(query, key_value, Wq, bq, Wk, bk, Wv, bv, Wo, bo):
        import jax, jax.numpy as jnp
        import numpy as np
        NUM_HEADS = 16
        CLAMP = 10000.0
        B, Nq, Cq = query.shape
        Nkv = key_value.shape[1]
        H = NUM_HEADS
        D = Cq // H
        scale = D ** (-0.5)
        q = (query @ Wq + bq).reshape(B, Nq, H, D).transpose(0, 2, 1, 3)
        k = (key_value @ Wk + bk).reshape(B, Nkv, H, D).transpose(0, 2, 1, 3)
        v = (key_value @ Wv + bv).reshape(B, Nkv, H, D).transpose(0, 2, 1, 3)
        attn = jnp.einsum('bhqd,bhkd->bhqk', q, k) * scale
        attn = jnp.clip(attn, -CLAMP, CLAMP)
        attn = jax.nn.softmax(attn, axis=-1)
        attn = jnp.where(jnp.any(jnp.isnan(attn)), jnp.asarray(1.0 / Nkv, attn.dtype), attn)
        x = jnp.einsum('bhqk,bhkd->bqhd', attn, v).reshape(B, Nq, Cq)
        return x @ Wo + bo

    def _L0_attn_ref(x, w_qkv, w_out, b_out, ln_gamma, ln_beta):
        import jax, jax.numpy as jnp
        import numpy as np
        HEADS = 32
        DIM_HEAD = 32
        EPS = 1e-06
        b, n, dim = x.shape
        scale = DIM_HEAD ** (-0.5)
        qkv = x @ w_qkv
        qkv = qkv.reshape(b, n, 3, HEADS, DIM_HEAD)
        qkv = jnp.transpose(qkv, (2, 0, 3, 1, 4))
        q, k, v = (qkv[0], qkv[1], qkv[2])
        dots = jnp.einsum('bhnd,bhmd->bhnm', q, k) * scale
        attn = jax.nn.softmax(dots, axis=-1)
        out = jnp.einsum('bhnm,bhmd->bhnd', attn, v)
        out = jnp.transpose(out, (0, 2, 1, 3)).reshape(b, n, HEADS * DIM_HEAD)
        out = out @ w_out + b_out
        mu = jnp.mean(out, axis=-1, keepdims=True)
        var = jnp.mean((out - mu) ** 2, axis=-1, keepdims=True)
        out = (out - mu) / jnp.sqrt(var + EPS) * ln_gamma + ln_beta
        return out

    def _L0_ffn_ref(hidden_states, W_fc, b_fc, A_fc, B_fc, W_proj, b_proj, A_proj, B_proj):
        import jax, jax.numpy as jnp
        import numpy as np
        BITS = 8
        LORA_RANK = 16
        LORA_ALPHA = 32
        SCALING = LORA_ALPHA / LORA_RANK

        def fake_quant_weight(w, bits=BITS):
            qmax = 2.0 ** (bits - 1) - 1
            scale = jnp.max(jnp.abs(w)) / qmax
            wq = jnp.clip(jnp.round(w / scale), -qmax - 1, qmax) * scale
            return w + jax.lax.stop_gradient(wq - w)

        def qat_lora_linear(x, W, b, A, B):
            Wq = fake_quant_weight(W)
            base = jnp.einsum('bsi,oi->bso', x, Wq) + b
            lora = jnp.einsum('bsr,or->bso', jnp.einsum('bsi,ri->bsr', x, A), B)
            return base + SCALING * lora
        h = qat_lora_linear(hidden_states, W_fc, b_fc, A_fc, B_fc)
        h = jax.nn.gelu(h, approximate=False)
        h = qat_lora_linear(h, W_proj, b_proj, A_proj, B_proj)
        return h
    x = x + _L0_xattn_ref(_layernorm(x, axis=-1), ctx_768, L0_xattn_Wq, L0_xattn_bq, L0_xattn_Wk, L0_xattn_bk, L0_xattn_Wv, L0_xattn_bv, L0_xattn_Wo, L0_xattn_bo)
    x = x + _L0_attn_ref(_layernorm(x, axis=-1), L0_attn_w_qkv, L0_attn_w_out, L0_attn_b_out, L0_attn_ln_gamma, L0_attn_ln_beta)
    x = x + _L0_ffn_ref(_layernorm(x, axis=-1), L0_ffn_W_fc, L0_ffn_b_fc, L0_ffn_A_fc, L0_ffn_B_fc, L0_ffn_W_proj, L0_ffn_b_proj, L0_ffn_A_proj, L0_ffn_B_proj)
    return x

_drawn_inputs = setup_inputs


def setup_inputs(seed=0):
    import zlib

    import numpy as np

    out = dict(_drawn_inputs(seed))
    spreads = {'L0_xattn_bq': (0.0, 0.303),
     'L0_xattn_bk': (0.0, 0.8),
     'L0_xattn_bv': (0.0, 0.1),
     'L0_xattn_bo': (0.0, 0.1),
     'L0_attn_b_out': (0.0, 0.1),
     'L0_attn_ln_gamma': (1.0, 0.2),
     'L0_attn_ln_beta': (0.0, 0.1),
     'L0_ffn_b_fc': (0.0, 0.1),
     'L0_ffn_B_fc': (0.0, 0.1),
     'L0_ffn_b_proj': (0.0, 0.1),
     'L0_ffn_B_proj': (0.0, 0.1)}
    factors = {}
    for name, (base, spread) in spreads.items():
        noise = np.random.default_rng([zlib.crc32(name.encode()), seed]).standard_normal(out[name].shape)
        drawn = base * np.exp(spread * noise) if base else spread * noise
        out[name] = jnp.asarray(drawn.astype(out[name].dtype))
    for name, factor in factors.items():
        out[name] = (out[name] * factor).astype(out[name].dtype)
    return out
```

```python
from contextlib import ExitStack

import concourse.bass as bass
from concourse import mybir
from concourse.alu_op_type import AluOpType as ALU

ACT = mybir.ActivationFunctionType
F32 = mybir.dt.float32
F32R = mybir.dt.float32r
BF16 = mybir.dt.bfloat16
I32 = mybir.dt.int32
X = mybir.AxisListType.X
MAX = bass.bass_isa.ReduceOp.max

P = 128
DMA = 16
BANK = 512


def at_least(eng, sem, value):
    if isinstance(value, int) and value <= 0:
        return
    eng.wait_ge(sem, value)


class Shapes:

    def __init__(self, x, ctx, w_qkv, w_fc):
        self.B, self.Q, self.D = x.shape
        _, self.S, self.C = ctx.shape
        self.TOK = self.B * self.Q
        self.TILES = self.TOK // P
        self.DC = self.D // P
        self.CC = self.C // P
        self.SC = self.S // P
        self.F = w_fc.shape[0]
        self.INNER = w_qkv.shape[1] // 3


class Arena:

    def __init__(self, nc, base):
        self.nc, self.at = nc, base

    def place(self, name, shape, dtype, at=None):
        size = 1
        for n in shape[1:]:
            size *= n
        size *= 2 if dtype == BF16 else 4
        offset = self.at if at is None else at
        t = self.nc.alloc_sbuf_tensor_at(name, shape, dtype, offset=offset)
        if at is None:
            self.at += -(-size // 32) * 32
        return t


def three_products(pe, out, high_l, low_l, high_r, low_r, chunks):
    last = None
    n = 0
    for c in range(chunks):
        for l, r in ((high_l, high_r), (high_l, low_r), (low_l, high_r)):
            last = pe.matmul(out, l(c), r(c), start=(n == 0), stop=(n == 3 * chunks - 1))
            n += 1
    return last


def by_pair_group(w):
    return w.rearrange("(g p e d) n -> p d g e n", g=2, p=4, e=2)


def cross_attention_block(nc, sh, later, arena, resid, ident, ident_ready, ctxsum, nansum, O_all, x, ctx_in, Wq, bq, Wk, bk, Wv):
    B, Q, S, D, TOK = sh.B, sh.Q, sh.S, sh.D, sh.TOK
    DC, CC, SC, TILES = sh.DC, sh.CC, sh.SC, sh.TILES
    HEADS = 16
    DH = D // HEADS
    SCALE = DH ** -0.5
    CLAMP = 10000.0
    PAIRS = HEADS // 2
    UNITS = DC + SC
    VW = 2 * DH + 2
    HALF = TOK // 2
    base = arena.at
    with ExitStack() as st:
        def sem(name):
            return st.enter_context(nc.semaphore(name))

        def psum(name):
            return st.enter_context(nc.psum_tensor(name, [P, BANK], F32))

        place = arena.place
        wkh, wkl = place("wkh", [P, CC, D], F32R), place("wkl", [P, CC, D], F32R)
        wvh, wvl = place("wvh", [P, CC, D], F32R), place("wvl", [P, CC, D], F32R)
        qT = place("qT", [P, DC, TOK], F32)
        qdh = [place(f"qdh{i}", [P, PAIRS, P], F32R) for i in range(2)]
        qdl = [place(f"qdl{i}", [P, DC, P], F32R) for i in range(2)]
        ctx_rows = [place(f"ctx_rows{i}", [P, SC, sh.C], F32) for i in range(2)]
        cth = [place(f"cth{i}", [P, CC, S], F32R) for i in range(2)]
        ctl = [place(f"ctl{i}", [P, CC, S], F32R) for i in range(2)]
        keys0 = place("keys0", [P, PAIRS, S], F32R)
        k1 = arena.at
        keys = [keys0, place("keys1", [P, PAIRS, S], F32R)]
        vals = [place(f"vals{i}", [P, SC, PAIRS, VW], F32) for i in range(2)]
        p1 = arena.at
        probs = [place(f"probs{i}", [P, S], F32) for i in range(2)]
        probsT = [place(f"probsT{i}", [P, S], F32) for i in range(2)]
        later.at = arena.at
        later.place(arena)
        xth, xtl = place("xth", [P, DC, HALF], F32R), place("xtl", [P, DC, HALF], F32R)
        wk_raw = place("wk_raw", [P, CC, D], F32, at=k1)
        wv_raw = place("wv_raw", [P, CC, D], F32, at=k1 + 4 * CC * D)
        wq_raw = place("wq_raw", [P, DC, D], F32, at=p1)
        wqh = place("wqh", [P, DC, D], F32R, at=O_all[1])
        wql = place("wql", [P, DC, D], F32R, at=O_all[1] + 4 * DC * D)
        outs = O_all[0]
        xn = [place(f"xn{i}", [P, D], F32) for i in range(2)]
        stats = place("stats", [P, TILES, 6], F32)
        moments = place("moments", [P, TILES, 2], F32)
        std = place("std", [P, TILES], F32)
        rstd = place("rstd", [P, TILES], F32)
        bqT, bkT = place("bqT", [P, DC], F32), place("bkT", [P, DC], F32)
        bqs = place("bqs", [P, DC], F32)
        lowest = place("lowest", [P, 1], F32)
        bounds = [place(f"bounds{i}", [P, 1], F32) for i in range(2)]
        rawmax = [place(f"rawmax{i}", [P, 1], F32) for i in range(2)]
        negmax = [place(f"negmax{i}", [P, 1], F32) for i in range(2)]
        rsum = place("rsum", [P, 4], F32)
        zero = place("zero", [P, 1], F32)
        q_here = place("q_here", [P, DC, Q], F32)

        S_ps = [psum(f"S_ps{i}") for i in range(2)]
        T_ps = [psum(f"T_ps{i}") for i in range(2)]
        U_ps = [psum(f"U_ps{i}") for i in range(2)]
        O_ps, C_ps = psum("O_ps"), psum("C_ps")

        x_loaded, wk_loaded, wv_loaded, wq_loaded = sem("x_loaded"), sem("wk_loaded"), sem("wv_loaded"), sem("wq_loaded")
        bias_loaded = sem("bias_loaded")
        ctx_loaded = [sem(f"ctx_loaded{i}") for i in range(2)]
        consts_set = sem("consts_set")
        w_high, w_split = sem("xw_high"), sem("xw_split")
        bq_scaled = sem("bq_scaled")
        stat_step, var_ready, std_ready, xn_ready = sem("stat_step"), sem("var_ready"), sem("std_ready"), sem("xn_ready")
        xn_turned, xt_high, xt_low = sem("xn_turned"), sem("xt_high"), sem("xt_low")
        q_ready, q_copied = sem("q_ready"), sem("q_copied")
        ctx_turned, ctx_high, ctx_low = sem("ctx_turned"), sem("ctx_high"), sem("ctx_low")
        unit_ready, k_high, k_low, v_ready = sem("unit_ready"), sem("k_high"), sem("k_low"), sem("v_ready")
        q_taken, q_high, q_spread, q_doubled = sem("xq_taken"), sem("q_high"), sem("q_spread"), sem("q_doubled")
        scores_ready, rawmax_ready, max_ready = sem("scores_ready"), sem("rawmax_ready"), sem("max_ready")
        exp_done, clipped = sem("exp_done"), sem("clipped")
        turned, turned_copied, pv_ready = sem("turned"), sem("turned_copied"), sem("pv_ready")
        sum_inverted, out_taken = sem("sum_inverted"), sem("out_taken")

        x_rows = x.rearrange("b q d -> (b q) d").rearrange("(t p) d -> t p d", p=P)

        def own(e):
            return slice(64 * e, 64 * e + 64)

        def high_queries(par, r, rows):
            by_group = qdh[par][rows].rearrange("p (g e) n -> p g e n", e=2)
            return by_group[:, :, r // 2, 64 * (r % 2):64 * (r % 2) + Q]

        def steps(eng, step):
            step(0, 0, True, True)
            step(1, 1, True, True)
            with eng.Fori(1, B // 2 - 1) as i:
                step(i * 2, 0, True, True)
                step(i * 2 + 1, 1, True, True)
            step(B - 2, 0, True, False)
            step(B - 1, 1, False, False)

        block = st.enter_context(nc.Block())

        @block.sync
        def _(sp):
            for b in range(2):
                sp.dma_start(ctx_rows[b][:], ctx_in[b].rearrange("(c p) d -> p c d", p=P)).then_inc(ctx_loaded[b], DMA)
                if b == 0:
                    sp.dma_start(wk_raw[:], Wk.rearrange("(c p) n -> p c n", p=P)).then_inc(wk_loaded, DMA)
                    sp.dma_start(wv_raw[:], Wv.rearrange("(c p) n -> p c n", p=P)).then_inc(wv_loaded, DMA)
            for t in range(TILES):
                sp.dma_start(resid[:, t, :], x_rows[t]).then_inc(x_loaded, DMA)
            sp.dma_start(wq_raw[:], Wq.rearrange("(c p) n -> p c n", p=P)).then_inc(wq_loaded, DMA)
            with nc.allow_non_contiguous_dma(reason="two biases of 512 values, turned"):
                sp.dma_start(bqT[:], bq.rearrange("(c p) -> p c", p=P)).then_inc(bias_loaded, DMA)
                sp.dma_start(bkT[:], bk.rearrange("(c p) -> p c", p=P)).then_inc(bias_loaded, DMA)

            def fetch(b, par):
                sp.wait_ge(ctx_turned, (b - 1) * SC)
                sp.dma_start(ctx_rows[par][:], ctx_in[b].rearrange("(c p) d -> p c d", p=P)).then_inc(ctx_loaded[par], DMA)

            with sp.Fori(1, B // 2) as i:
                fetch(i * 2, 0)
                fetch(i * 2 + 1, 1)
            sp.wait_ge(q_copied, 2 * DC)
            later.fetch(sp)

        @block.gpsimd
        def _(pool):
            pool.memset(lowest[:], -CLAMP).then_inc(consts_set, 1)
            pool.memset(zero[:], 0.0).then_inc(consts_set, 1)
            for i in range(2):
                pool.memset(vals[i][:, :, :, 2 * DH:VW], 1.0).then_inc(consts_set, 1)
                pool.memset(qdh[i][:].bitcast(F32), 0.0).then_inc(consts_set, 1)
                pool.memset(qdl[i][:].bitcast(F32), 0.0).then_inc(consts_set, 1)
            pool.wait_ge(consts_set, 8)

            def step(b, par, more, turn):
                if isinstance(b, int) and b < 2:
                    pool.wait_ge(q_copied, DC)
                at_least(pool, scores_ready, (b - 1) * PAIRS)
                at_least(pool, q_spread, b * 4)
                pool.tensor_copy(q_here[:], qT[:, :, bass.ds(b * Q, Q)]).then_inc(q_taken, 1)
                pool.wait_ge(q_taken, b + 1)
                for r in range(4):
                    rows = slice(32 * r, 32 * r + 32)
                    cols = slice(64 * (r % 2), 64 * (r % 2) + Q)
                    src = q_here[rows, :, :]
                    if r > 0:
                        pool.wait_ge(q_spread, b * 4 + r)
                    pool.tensor_tensor(high_queries(par, r, rows), src, zero[rows].unsqueeze(2).to_broadcast((32, DC, Q)), ALU.add).then_inc(q_high, 1)
                    pool.wait_ge(q_high, b * 4 + r + 1)
                    pool.tensor_tensor(qdl[par][rows, :, cols], src, high_queries(par, r, rows).bitcast(F32), ALU.subtract).then_inc(q_spread, 1)
                pool.wait_ge(q_spread, b * 4 + 4)

            steps(pool, step)

        @block.scalar
        def _(act):
            def split(raw, high, loaded):
                act.wait_ge(loaded, DMA)
                act.copy(high[:], raw[:]).then_inc(w_high, 1)

            def ctx_chunk(b, par, c):
                act.wait_ge(ctx_turned, b * SC + c + 1)
                act.copy(cth[par][:, :, c * P:(c + 1) * P], C_ps[:, 0:CC * P].rearrange("p (c t) -> p c t", c=CC)).then_inc(ctx_high, 1)

            def unit(b, par, u):
                act.wait_ge(unit_ready, b * UNITS + u + 1)
                if u < DC:
                    for e in range(2):
                        act.activation(keys[par][own(e), 2 * u + e, :], U_ps[u % 2][own(e), :], ACT.Identity, bias=bkT[own(e), u:u + 1]).then_inc(k_high, 1)
                else:
                    act.copy(vals[par][:, u - DC, :, 0:2 * DH], U_ps[u % 2][:].rearrange("p (h e) -> p h e", h=PAIRS)).then_inc(v_ready, 1)

            split(wk_raw, wkh, wk_loaded)
            for c in range(SC):
                ctx_chunk(0, 0, c)
            split(wv_raw, wvh, wv_loaded)
            act.wait_ge(var_ready, 1)
            act.activation(std[:], moments[:, :, 1], ACT.Sqrt).then_inc(std_ready, 1)
            act.wait_ge(bias_loaded, 2 * DMA)
            act.wait_ge(consts_set, 8)
            for u in range(UNITS):
                unit(0, 0, u)
            split(wq_raw, wqh, wq_loaded)
            for c in range(SC):
                ctx_chunk(1, 1, c)
            act.wait_ge(bq_scaled, 1)
            for h in range(2):
                for t in range(TILES // 2):
                    n = h * (TILES // 2) + t
                    act.wait_ge(xn_turned, n + 1)
                    act.copy(xth[:, :, t * P:(t + 1) * P], S_ps[t % 2][:].rearrange("p (c t) -> p c t", c=DC)).then_inc(xt_high, 1)
                for m in range(DC):
                    act.wait_ge(q_ready, h * DC + m + 1)
                    act.activation(qT[:, m, h * HALF:(h + 1) * HALF], U_ps[m % 2][:], ACT.Identity, bias=bqs[:, m:m + 1], scale=SCALE).then_inc(q_copied, 1)

            def double_queries(b, par):
                act.wait_ge(q_spread, b * 4 + 4)
                for r in range(4):
                    rows, other = slice(32 * r, 32 * r + 32), slice(32 * (r ^ 2), 32 * (r ^ 2) + 32)
                    act.copy(high_queries(par, r, other), high_queries(par, r, rows).bitcast(F32)).then_inc(q_doubled, 1)

            double_queries(0, 0)

            def step(b, par, more, turn):
                first = isinstance(b, int) and b == 0
                for j in range(PAIRS):
                    n = b * PAIRS + j
                    if j == 0 and not first:
                        unit(b, par, UNITS - 1)
                    if j > 0 and more:
                        unit(b + 1, 1 - par, j - 1)
                    if turn and j >= PAIRS - SC:
                        ctx_chunk(b + 2, par, j - PAIRS + SC)
                    act.wait_ge(max_ready, n + 1)
                    at_least(act, turned, n - 1)
                    act.activation(bounds[j % 2][:], lowest[:], ACT.Exp, bias=negmax[j % 2][:])
                    act.activation(probs[j % 2][:], S_ps[j % 2][:], ACT.Exp, bias=negmax[j % 2][:],
                                   accum_out=nansum[:, bass.ds(n, 1)]).then_inc(exp_done, 1)
                    if j == 6 and more:
                        double_queries(b + 1, 1 - par)

            steps(act, step)

        @block.vector
        def _(dve):
            def split(raw, high, low, n):
                dve.wait_ge(w_high, n)
                dve.tensor_tensor(low[:], raw[:], high[:].bitcast(F32), ALU.subtract).then_inc(w_split, 1)

            def ctx_chunk(b, par, c):
                dve.wait_ge(ctx_high, b * SC + c + 1)
                turned_ctx = C_ps[:, 0:CC * P].rearrange("p (c t) -> p c t", c=CC)
                dve.tensor_reduce(ctxsum[:, bass.ds(b, 1), c, :].rearrange("p b c -> p (b c)"), turned_ctx, X, ALU.add).then_inc(ctx_low, 1)
                dve.tensor_tensor(ctl[par][:, :, c * P:(c + 1) * P], turned_ctx, cth[par][:, :, c * P:(c + 1) * P].bitcast(F32), ALU.subtract).then_inc(ctx_low, 1)

            def unit(b, par, u):
                if u < DC:
                    dve.wait_ge(k_high, (b * DC + u + 1) * 2)
                    for e in range(2):
                        dve.scalar_tensor_tensor(keys[par][own(1 - e), 2 * u + e, :], U_ps[u % 2][own(e), :], bkT[own(e), u:u + 1],
                                                 keys[par][own(e), 2 * u + e, :].bitcast(F32), ALU.add, ALU.subtract).then_inc(k_low, 1)

            split(wk_raw, wkh, wkl, 1)
            for c in range(SC):
                ctx_chunk(0, 0, c)
            split(wv_raw, wvh, wvl, 2)
            for t in range(TILES):
                dve.wait_ge(x_loaded, DMA * TILES)
                dve.bn_stats(stats[:, t, :], resid[:, t, :]).then_inc(stat_step, 1)
            for t in range(TILES):
                dve.wait_ge(stat_step, t + 1)
                dve.bn_aggr(moments[:, t, :], stats[:, t, :]).then_inc(stat_step, 1)
            dve.wait_ge(stat_step, 2 * TILES)
            dve.tensor_scalar(moments[:, :, 1], moments[:, :, 1], 1e-5, None, ALU.add).then_inc(var_ready, 1)
            for u in range(UNITS):
                unit(0, 0, u)
            split(wq_raw, wqh, wql, 3)
            for c in range(SC):
                ctx_chunk(1, 1, c)
            dve.tensor_scalar(bqs[:], bqT[:], SCALE, None, ALU.mult).then_inc(bq_scaled, 1)
            dve.wait_ge(std_ready, 1)
            dve.reciprocal(rstd[:], std[:]).then_inc(stat_step, 1)
            dve.wait_ge(stat_step, 2 * TILES + 1)

            def norm(n):
                at_least(dve, xn_turned, n - 1)
                dve.tensor_scalar(xn[n % 2][:], resid[:, n, :], moments[:, n, 0:1], rstd[:, n:n + 1], ALU.subtract, ALU.mult).then_inc(xn_ready, 1)

            norm(0)
            for h in range(2):
                for t in range(TILES // 2):
                    n = h * (TILES // 2) + t
                    if n + 1 < TILES:
                        norm(n + 1)
                    dve.wait_ge(xt_high, n + 1)
                    dve.tensor_tensor(xtl[:, :, t * P:(t + 1) * P], S_ps[t % 2][:].rearrange("p (c t) -> p c t", c=DC),
                                      xth[:, :, t * P:(t + 1) * P].bitcast(F32), ALU.subtract).then_inc(xt_low, 1)

            def clamp(n, par):
                dve.wait_ge(exp_done, n + 1)
                dve.tensor_scalar(probs[par][:], probs[par][:], 1.0, bounds[par][:], ALU.min, ALU.max).then_inc(clipped, 1)

            def copy_turned(n, par):
                dve.wait_ge(turned, n + 1)
                dve.tensor_copy(probsT[par][:], T_ps[par][:]).then_inc(turned_copied, 1)

            def take_outputs(b, half):
                g = b * 2 + half
                dve.wait_ge(pv_ready, g * 4 + 4)
                o = O_ps[:, 0:4 * (VW - 1)].rearrange("p (h e) -> p h e", h=4)
                dve.reciprocal(rsum[:], o[:, :, 2 * DH]).then_inc(sum_inverted, 1)
                dve.wait_ge(sum_inverted, g + 1)
                for e in range(2):
                    rows = slice(64 * e, 64 * e + 64)
                    dst = outs[rows, bass.ds(b, 1), half * P:(half + 1) * P].rearrange("p b (h e) -> p (b h) e", h=4)
                    dve.tensor_tensor(dst, o[rows, :, e * DH:(e + 1) * DH],
                                      rsum[rows].unsqueeze(2).to_broadcast((64, 4, DH)), ALU.mult).then_inc(out_taken, 1)

            def step(b, par, more, turn):
                first = isinstance(b, int) and b == 0
                for j in range(PAIRS):
                    n = b * PAIRS + j
                    if not (first and j == 0):
                        clamp(n - 1, (j - 1) % 2)
                    dve.wait_ge(scores_ready, n + 1)
                    dve.tensor_reduce(rawmax[j % 2][:], S_ps[j % 2][:], X, ALU.max, negate=True).then_inc(rawmax_ready, 1)
                    dve.wait_ge(rawmax_ready, n + 1)
                    dve.tensor_scalar(negmax[j % 2][:], rawmax[j % 2][:], CLAMP, -CLAMP, ALU.min, ALU.max).then_inc(max_ready, 1)
                    if j > 0 and more:
                        unit(b + 1, 1 - par, j - 1)
                    if turn and j >= PAIRS - SC:
                        ctx_chunk(b + 2, par, j - PAIRS + SC)
                    if not (first and j == 0):
                        copy_turned(n - 1, (j - 1) % 2)
                    if j == 1 and not first:
                        take_outputs(b - 1, 1)
                    if j == 5:
                        take_outputs(b, 0)

            steps(dve, step)
            clamp(B * PAIRS - 1, 1)
            copy_turned(B * PAIRS - 1, 1)
            take_outputs(B - 1, 1)

        @block.tensor
        def _(pe):
            def ctx_chunk(b, par, c):
                if c == 0:
                    if par == 0:
                        pe.wait_ge(ctx_loaded[0], (b // 2 + 1) * DMA if isinstance(b, int) else b * (DMA // 2) + DMA)
                    else:
                        pe.wait_ge(ctx_loaded[1], (b // 2 + 1) * DMA if isinstance(b, int) else b * (DMA // 2) + DMA // 2)
                at_least(pe, ctx_low, (b * SC + c) * 2)
                for d in range(CC):
                    mm = pe.transpose(C_ps[:, d * P:(d + 1) * P], ctx_rows[par][:, c, d * P:(d + 1) * P], ident[:])
                mm.then_inc(ctx_turned, 1)

            def unit(b, par, u, part):
                out = U_ps[u % 2][:]
                if part == 0:
                    if u == 0:
                        pe.wait_ge(ctx_low, (b * SC + SC) * 2)
                    if u in (0, 1):
                        at_least(pe, v_ready, b * SC - 1 + u)
                    elif u - 2 < DC:
                        pe.wait_ge(k_low, (b * DC + u - 1) * 2)
                    else:
                        pe.wait_ge(v_ready, b * SC + u - 1 - DC)
                if u < DC:
                    cols = slice(u * P, (u + 1) * P)
                    ops = [(wkh[:, c, cols], cth[par][:, c, :]) for c in range(CC)]
                    ops += [(wkh[:, c, cols], ctl[par][:, c, :]) for c in range(CC)]
                    ops += [(wkl[:, c, cols], cth[par][:, c, :]) for c in range(CC)]
                else:
                    cols = slice((u - DC) * P, (u - DC + 1) * P)
                    ops = [(cth[par][:, c, cols], wvh[:, c, :]) for c in range(CC)]
                    ops += [(cth[par][:, c, cols], wvl[:, c, :]) for c in range(CC)]
                    ops += [(ctl[par][:, c, cols], wvh[:, c, :]) for c in range(CC)]
                cut = 5
                for k in range(cut) if part == 0 else range(cut, len(ops)):
                    mm = pe.matmul(out, ops[k][0], ops[k][1], start=(k == 0), stop=(k == len(ops) - 1))
                if part == 1:
                    mm.then_inc(unit_ready, 1)

            pe.wait_ge(ident_ready, 2)
            for c in range(SC):
                ctx_chunk(0, 0, c)
            pe.wait_ge(w_split, 1)
            for u in range(UNITS):
                if u == DC:
                    pe.wait_ge(w_split, 2)
                unit(0, 0, u, 0)
                unit(0, 0, u, 1)
            for c in range(SC):
                ctx_chunk(1, 1, c)
            for h in range(2):
                for t in range(TILES // 2):
                    n = h * (TILES // 2) + t
                    pe.wait_ge(xn_ready, n + 1)
                    at_least(pe, xt_low, n - 1)
                    for c in range(DC):
                        mm = pe.transpose(S_ps[t % 2][:, c * P:(c + 1) * P], xn[n % 2][:, c * P:(c + 1) * P], ident[:])
                    mm.then_inc(xn_turned, 1)
                pe.wait_ge(xt_low, (h + 1) * (TILES // 2))
                pe.wait_ge(w_split, 3)
                for m in range(DC):
                    k = h * DC + m
                    if k < 2:
                        pe.wait_ge(v_ready, SC)
                    else:
                        pe.wait_ge(q_copied, k - 1)
                    three_products(pe, U_ps[m % 2][:], lambda c: wqh[:, c, m * P:(m + 1) * P], lambda c: wql[:, c, m * P:(m + 1) * P],
                                   lambda c: xth[:, c, :], lambda c: xtl[:, c, :], DC).then_inc(q_ready, 1)
            pe.wait_ge(q_copied, 2 * DC)

            def scores(b, par, j):
                n = b * PAIRS + j
                g, rows = j // 2, slice(64 * (j % 2), 64 * (j % 2) + 64)
                if j == 0:
                    pe.wait_ge(q_spread, b * 4 + 4)
                    pe.wait_ge(q_doubled, b * 4 + 4)
                if j % 2 == 0:
                    pe.wait_ge(k_low, (b * DC + g + 1) * 2)
                at_least(pe, exp_done, n - 1)
                out = S_ps[j % 2][:]
                pe.matmul(out, qdh[par][:, j, :], keys[par][:, j, :], start=True, stop=False)
                pe.matmul(out, qdl[par][rows, g, :], keys[par][rows, j, :], start=False, stop=True).then_inc(scores_ready, 1)

            def turn_probs(n, par):
                pe.wait_ge(clipped, n + 1)
                at_least(pe, turned_copied, n - 1)
                for c in range(SC):
                    mm = pe.transpose(T_ps[par][:, c * P:(c + 1) * P], probs[par][:, c * P:(c + 1) * P], ident[:])
                mm.then_inc(turned, 1)

            def weighted_values(b, vpar, j):
                n = b * PAIRS + j
                pe.wait_ge(turned_copied, n + 1)
                if j == 0:
                    pe.wait_ge(v_ready, b * SC + SC)
                if j % 4 == 0:
                    at_least(pe, out_taken, b * 4 + j // 2)
                w = VW - 1
                for c in range(SC):
                    mm = pe.matmul(O_ps[:, (j % 4) * w:(j % 4 + 1) * w], probsT[j % 2][:, c * P:(c + 1) * P], vals[vpar][:, c, j, 0:w],
                                   start=(c == 0), stop=(c == SC - 1))
                mm.then_inc(pv_ready, 1)

            def step(b, par, more, turn):
                first = isinstance(b, int) and b == 0
                for j in range(PAIRS):
                    n = b * PAIRS + j
                    scores(b, par, j)
                    if more:
                        unit(b + 1, 1 - par, j, 0)
                    if not (first and j < 1):
                        turn_probs(n - 1, (j - 1) % 2)
                    if j >= 2:
                        weighted_values(b, par, j - 2)
                    elif not first:
                        weighted_values(b - 1, 1 - par, PAIRS + j - 2)
                    if more:
                        unit(b + 1, 1 - par, j, 1)
                    if turn and PAIRS - SC - 1 <= j < PAIRS - 1:
                        ctx_chunk(b + 2, par, j - PAIRS + SC + 1)

            steps(pe, step)
            turn_probs(B * PAIRS - 1, 1)
            weighted_values(B - 1, 1, PAIRS - 2)
            weighted_values(B - 1, 1, PAIRS - 1)
    arena.at = base


class CrossWeights:

    def __init__(self, nc, sh, st, arena, Wv, bv, Wo, bo):
        self.nc, self.sh, self.Wv, self.bv, self.Wo, self.bo = nc, sh, Wv, bv, Wo, bo
        self.bvT = arena.place("bvT", [P, sh.DC], F32)
        self.bo_rows = arena.place("bo_rows", [P, sh.D], F32)
        self.wo_loaded = st.enter_context(nc.semaphore("wo_loaded"))
        self.wv_loaded = st.enter_context(nc.semaphore("wv_again"))
        self.bv_loaded = st.enter_context(nc.semaphore("bv_loaded"))
        self.bo_loaded = st.enter_context(nc.semaphore("bo_loaded"))

    def place(self, arena):
        sh = self.sh
        self.wo_raw = arena.place("wo_raw", [P, sh.DC, sh.D], F32, at=self.at)
        self.wv = arena.place("wv_all", [P, sh.CC, sh.D], F32, at=self.at + 4 * sh.DC * sh.D)

    def fetch(self, sp):
        wo = by_pair_group(self.Wo)
        bv = by_pair_group(self.bv.rearrange("(n o) -> n o", o=1))
        for p in range(4):
            rows = slice(32 * p, 32 * p + 32)
            for g in range(2):
                sp.dma_start(self.wo_raw[rows, 2 * g:2 * g + 2, :], wo[p][:, g]).then_inc(self.wo_loaded, DMA)
        sp.dma_start(self.wv[:], self.Wv.rearrange("(c p) n -> p c n", p=P)).then_inc(self.wv_loaded, DMA)
        with self.nc.allow_non_contiguous_dma(reason="a bias of 512 values, turned"):
            for p in range(4):
                rows = slice(32 * p, 32 * p + 32)
                for g in range(2):
                    sp.dma_start(self.bvT[rows, 2 * g:2 * g + 2], bv[p][:, g, :, 0]).then_inc(self.bv_loaded, DMA)
        sp.dma_start(self.bo_rows[:], self.bo.partition_broadcast(P)).then_inc(self.bo_loaded, DMA)


class FeedForwardWeights:
    QMAX = 127.0
    MAGIC = 1.5 * 2.0 ** 23
    LORA = 2.0
    PARTS = 8

    def __init__(self, nc, sh, st, arena, W_fc, W_proj):
        self.sh, self.W_fc, self.W_proj = sh, W_fc, W_proj
        self.scale, self.inv, self.twice = (arena.place(name, [P, 2], F32) for name in ("wscale", "winv", "wtwice"))
        self.absmax = arena.place("absmax", [P, 2, self.PARTS], F32)
        self.wmax, self.allmax = arena.place("wmax", [P, 2], F32), arena.place("allmax", [P, 2], F32)
        self.fc_tiles = sh.TILES // 2
        self.late = sh.TILES - 3
        self.loaded = [st.enter_context(nc.semaphore(f"ffw_loaded{i}")) for i in range(2)]
        self.loaded_late = st.enter_context(nc.semaphore("ffw_loaded_late"))
        self.rounded = st.enter_context(nc.semaphore("ffw_rounded"))
        self.clipped = st.enter_context(nc.semaphore("ffw_clipped"))

    def part(self, n):
        if n < self.PARTS:
            return self.W_fc.rearrange("(k p a) d -> k p (a d)", k=self.PARTS, p=P)[n]
        n -= self.PARTS
        half = self.sh.F // 2
        return self.W_proj[(n // 2) * P:(n // 2 + 1) * P, (n % 2) * half:(n % 2 + 1) * half]

    def fetch(self, sp, qk, t):
        done = self.loaded_late if t >= self.late else self.loaded[t % 2]
        for i in range(4):
            if t < 4:
                src = self.W_fc[(4 * t + i) * P:(4 * t + i + 1) * P, :]
            else:
                src = self.W_proj[i * P:(i + 1) * P, (t - 4) * BANK:(t - 3) * BANK]
            sp.dma_start(qk[:, 4 * i:4 * i + 4, t * P:(t + 1) * P], src.rearrange("p (c n) -> p c n", c=4)).then_inc(done, DMA)

    def round(self, act, qk, t, i, w):
        piece = qk[:, 4 * i:4 * i + 4, bass.ds(t * P, P)]
        act.activation(piece, piece, ACT.Copy, scale=self.inv[:, w:w + 1], bias=self.MAGIC).then_inc(self.rounded, 1)

    def clip(self, eng, qk, t, i, done):
        piece = qk[:, 4 * i:4 * i + 4, bass.ds(t * P, P)]
        eng.tensor_scalar(piece, piece, self.MAGIC + self.QMAX, self.MAGIC - self.QMAX - 1, ALU.min, ALU.max).then_inc(done, 1)


def latent_block(nc, sh, later, ffw, arena, resid, ident, ctxsum, nansum, O_all, w_qkv, ln_beta):
    D, TOK, TILES, DC, CC, SC, B, Q = sh.D, sh.TOK, sh.TILES, sh.DC, sh.CC, sh.SC, sh.B, sh.Q
    INNER = sh.INNER
    COLS = 512
    WBLOCKS = 3 * INNER // COLS
    QK = 2 * INNER // COLS
    G = INNER // P
    HEADS = INNER // 32
    VW = 33
    HALF = TOK // 2
    base = arena.at
    with ExitStack() as st:
        def sem(name):
            return st.enter_context(nc.semaphore(name))

        def psum(name):
            return st.enter_context(nc.psum_tensor(name, [P, BANK], F32))

        place = arena.place
        region = O_all[1]
        arena.at = region
        qk = place("qk", [P, 2 * G, TOK], F32)
        early = Arena(nc, region + 16 * 1024)
        woh, wol = early.place("woh", [P, DC, D], F32R), early.place("wol", [P, DC, D], F32R)
        at = [early.place(f"at{i}", [P, D], F32) for i in range(2)]
        ath = [early.place(f"ath{i}", [P, DC, P], F32R) for i in range(2)]
        atl = [early.place(f"atl{i}", [P, DC, P], F32R) for i in range(2)]
        xn = [early.place(f"lxn{i}", [P, D], F32) for i in range(2)]
        ctxmean = early.place("ctxmean", [P, B, CC], F32)
        uniform = early.place("uniform", [P, DC, B], F32)
        isnan = early.place("isnan", [P, nansum.shape[1]], F32)
        anynan = early.place("anynan", [P, 1], F32)
        flag = early.place("flag", [P, 1], F32)
        assert early.at <= region + 64 * 1024
        xnh, xnl = place("xnh", [P, DC, TOK], F32R), place("xnl", [P, DC, TOK], F32R)
        w_at = arena.at
        w_raw = [place(f"w_raw{i}", [P, DC, COLS], F32) for i in range(2)]
        wh = [place(f"wh{i}", [P, DC, COLS], F32R) for i in range(2)]
        wl = [place(f"wl{i}", [P, DC, COLS], F32R) for i in range(2)]
        vals = place("lvals", [P, TILES, HEADS, VW], F32)
        stats = place("lstats", [P, TILES, 6], F32)
        moments = place("lmoments", [P, TILES, 2], F32)
        std = place("lstd", [P, TILES], F32)
        rstd = place("lrstd", [P, TILES], F32)
        beta_rows = place("beta_rows", [P, D], F32)
        part = [place(f"ffw_part{i}", [P, 1024], F32) for i in range(2)]
        kbd = [place(f"kbd{i}", [P, G // 2, 2, 4, Q], F32, at=w_at + 8 * 1024 * i) for i in range(2)]
        qt = [place(f"qt{i}", [P, G // 2, P], F32, at=w_at + 16 * 1024 + 2 * 1024 * i) for i in range(2)]
        assert arena.at <= 229368, arena.at

        A_ps = [psum(f"A_ps{i}") for i in range(2)]
        Y_ps = [psum(f"Y_ps{i}") for i in range(2)]
        N_ps = [psum(f"N_ps{i}") for i in range(2)]
        U_ps = [psum(f"LU_ps{i}") for i in range(2)]

        wo_high, wo_split = sem("wo_high"), sem("wo_split")
        w_loaded = [sem(f"w_loaded{i}") for i in range(2)]
        w_high, w_split_early, w_split = sem("w_high"), sem("w_split_early"), sem("w_split")
        ones_set = sem("ones_set")
        nan_step, any_ready, flag_ready = sem("nan_step"), sem("any_ready"), sem("flag_ready")
        mean_step, uniform_turned, uniform_ready = sem("mean_step"), sem("uniform_turned"), sem("uniform_ready")
        bo_added = sem("bo_added")
        out_turned, at_step, at_high, at_low = sem("out_turned"), sem("at_step"), sem("at_high"), sem("at_low")
        y_ready, x_ready = sem("y_ready"), sem("x_ready")
        ln_step, var_ready, std_ready, rstd_ready, xn_ready = sem("ln_step"), sem("lvar_ready"), sem("lstd_ready"), sem("lrstd_ready"), sem("lxn_ready")
        xn_turned, xt_high, xt_low = sem("lxn_turned"), sem("lxt_high"), sem("lxt_low")
        unit_ready, unit_copied = sem("lunit_ready"), sem("lunit_copied")
        beta_loaded, beta_added, kbd_step = sem("beta_loaded"), sem("beta_added"), sem("kbd_step")
        part_loaded, part_seen = [sem(f"part_loaded{i}") for i in range(2)], sem("part_seen")
        wmax_ready, allmax_ready, scale_step = sem("wmax_ready"), sem("allmax_ready"), sem("scale_step")

        UNITS = 8
        block = st.enter_context(nc.Block())

        @block.sync
        def _(sp):
            for k in range(WBLOCKS):
                if 2 <= k < 4:
                    sp.wait_ge(w_split_early, 4 * (k - 1))
                at_least(sp, w_split, k - 3)
                src = w_qkv[:, k * COLS:(k + 1) * COLS].rearrange("(c p) n -> p c n", p=P)
                sp.dma_start(w_raw[k % 2][:], src).then_inc(w_loaded[k % 2], DMA)
                if k == 0:
                    sp.dma_start(beta_rows[:], ln_beta.partition_broadcast(P)).then_inc(beta_loaded, DMA)
                for n in range(*{WBLOCKS - 3: (0, 5), WBLOCKS - 2: (5, 10), WBLOCKS - 1: (10, 2 * ffw.PARTS)}.get(k, (0, 0))):
                    at_least(sp, part_seen, n - 1)
                    sp.dma_start(part[n % 2][:], ffw.part(n)).then_inc(part_loaded[n % 2], DMA)

        @block.gpsimd
        def _(pool):
            def split_piece(n):
                k, c = n // 4, n % 4
                pool.wait_ge(w_high, n + 1)
                pool.tensor_tensor(wl[k][:, c, :], w_raw[k][:, c, :], wh[k][:, c, :].bitcast(F32), ALU.subtract).then_inc(w_split_early, 1)

            pool.wait_ge(later.bo_loaded, DMA)
            for t in range(TILES):
                pool.tensor_tensor(resid[:, t, :], resid[:, t, :], later.bo_rows[:], ALU.add).then_inc(bo_added, 1)
                if t == 0:
                    pool.wait_ge(any_ready, 1)
                    pool.partition_all_reduce(flag[:], anynan[:], P, MAX).then_inc(flag_ready, 1)
                if t >= 1:
                    split_piece(t - 1)
                pool.wait_ge(at_high, t + 1)
                at_least(pool, y_ready, t - 1)
                pool.tensor_tensor(atl[t % 2][:].rearrange("p k (b q) -> p b k q", b=2), at[t % 2][:].rearrange("p (b k q) -> p b k q", b=2, k=DC),
                                   ath[t % 2][:].bitcast(F32).rearrange("p k (b q) -> p b k q", b=2), ALU.subtract).then_inc(at_low, 1)
            split_piece(2 * DC - 1)
            pool.wait_ge(beta_loaded, DMA)
            pool.wait_ge(xn_ready, TILES)
            for t in range(TILES):
                pool.tensor_tensor(resid[:, t, :], resid[:, t, :], beta_rows[:], ALU.add).then_inc(beta_added, 1)
            pool.wait_ge(w_split, WBLOCKS - 2)
            for i in range(2):
                pool.memset(kbd[i][:], 0.0).then_inc(kbd_step, 1)
            pool.wait_ge(unit_copied, QK * UNITS)
            for f in range(2):
                for r in range(4):
                    pool.wait_ge(kbd_step, 2 + 4 * f + r)
                    spread(pool.tensor_copy, qk, kbd, 0, f, r).then_inc(kbd_step, 1)
            pool.wait_ge(kbd_step, 10)
            pool.wait_ge(unit_ready, (WBLOCKS - 1) * UNITS)
            for f in range(2):
                pool.tensor_copy(qt[f][:], qk[:, f * (G // 2):(f + 1) * (G // 2), 0:P]).then_inc(kbd_step, 1)
            for w in range(2):
                pool.wait_ge(wmax_ready, w + 1)
                pool.partition_all_reduce(ffw.allmax[:, w:w + 1], ffw.wmax[:, w:w + 1], P, MAX).then_inc(allmax_ready, 1)

        @block.scalar
        def _(act):
            def root(t):
                act.wait_ge(var_ready, t + 1)
                act.activation(std[:, t:t + 1], moments[:, t, 1:2], ACT.Sqrt).then_inc(std_ready, 1)

            def high(t):
                act.wait_ge(xn_turned, t + 1)
                act.copy(xnh[:, :, t * P:(t + 1) * P], N_ps[t % 2][:].rearrange("p (c t) -> p c t", c=DC)).then_inc(xt_high, 1)

            def split_high(k):
                act.wait_ge(w_loaded[k % 2], (k // 2 + 1) * DMA)
                at_least(act, unit_ready, (k - 1) * UNITS)
                act.copy(wh[k % 2][:], w_raw[k % 2][:]).then_inc(w_high, DC)

            act.wait_ge(later.wo_loaded, 8 * DMA)
            act.copy(woh[:], later.wo_raw[:]).then_inc(wo_high, 1)
            def outputs_high(t):
                act.wait_ge(at_step, 2 * t + 2)
                at_least(act, y_ready, t - 1)
                act.copy(ath[t % 2][:].rearrange("p k (b q) -> p b k q", b=2), at[t % 2][:].rearrange("p (b k q) -> p b k q", b=2, k=DC)).then_inc(at_high, 1)

            outputs_high(0)
            for t in range(TILES):
                if t + 1 < TILES:
                    outputs_high(t + 1)
                k, c = t // 4, t % 4
                act.wait_ge(w_loaded[k], DMA)
                act.copy(wh[k][:, c, :], w_raw[k][:, c, :]).then_inc(w_high, 1)
                if t >= 1:
                    root(t - 1)
                if t >= 2:
                    high(t - 2)
            root(TILES - 1)
            high(TILES - 2)
            high(TILES - 1)
            for n in range(WBLOCKS * UNITS):
                if n % UNITS == 0 and UNITS <= n < (WBLOCKS - 1) * UNITS:
                    split_high(n // UNITS + 1)
                act.wait_ge(unit_ready, n + 1)
                if n < QK * UNITS:
                    m, h = n // 2, n % 2
                    act.copy(qk[:, m, h * HALF:(h + 1) * HALF], U_ps[n % 2][:]).then_inc(unit_copied, 1)
                else:
                    if n == QK * UNITS:
                        act.wait_ge(ones_set, 1)
                    vb, t = (n - QK * UNITS) // UNITS, n % UNITS
                    act.copy(vals[:, t, vb * 16:(vb + 1) * 16, 0:32], U_ps[n % 2][:].rearrange("p (h e) -> p h e", h=16)).then_inc(unit_copied, 1)

        @block.vector
        def _(dve):
            dve.tensor_tensor(isnan[:], nansum[:], nansum[:], ALU.not_equal).then_inc(nan_step, 1)
            dve.tensor_reduce(ctxmean[:], ctxsum[:].rearrange("p b s c -> p b c s"), X, ALU.add).then_inc(mean_step, 1)
            dve.wait_ge(nan_step, 1)
            dve.tensor_reduce(anynan[:], isnan[:], X, ALU.max).then_inc(any_ready, 1)
            dve.wait_ge(mean_step, 1)
            dve.tensor_scalar(ctxmean[:], ctxmean[:], 1.0 / sh.S, None, ALU.mult).then_inc(mean_step, 1)
            dve.wait_ge(wo_high, 1)
            dve.tensor_tensor(wol[:], later.wo_raw[:], woh[:].bitcast(F32), ALU.subtract).then_inc(wo_split, 1)
            dve.wait_ge(uniform_turned, 1)
            dve.wait_ge(later.bv_loaded, 8 * DMA)
            dve.tensor_tensor(uniform[:], Y_ps[1][:, 0:DC * B].rearrange("p (k b) -> p k b", k=DC),
                              later.bvT[:].unsqueeze(2).to_broadcast((P, DC, B)), ALU.add).then_inc(uniform_ready, 1)
            dve.wait_ge(uniform_ready, 1)
            dve.wait_ge(flag_ready, 1)

            def outputs(t):
                dve.wait_ge(out_turned, t + 1)
                at_least(dve, at_low, t - 1)
                dst = at[t % 2][:].rearrange("p (b k q) -> p b k q", b=2, k=DC)
                src = A_ps[t % 2][:].rearrange("p (b k q) -> p b k q", b=2, k=DC)
                dve.tensor_tensor(dst, src, later.bvT[:].unsqueeze(1).unsqueeze(3).to_broadcast((P, 2, DC, Q)), ALU.add).then_inc(at_step, 1)
                dve.wait_ge(at_step, 2 * t + 1)
                dve.copy_predicated(dst, flag[:].bitcast(I32).unsqueeze(1).unsqueeze(2).to_broadcast((P, 2, DC, Q)),
                                    uniform[:, :, 2 * t:2 * t + 2].rearrange("p k b -> p b k").unsqueeze(3).to_broadcast((P, 2, DC, Q))).then_inc(at_step, 1)

            def residual(t):
                dve.wait_ge(y_ready, t + 1)
                dve.wait_ge(bo_added, t + 1)
                dve.tensor_tensor(resid[:, t, :], Y_ps[t % 2][:], resid[:, t, :], ALU.add).then_inc(x_ready, 1)
                dve.wait_ge(x_ready, t + 1)
                dve.bn_stats(stats[:, t, :], resid[:, t, :]).then_inc(ln_step, 1)
                dve.wait_ge(ln_step, 2 * t + 1)
                dve.bn_aggr(moments[:, t, :], stats[:, t, :]).then_inc(ln_step, 1)
                dve.wait_ge(ln_step, 2 * t + 2)
                dve.tensor_scalar(moments[:, t, 1:2], moments[:, t, 1:2], 1e-5, None, ALU.add).then_inc(var_ready, 1)

            def norm(t):
                dve.wait_ge(std_ready, t + 1)
                dve.reciprocal(rstd[:, t:t + 1], std[:, t:t + 1]).then_inc(rstd_ready, 1)
                dve.wait_ge(rstd_ready, t + 1)
                at_least(dve, xn_turned, t - 1)
                dve.tensor_scalar(xn[t % 2][:], resid[:, t, :], moments[:, t, 0:1], rstd[:, t:t + 1], ALU.subtract, ALU.mult).then_inc(xn_ready, 1)

            def low(t):
                dve.wait_ge(xt_high, t + 1)
                dve.tensor_tensor(xnl[:, :, t * P:(t + 1) * P], N_ps[t % 2][:].rearrange("p (c t) -> p c t", c=DC),
                                  xnh[:, :, t * P:(t + 1) * P].bitcast(F32), ALU.subtract).then_inc(xt_low, 1)

            def split_low(k):
                dve.wait_ge(w_high, (k + 1) * DC)
                at_least(dve, unit_ready, (k - 1) * UNITS)
                dve.tensor_tensor(wl[k % 2][:], w_raw[k % 2][:], wh[k % 2][:].bitcast(F32), ALU.subtract).then_inc(w_split, 1)

            outputs(0)
            for t in range(TILES + 3):
                if t + 1 < TILES:
                    outputs(t + 1)
                if 1 <= t <= TILES:
                    residual(t - 1)
                if 2 <= t <= TILES + 1:
                    norm(t - 2)
                if t >= 3:
                    low(t - 3)
            dve.memset(vals[:, :, :, VW - 1:VW], 1.0).then_inc(ones_set, 1)
            for n in range(2 * ffw.PARTS):
                w, k = n // ffw.PARTS, n % ffw.PARTS
                if n in (0, 5, 10):
                    split_low(2 + n // 5)
                dve.wait_ge(part_loaded[n % 2], (n // 2 + 1) * DMA)
                dve.tensor_reduce(ffw.absmax[:, w, k:k + 1], part[n % 2][:], X, ALU.max, apply_absolute_value=True).then_inc(part_seen, 1)
            split_low(WBLOCKS - 1)
            dve.wait_ge(part_seen, 2 * ffw.PARTS)
            for w in range(2):
                dve.tensor_reduce(ffw.wmax[:, w:w + 1], ffw.absmax[:, w, :], X, ALU.max).then_inc(wmax_ready, 1)
            dve.wait_ge(allmax_ready, 2)
            dve.tensor_scalar(ffw.scale[:], ffw.allmax[:], 1.0 / ffw.QMAX, None, ALU.mult).then_inc(scale_step, 1)
            dve.wait_ge(scale_step, 1)
            dve.reciprocal(ffw.inv[:], ffw.scale[:]).then_inc(scale_step, 1)
            dve.wait_ge(scale_step, 2)
            dve.tensor_scalar(ffw.twice[:], ffw.inv[:], ffw.LORA, None, ALU.mult).then_inc(scale_step, 1)

        @block.tensor
        def _(pe):
            pe.wait_ge(mean_step, 2)
            pe.wait_ge(later.wv_loaded, DMA)
            for k in range(DC):
                for p in range(4):
                    head = 8 * (k // 2) + 2 * p + k % 2
                    for c in range(CC):
                        mm = pe.matmul(Y_ps[1][32 * p:32 * p + 32, k * B:(k + 1) * B], later.wv[:, c, 32 * head:32 * head + 32],
                                       ctxmean[:, :, c], start=(c == 0), stop=(c == CC - 1))
            mm.then_inc(uniform_turned, 1)

            def turn_outputs(t):
                at_least(pe, at_step, 2 * t - 2)
                for b in range(2):
                    for g in range(2):
                        mm = pe.transpose(A_ps[t % 2][:, (2 * b + g) * P:(2 * b + g + 1) * P], O_all[0][:, 2 * t + b, g * P:(g + 1) * P], ident[:])
                mm.then_inc(out_turned, 1)

            def project(t):
                pe.wait_ge(at_low, t + 1)
                if t == 1:
                    pe.wait_ge(uniform_ready, 1)
                at_least(pe, x_ready, t - 1)
                three_products(pe, Y_ps[t % 2][:], lambda c: ath[t % 2][:, c, :], lambda c: atl[t % 2][:, c, :],
                               lambda c: woh[:, c, :], lambda c: wol[:, c, :], DC).then_inc(y_ready, 1)

            def turn_norm(t):
                pe.wait_ge(xn_ready, t + 1)
                at_least(pe, xt_low, t - 1)
                for c in range(DC):
                    mm = pe.transpose(N_ps[t % 2][:, c * P:(c + 1) * P], xn[t % 2][:, c * P:(c + 1) * P], ident[:])
                mm.then_inc(xn_turned, 1)

            turn_outputs(0)
            pe.wait_ge(wo_split, 1)
            for t in range(TILES + 2):
                if t + 1 < TILES:
                    turn_outputs(t + 1)
                if t < TILES:
                    project(t)
                if t >= 2:
                    turn_norm(t - 2)
            pe.wait_ge(xt_low, TILES)
            for n in range(WBLOCKS * UNITS):
                k, u = n // UNITS, n % UNITS
                par = k % 2
                if u == 0:
                    if k < 2:
                        pe.wait_ge(w_split_early, (k + 1) * DC)
                    else:
                        pe.wait_ge(w_split, k - 1)
                at_least(pe, unit_copied, n - 1)
                if k < QK:
                    cols, toks = slice((u // 2) * P, (u // 2 + 1) * P), slice((u % 2) * HALF, (u % 2 + 1) * HALF)
                    mm = three_products(pe, U_ps[n % 2][:], lambda c: wh[par][:, c, cols], lambda c: wl[par][:, c, cols],
                                        lambda c: xnh[:, c, toks], lambda c: xnl[:, c, toks], DC)
                else:
                    toks = slice(u * P, (u + 1) * P)
                    mm = three_products(pe, U_ps[n % 2][:], lambda c: xnh[:, c, toks], lambda c: xnl[:, c, toks],
                                        lambda c: wh[par][:, c, :], lambda c: wl[par][:, c, :], DC)
                mm.then_inc(unit_ready, 1)
    arena.at = base
    return qk, vals, (kbd, qt)


def spread(copy, qk, kbd, t, f, r):
    G, Q = qk.shape[1] // 2, 64
    rows = slice(32 * r, 32 * r + 32)
    g0 = G + f * (G // 2)
    src = qk[rows, g0:g0 + G // 2, bass.ds(t * P, P)].rearrange("d g (b k) -> d g b k", b=2)
    return copy(kbd[f][rows, :, :, r, :], src)


def self_attention_block(nc, sh, ffw, bout_rows, region, resid, ident, qk, vals, taken, w_out, b_out, ln_gamma):
    D, TOK, TILES, B, Q = sh.D, sh.TOK, sh.TILES, sh.B, sh.Q
    INNER = sh.INNER
    G = INNER // P
    KC = INNER // P
    OCTETS = INNER // 32 // 8
    SCALE = 32 ** -0.5
    VW = 33
    with ExitStack() as st:
        def sem(name):
            return st.enter_context(nc.semaphore(name))

        def psum(name):
            return st.enter_context(nc.psum_tensor(name, [P, BANK], F32))

        mid = Arena(nc, region + 64 * 1024)
        woh = mid.place("owh", [P, KC, D], F32R)
        wol_at = mid.at
        wol = mid.place("owl", [P, KC, D], F32R)
        wo_raw = mid.place("ow_raw", [P, KC, D], F32, at=wol_at)
        kbd, qt = taken
        mid.at += 20 * 1024
        shifted = [mid.place(f"shifted{i}", [P, BANK], F32) for i in range(2)]
        probs = [mid.place(f"sprobs{i}", [P, 8, P], F32) for i in range(2)]
        outs = mid.place("souts", [P, INNER], F32)
        oth, otl = mid.place("oth", [P, KC, P], F32R), mid.place("otl", [P, KC, P], F32R)
        y_rows = [mid.place(f"y_rows{i}", [P, D], F32) for i in range(2)]
        assert mid.at <= region + 144 * 1024
        end = Arena(nc, region + 177 * 1024)
        probsT = [end.place(f"sprobsT{i}", [P, 8, P], F32) for i in range(2)]
        gamma_rows = end.place("gamma_rows", [P, D], F32)
        y_stats = [end.place(f"y_stats{i}", [P, 6], F32) for i in range(2)]
        y_moments = end.place("y_moments", [P, 2, 2], F32)
        y_std, y_rstd = end.place("y_std", [P, 2], F32), end.place("y_rstd", [P, 2], F32)
        rsum = end.place("srsum", [P, 8], F32)
        no_use = end.place("no_use", [P, 1], F32)
        rowmax = [end.place(f"rowmax{i}", [P, 8], F32) for i in range(2)]

        S_ps = [psum(f"SS_ps{i}") for i in range(2)]
        T_ps = [psum(f"ST_ps{i}") for i in range(2)]
        A_ps = [psum(f"SA_ps{i}") for i in range(2)]
        O_ps, Y_ps = psum("SO_ps"), psum("SY_ps")

        w_loaded, b_loaded = sem("ow_loaded"), sem("ob_loaded")
        w_high, w_split = sem("ow_high"), sem("ow_split")
        zeroed = sem("zeroed")
        q_taken, k_spread = sem("q_taken"), [sem(f"k_spread{i}") for i in range(2)]
        scores_ready, max_ready, shifted_ready = sem("sscores_ready"), sem("smax_ready"), sem("shifted_ready")
        exp_done = sem("sexp_done")
        turned, turned_copied = sem("sturned"), [sem(f"sturned_copied{i}") for i in range(2)]
        pv_ready, sum_inverted, out_taken = sem("spv_ready"), sem("ssum_inverted"), sem("sout_taken")
        outs_turned, ot_high, ot_low = sem("outs_turned"), sem("ot_high"), sem("ot_low")
        y_ready, y_copied, stat_step = sem("sy_ready"), sem("sy_copied"), sem("sstat_step")
        y_moved, y_var_ready, y_std_ready, y_inverted = sem("y_moved"), sem("y_var_ready"), sem("y_std_ready"), sem("y_inverted")
        y_normed, y_scaled, x_ready = sem("y_normed"), sem("y_scaled"), sem("sx_ready")
        y_added = sem("y_added")

        def steps(eng, step):
            step(0, 0, 0)
            step(1, 1, 0)
            step(2, 0, 0)
            with eng.Fori(1, TILES // 2 - 1) as i:
                step(i * 2 + 1, 1, i)
                step(i * 2 + 2, 0, i)
            step(TILES - 1, 1, 0)

        block = st.enter_context(nc.Block())

        @block.sync
        def _(sp):
            sp.dma_start(wo_raw[:], w_out.rearrange("(c p) n -> p c n", p=P)).then_inc(w_loaded, DMA)
            sp.dma_start(bout_rows[:], b_out.partition_broadcast(P)).then_inc(b_loaded, DMA)
            sp.dma_start(gamma_rows[:], ln_gamma.partition_broadcast(P)).then_inc(b_loaded, DMA)
            for t in range(TILES):
                at_least(sp, q_taken, 2 * t)
                at_least(sp, k_spread[0], 4 * t)
                at_least(sp, k_spread[1], 4 * t)
                if t < ffw.late:
                    at_least(sp, ffw.rounded, 4 * (t - 1))
                ffw.fetch(sp, qk, t)

        def spread_keys(eng, copy, t, f, r):
            spread(copy, qk, kbd, t, f, r).then_inc(k_spread[f], 1)

        @block.gpsimd
        def _(pool):
            def take(t):
                for f in range(2):
                    at_least(pool, scores_ready, (t - 1) * OCTETS + 2 * f + 2)
                    at_least(pool, k_spread[0], (t - 1) * 4 + 4 * f)
                    pool.tensor_copy(qt[f][:], qk[:, f * (G // 2):(f + 1) * (G // 2), bass.ds(t * P, P)]).then_inc(q_taken, 1)
                    if f == 0:
                        pool.wait_ge(q_taken, 2 * (t - 1) + 1)
                        for r in range(4):
                            if r > 0:
                                pool.wait_ge(k_spread[0], (t - 1) * 4 + r)
                            spread_keys(pool, pool.tensor_copy, t, 0, r)

            def step(t, par, i):
                if not (isinstance(t, int) and t == TILES - 1):
                    take(t + 1)
                if par == 0 and not (isinstance(t, int) and t < 4):
                    for p in range(2):
                        m = t - 4 + p
                        x = resid[:, bass.ds(m, 1), :].rearrange("p o d -> p (o d)")
                        pool.wait_ge(y_normed, m + 1)
                        pool.tensor_tensor(y_rows[p][:], y_rows[p][:], gamma_rows[:], ALU.mult).then_inc(y_scaled, 1)
                        pool.wait_ge(y_scaled, m + 1)
                        pool.tensor_tensor(x, x, y_rows[p][:], ALU.add).then_inc(x_ready, 1)

            steps(pool, step)
            pool.wait_ge(q_taken, 2 * (TILES - 1))

        @block.scalar
        def _(act):
            act.wait_ge(zeroed, 2)

            def copy_turned(n, par):
                act.wait_ge(turned, 2 * n + 1)
                act.copy(probsT[par][:, 0:4, :], T_ps[0][:].rearrange("p (h q) -> p h q", h=4)).then_inc(turned_copied[0], 1)

            def outs_high(t):
                for f in range(2):
                    act.wait_ge(outs_turned, 2 * t + f + 1)
                    at_least(act, y_ready, t)
                    act.copy(oth[:, 4 * f:4 * f + 4, :], A_ps[f][:].rearrange("p (c q) -> p c q", c=4)).then_inc(ot_high, 1)

            def root():
                act.activation(y_std[:], y_moments[:, :, 1], ACT.Sqrt).then_inc(y_std_ready, 1)

            def step(t, par, i):
                static = isinstance(t, int)
                first = static and t == 0
                pair = par == 0 and not (static and t < 4)
                for k in range(OCTETS):
                    n = t * OCTETS + k
                    if not (first and k == 0):
                        copy_turned(n - 1, (k - 1) % 2)
                    act.wait_ge(shifted_ready, n + 1)
                    at_least(act, turned, 2 * (n - 1))
                    for b in range(2):
                        rows = slice(64 * b, 64 * b + 64)
                        act.activation(probs[k % 2][rows, :, 64 * b:64 * b + Q], shifted[k % 2][rows].rearrange("p (h k) -> p h k", h=8),
                                       ACT.Exp, scale=SCALE).then_inc(exp_done, 1)
                    if static and t == 1:
                        act.wait_ge(w_loaded, DMA)
                        act.copy(woh[:, 2 * k:2 * k + 2, :], wo_raw[:, 2 * k:2 * k + 2, :]).then_inc(w_high, 1)
                    if k == 0 and not first:
                        at_least(act, scores_ready, t * OCTETS)
                        for r in range(4):
                            spread_keys(act, act.copy, t, 1, r)
                    if k in (1, 2) and not (static and t < 3):
                        if k == 1:
                            act.wait_ge(ffw.loaded[1 - par], (t - 2 + par) * (4 * DMA // 2))
                        for piece in ((0, 1), (2, 3))[k - 1]:
                            ffw.round(act, qk, t - 3, piece, 1 if static and t - 3 >= ffw.fc_tiles else 0)
                    if pair and k == 2:
                        act.wait_ge(y_var_ready, i)
                        root()
                        act.activation(no_use[:], y_moments[:, 0, 0:1], ACT.Exp, scale=0.0)
                    if k == 3 and not first:
                        outs_high(t - 1)

            steps(act, step)
            copy_turned(TILES * OCTETS - 1, 1)
            act.wait_ge(y_var_ready, TILES // 2 - 1)
            root()
            outs_high(TILES - 1)
            act.wait_ge(y_var_ready, TILES // 2)
            root()

        @block.vector
        def _(dve):
            for i in range(2):
                dve.memset(probs[i][:], 0.0).then_inc(zeroed, 1)

            def copy_turned(n, par):
                dve.wait_ge(turned, 2 * n + 2)
                dve.tensor_copy(probsT[par][:, 4:8, :], T_ps[1][:].rearrange("p (h q) -> p h q", h=4)).then_inc(turned_copied[1], 1)

            def take_outputs(n, t, k):
                dve.wait_ge(pv_ready, n + 1)
                o = O_ps[:, 0:8 * VW].rearrange("p (h e) -> p h e", h=8)
                dve.reciprocal(rsum[:], o[:, :, 32]).then_inc(sum_inverted, 1)
                dve.wait_ge(sum_inverted, n + 1)
                if k == 0:
                    at_least(dve, outs_turned, 2 * t)
                dve.tensor_tensor(outs[:, k * 256:(k + 1) * 256].rearrange("p (h e) -> p h e", h=8), o[:, :, 0:32],
                                  rsum[:].unsqueeze(2).to_broadcast((P, 8, 32)), ALU.mult).then_inc(out_taken, 1)

            def outs_low(t):
                for f in range(2):
                    dve.wait_ge(ot_high, 2 * t + f + 1)
                    dve.tensor_tensor(otl[:, 4 * f:4 * f + 4, :], A_ps[f][:].rearrange("p (c q) -> p c q", c=4),
                                      oth[:, 4 * f:4 * f + 4, :].bitcast(F32), ALU.subtract).then_inc(ot_low, 1)

            def w_out_low(k):
                dve.wait_ge(w_high, k + 1)
                chunks = slice(2 * k, 2 * k + 2)
                dve.tensor_tensor(wol[:, chunks, :], wo_raw[:, chunks, :], woh[:, chunks, :].bitcast(F32), ALU.subtract).then_inc(w_split, 1)

            def take_y(t, par):
                dve.wait_ge(y_ready, t + 1)
                at_least(dve, x_ready, t - par)
                dve.tensor_tensor(y_rows[par][:], Y_ps[:], bout_rows[:], ALU.add).then_inc(y_copied, 1)

            def see_y(t, par):
                dve.wait_ge(y_copied, t + 1)
                dve.bn_stats(y_stats[par][:], y_rows[par][:]).then_inc(stat_step, 1)

            def y_means(i):
                for p in range(2):
                    dve.bn_aggr(y_moments[:, p, :], y_stats[p][:]).then_inc(y_moved, 1)
                dve.wait_ge(y_moved, i * 2)
                dve.tensor_scalar(y_moments[:, :, 1], y_moments[:, :, 1], 1e-6, None, ALU.add).then_inc(y_var_ready, 1)

            def norm_y(t, i):
                dve.wait_ge(y_std_ready, i)
                dve.reciprocal(y_rstd[:], y_std[:]).then_inc(y_inverted, 1)
                dve.wait_ge(y_inverted, i)
                for p in range(2):
                    dve.tensor_scalar(y_rows[p][:], y_rows[p][:], y_moments[:, p, 0:1], y_rstd[:, p:p + 1], ALU.subtract, ALU.mult).then_inc(y_normed, 1)

            def step(t, par, i):
                static = isinstance(t, int)
                first = static and t == 0
                pair = par == 0 and not (static and t < 4)
                for k in range(OCTETS):
                    n = t * OCTETS + k
                    dve.wait_ge(scores_ready, n + 1)
                    s = S_ps[k % 2][:].rearrange("p (h k) -> p h k", h=8)
                    dve.tensor_reduce(rowmax[k % 2][:], s, X, ALU.max).then_inc(max_ready, 1)
                    dve.wait_ge(max_ready, n + 1)
                    at_least(dve, exp_done, 2 * (n - 1))
                    dve.tensor_tensor(shifted[k % 2][:].rearrange("p (h k) -> p h k", h=8), s,
                                      rowmax[k % 2][:].unsqueeze(2).to_broadcast((P, 8, Q)), ALU.subtract).then_inc(shifted_ready, 1)
                    if static and t == 1 and k >= 1:
                        w_out_low(k - 1)
                        if k == 3:
                            w_out_low(3)
                            dve.wait_ge(b_loaded, 2 * DMA)
                    if k == 0 and not (static and t < 3):
                        take_y(t - 3, 1 - par)
                    if pair and k == 3:
                        norm_y(t - 4, i)
                    if not (first and k == 0):
                        copy_turned(n - 1, (k - 1) % 2)
                    if k == 0 and not (static and t < 2):
                        outs_low(t - 2)
                    if k == 1 and not (static and t < 3):
                        see_y(t - 3, 1 - par)
                    if k >= 2 and not (static and t < 3):
                        for piece in ((0, 1), (2, 3))[k - 2]:
                            dve.wait_ge(ffw.rounded, (t - 3) * 4 + piece + 1)
                            if k == 2 and piece == 1:
                                dve.wait_ge(stat_step, t - 2)
                            ffw.clip(dve, qk, t - 3, piece, ffw.clipped)
                            if pair and k == 2 and piece == 1:
                                y_means(i)
                    if k >= 2:
                        take_outputs(n - 2, t, k - 2)
                    elif not first:
                        take_outputs(n - 2, t - 1, k + 2)

            steps(dve, step)
            last = TILES * OCTETS
            take_y(TILES - 3, 1)
            outs_low(TILES - 2)
            copy_turned(last - 1, 1)
            take_outputs(last - 2, TILES - 1, 2)
            take_outputs(last - 1, TILES - 1, 3)
            see_y(TILES - 3, 1)
            dve.wait_ge(stat_step, TILES - 2)
            y_means(TILES // 2 - 1)
            outs_low(TILES - 1)

            def add_y(t, p):
                dve.wait_ge(y_normed, t + 1)
                dve.tensor_tensor(y_rows[p][:], y_rows[p][:], gamma_rows[:], ALU.mult).then_inc(y_added, 1)
                dve.wait_ge(y_added, 2 * (t - TILES) + 9)
                dve.tensor_tensor(resid[:, t, :], resid[:, t, :], y_rows[p][:], ALU.add).then_inc(y_added, 1)

            norm_y(TILES - 4, TILES // 2 - 1)
            for p in range(2):
                add_y(TILES - 4 + p, p)
            for p in range(2):
                dve.wait_ge(y_ready, TILES - 1 + p)
                dve.tensor_tensor(y_rows[p][:], (Y_ps, O_ps)[p][:], bout_rows[:], ALU.add).then_inc(y_copied, 1)
                see_y(TILES - 2 + p, p)
            dve.wait_ge(stat_step, TILES)
            y_means(TILES // 2)
            norm_y(TILES - 2, TILES // 2)
            for p in range(2):
                add_y(TILES - 2 + p, p)

        @block.tensor
        def _(pe):
            def scores(n, t, par, k):
                if k % 2 == 0:
                    at_least(pe, q_taken, (t - 1) * 2 + k // 2 + 1)
                    at_least(pe, k_spread[k // 2], t * 4)
                at_least(pe, shifted_ready, n - 1)
                for g in range(2):
                    for b in range(2):
                        keys = kbd[k // 2][:, (2 * k + g) % 4, b].rearrange("p r k -> p (r k)")
                        mm = pe.matmul(S_ps[k % 2][64 * b:64 * b + 64, g * 256:(g + 1) * 256], qt[k // 2][:, (2 * k + g) % 4, 64 * b:64 * b + Q],
                                       keys, start=True, stop=True)
                mm.then_inc(scores_ready, 1)

            def turn_probs(n, par):
                pe.wait_ge(exp_done, 2 * n + 2)
                for f in range(2):
                    at_least(pe, turned_copied[f], n)
                    for h in range(4):
                        mm = pe.transpose(T_ps[f][:, h * P:(h + 1) * P], probs[par][:, 4 * f + h, :], ident[:])
                    mm.then_inc(turned, 1)

            def weighted_values(n, t, k):
                for f in range(2):
                    pe.wait_ge(turned_copied[f], n + 1)
                at_least(pe, out_taken, n)
                for h in range(8):
                    v = vals[:, bass.ds(t, 1), 8 * k + h, 0:VW].rearrange("p t e -> p (t e)")
                    mm = pe.matmul(O_ps[:, h * VW:(h + 1) * VW], probsT[k % 2][:, h, :], v, start=True, stop=True)
                mm.then_inc(pv_ready, 1)

            def turn_outs(t):
                pe.wait_ge(out_taken, (t + 1) * OCTETS)
                for f in range(2):
                    at_least(pe, ot_low, 2 * t - 1 + f)
                    for c in range(4):
                        mm = pe.transpose(A_ps[f][:, c * P:(c + 1) * P], outs[:, (4 * f + c) * P:(4 * f + c + 1) * P], ident[:])
                    mm.then_inc(outs_turned, 1)

            def project(t, part, bank=Y_ps):
                if part == 0:
                    if isinstance(t, int) and t == 0:
                        pe.wait_ge(w_split, KC // 2)
                    pe.wait_ge(ot_low, 2 * t + 2)
                    if bank is Y_ps:
                        at_least(pe, y_copied, t)
                for c in ((0, 1, 2), (3, 4), (5, 6, 7))[part]:
                    for l, r in ((oth, woh), (oth, wol), (otl, woh)):
                        mm = pe.matmul(bank[:], l[:, c, :], r[:, c, :], start=(c == 0 and l is oth and r is woh), stop=(c == KC - 1 and l is otl))
                if part == 2:
                    mm.then_inc(y_ready, 1)

            def step(t, par, i):
                first = isinstance(t, int) and t == 0
                for k in range(OCTETS):
                    n = t * OCTETS + k
                    scores(n, t, par, k)
                    if k == 2 and not first:
                        turn_outs(t - 1)
                    if k >= 2 and not (isinstance(t, int) and t < 2):
                        project(t - 2, k - 1)
                    if not (first and k == 0):
                        turn_probs(n - 1, (k - 1) % 2)
                    if k == 1 and not (isinstance(t, int) and t < 2):
                        project(t - 2, 0)
                    if k >= 2:
                        weighted_values(n - 2, t, k - 2)
                    elif not first:
                        weighted_values(n - 2, t - 1, k + 2)

            steps(pe, step)
            last = TILES * OCTETS
            turn_probs(last - 1, 1)
            weighted_values(last - 2, TILES - 1, 2)
            weighted_values(last - 1, TILES - 1, 3)
            for part in range(3):
                project(TILES - 2, part)
            turn_outs(TILES - 1)
            for part in range(3):
                if part == 0:
                    pe.wait_ge(out_taken, last)
                project(TILES - 1, part, O_ps)


def feed_forward_block(nc, sh, ffw, region, resid, ident, qk, b_fc, A_fc, B_fc, b_proj, A_proj, B_proj, out):
    D, TOK, TILES, DC, F = sh.D, sh.TOK, sh.TILES, sh.DC, sh.F
    FT = F // P
    R = A_fc.shape[0]
    MAGIC = ffw.MAGIC
    HALF = TOK // 2
    HT = TILES // 2
    PACK = 6 * R
    K = 1024
    with ExitStack() as st:
        def sem(name):
            return st.enter_context(nc.semaphore(name))

        def psum(name):
            return st.enter_context(nc.psum_tensor(name, [P, BANK], F32))

        def at(name, shape, dtype, kib):
            return nc.alloc_sbuf_tensor_at(name, shape, dtype, offset=region + kib * K)

        hh, hl = at("hh", [P, FT, HALF], F32R, 0), at("hl", [P, FT, HALF], F32R, 32)
        wfT, wpT = at("wfT", [P, DC, F], F32R, 64), at("wpT", [P, FT, D], F32R, 96)
        xh, xl = at("fxh", [P, DC, TOK], F32R, 128), at("fxl", [P, DC, TOK], F32R, 144)
        a_raw = at("a_raw", [R, D + F], F32, 96)
        b_raw = at("b_raw", [P, FT + DC, R], F32, 106)
        b_pack = at("b_pack", [P, FT + DC, PACK], F32R, 108)
        tail = Arena(nc, region + 160 * K)
        xn = [tail.place(f"fxn{i}", [P, D], F32) for i in range(2)]
        bp_rows = tail.place("bp_rows", [P, D], F32)
        aT = tail.place("aT", [P, DC + FT, 2 * R], F32R)
        bfP, bpP = tail.place("bfP", [PACK, F], F32R), tail.place("bpP", [PACK, D], F32R)
        upack = [tail.place(f"upack{i}", [PACK, HALF], F32R) for i in range(2)]
        o_rows = [tail.place(f"o_rows{i}", [P, D], F32) for i in range(2)]
        bf_bias = tail.place("bf_bias", [P, FT], F32)
        stats = tail.place("fstats", [P, TILES, 6], F32)
        moments = tail.place("fmoments", [P, TILES, 2], F32)
        std, rstd = tail.place("fstd", [P, TILES], F32), tail.place("frstd", [P, TILES], F32)
        wscale, twice = ffw.scale, ffw.twice
        assert tail.at <= 229368 - 224, tail.at

        N_ps = [psum(f"FN_ps{i}") for i in range(2)]
        W_ps = [psum(f"FW_ps{i}") for i in range(2)]
        H_ps = [psum(f"FH_ps{i}") for i in range(2)]
        U_ps = psum("FU_ps")

        a_loaded, b_loaded, bias_loaded = sem("a_loaded"), sem("b_loaded"), sem("fbias_loaded")
        b_high, b_split = sem("b_high"), sem("b_split")
        small_turned, a_high, a_split, small_copied = sem("small_turned"), sem("a_high"), sem("a_split"), sem("small_copied")
        w_turned, w_copied = sem("w_turned"), [sem(f"w_copied{i}") for i in range(2)]
        ln_step, var_ready, std_ready, rstd_ready, xn_ready = sem("fln_step"), sem("fvar_ready"), sem("fstd_ready"), sem("frstd_ready"), sem("fxn_ready")
        xn_turned, xt_high, xt_low = sem("fxn_turned"), sem("fxt_high"), sem("fxt_low")
        u_ready, u_high, u_packed = sem("u_ready"), sem("u_high"), sem("u_packed")
        h_ready, gelu_done, h_high, h_low = sem("h_ready"), sem("gelu_done"), sem("h_high"), sem("h_low")
        bias_added, z_ready, o_ready, o_stored = sem("bias_added"), sem("z_ready"), sem("o_ready"), [sem("o_stored0"), sem("o_stored1")]

        SMALL = 1 + (FT + DC) // 4
        out_rows = out.rearrange("b q d -> (b q) d").rearrange("(t p) d -> t p d", p=P)
        block = st.enter_context(nc.Block())

        def as_chunks(ap):
            return ap.rearrange("p (c n) -> p c n", c=DC)

        @block.sync
        def _(sp):
            sp.dma_start(b_raw[:, 0:FT, :], B_fc.rearrange("(t p) r -> p t r", p=P)).then_inc(b_loaded, DMA)
            sp.dma_start(b_raw[:, FT:, :], B_proj.rearrange("(t p) r -> p t r", p=P)).then_inc(b_loaded, DMA)
            sp.dma_start(a_raw[:, 0:D], A_fc).then_inc(a_loaded, DMA)
            sp.dma_start(a_raw[:, D:D + F], A_proj).then_inc(a_loaded, DMA)
            sp.dma_start(bp_rows[:], b_proj.partition_broadcast(P)).then_inc(bias_loaded, DMA)
            with nc.allow_non_contiguous_dma(reason="a bias of 2048 values, turned"):
                sp.dma_start(bf_bias[:], b_fc.rearrange("(t p) -> p t", p=P)).then_inc(bias_loaded, DMA)
            for t in range(TILES):
                sp.wait_ge(o_ready, t + 1)
                sp.dma_start(out_rows[t], o_rows[t % 2][:]).then_inc(o_stored[t % 2], DMA)
            for i in range(2):
                sp.wait_ge(o_stored[i], TILES // 2 * DMA)

        @block.gpsimd
        def _(pool):
            pool.wait_ge(bias_loaded, 2 * DMA)
            for n in range(2 * FT):
                if n < TILES:
                    pool.wait_ge(xn_ready, n + 1)
                    pool.tensor_tensor(resid[:, n, :], resid[:, n, :], bp_rows[:], ALU.add).then_inc(bias_added, 1)
                h, ft = n // FT, n % FT
                pool.wait_ge(h_high, n + 1)
                pool.tensor_tensor(hl[:, ft, :], xn[n % 2][:], hh[:, ft, :].bitcast(F32), ALU.subtract).then_inc(h_low, 1)

        def copy_weight(eng, k):
            eng.wait_ge(w_turned, k + 1)
            if k < FT:
                dst, src = wfT[:, :, k * P:(k + 1) * P], as_chunks(W_ps[k % 2][:])
            else:
                dst, src = wpT[:, k - FT, :], W_ps[k % 2][:]
            if k % 2 == 0:
                eng.activation(dst, src, ACT.Copy, bias=-MAGIC).then_inc(w_copied[0], 1)
            else:
                eng.tensor_scalar(dst, src, MAGIC, None, ALU.subtract).then_inc(w_copied[1], 1)

        @block.scalar
        def _(act):
            def round_late(n):
                ffw.round(act, qk, ffw.late + n // 4, n % 4, 1)

            for k in range(0, FT, 2):
                copy_weight(act, k)
                if k == 0:
                    act.wait_ge(ffw.loaded_late, (TILES - ffw.late) * 4 * DMA)
                round_late(k // 2)
                if k == 4:
                    act.wait_ge(b_loaded, 2 * DMA)
                    act.copy(b_pack[:, :, 0:4 * R].rearrange("p t (k r) -> p t k r", k=4), b_raw[:].unsqueeze(2).to_broadcast((P, FT + DC, 4, R))).then_inc(b_high, 1)
            act.wait_ge(small_turned, 1)
            act.copy(aT[:, :, 0:R], W_ps[0][:, 0:(DC + FT) * R].rearrange("p (t r) -> p t r", r=R)).then_inc(a_high, 1)
            for k in range(1, SMALL):
                act.wait_ge(small_turned, k + 1)
                dst = bfP[:, (k - 1) * BANK:k * BANK] if k < SMALL - 1 else bpP[:]
                act.copy(dst, W_ps[k % 2][0:PACK, :]).then_inc(small_copied, 1)

            act.wait_ge(var_ready, 1)
            act.activation(std[:], moments[:, :, 1], ACT.Sqrt).then_inc(std_ready, 1)

            def high(t):
                act.wait_ge(xn_turned, t + 1)
                act.copy(xh[:, :, t * P:(t + 1) * P], as_chunks(N_ps[t % 2][:])).then_inc(xt_high, 1)

            for t in range(TILES):
                copy_weight(act, FT + 2 * t)
                if t < 4:
                    round_late(8 + t)
                high(t)

            def pack(k):
                act.wait_ge(u_ready, k + 1)
                w, h = k % 2, k // 2
                rows = slice(0, 2 * R)
                at_least(act, z_ready if w else h_ready, (HT * h if w else FT * h))
                act.activation(upack[w][rows, :], U_ps[rows, :], ACT.Copy, scale=twice[rows, w:w + 1]).then_inc(u_high, 1)
                act.activation(upack[w][4 * R:6 * R, :], U_ps[rows, :], ACT.Copy, scale=twice[rows, w:w + 1]).then_inc(u_high, 1)

            act.wait_ge(bias_loaded, 2 * DMA)
            for h in range(2):
                pack(2 * h)
                for ft in range(FT):
                    n = h * FT + ft
                    act.wait_ge(h_ready, n + 1)
                    at_least(act, h_low, n - 1)
                    act.activation(xn[n % 2][:], H_ps[n % 2][:], ACT.Gelu, bias=bf_bias[:, ft:ft + 1], scale=wscale[:, 0:1]).then_inc(gelu_done, 1)
                pack(2 * h + 1)

        @block.vector
        def _(dve):
            def clip_late(n):
                dve.wait_ge(ffw.rounded, 4 * ffw.late + n + 1)
                ffw.clip(dve, qk, ffw.late + n // 4, n % 4, ffw.clipped)

            def norm(t):
                at_least(dve, xn_turned, t - 1)
                dve.tensor_scalar(xn[t % 2][:], resid[:, t, :], moments[:, t, 0:1], rstd[:, t:t + 1], ALU.subtract, ALU.mult).then_inc(xn_ready, 1)

            def low(t):
                dve.wait_ge(xt_high, t + 1)
                dve.tensor_tensor(xl[:, :, t * P:(t + 1) * P], as_chunks(N_ps[t % 2][:]), xh[:, :, t * P:(t + 1) * P].bitcast(F32), ALU.subtract).then_inc(xt_low, 1)

            for k in range(1, FT, 2):
                dve.bn_stats(stats[:, k // 2, :], resid[:, k // 2, :]).then_inc(ln_step, 1)
                copy_weight(dve, k)
                clip_late(k // 2)
                if k == 5:
                    dve.wait_ge(b_high, 1)
                    dve.tensor_tensor(b_pack[:, :, 4 * R:6 * R].rearrange("p t (k r) -> p t k r", k=2), b_raw[:].unsqueeze(2).to_broadcast((P, FT + DC, 2, R)),
                                      b_pack[:, :, 0:2 * R].bitcast(F32).rearrange("p t (k r) -> p t k r", k=2), ALU.subtract).then_inc(b_split, 1)
            dve.wait_ge(ln_step, TILES)
            for t in range(TILES):
                dve.bn_aggr(moments[:, t, :], stats[:, t, :]).then_inc(ln_step, 1)
            dve.wait_ge(ln_step, 2 * TILES)
            dve.tensor_scalar(moments[:, :, 1], moments[:, :, 1], 1e-5, None, ALU.add).then_inc(var_ready, 1)
            dve.wait_ge(a_high, 1)
            dve.tensor_tensor(aT[:, :, R:2 * R], W_ps[0][:, 0:(DC + FT) * R].rearrange("p (t r) -> p t r", r=R),
                              aT[:, :, 0:R].bitcast(F32), ALU.subtract).then_inc(a_split, 1)
            dve.wait_ge(std_ready, 1)
            dve.reciprocal(rstd[:], std[:]).then_inc(rstd_ready, 1)
            dve.wait_ge(rstd_ready, 1)
            norm(0)
            norm(1)
            for t in range(TILES):
                copy_weight(dve, FT + 2 * t + 1)
                if t < 4:
                    clip_late(8 + t)
                low(t)
                if t + 2 < TILES:
                    norm(t + 2)

            def pack(k):
                dve.wait_ge(u_high, 2 * k + 2)
                w, rows = k % 2, slice(0, 2 * R)
                dve.scalar_tensor_tensor(upack[w][2 * R:4 * R, :], U_ps[rows, :], twice[rows, w:w + 1], upack[w][rows, :].bitcast(F32),
                                         ALU.mult, ALU.subtract).then_inc(u_packed, 1)

            for h in range(2):
                pack(2 * h)
                for ft in range(FT):
                    n = h * FT + ft
                    dve.wait_ge(gelu_done, n + 1)
                    dve.tensor_copy(hh[:, ft, :], xn[n % 2][:]).then_inc(h_high, 1)
                pack(2 * h + 1)
                for i in range(HT):
                    t = h * HT + i
                    dve.wait_ge(z_ready, t + 1)
                    dve.wait_ge(bias_added, t + 1)
                    at_least(dve, o_stored[t % 2], t // 2 * DMA)
                    dve.scalar_tensor_tensor(o_rows[t % 2][:], W_ps[t % 2][:], wscale[:, 1:2], resid[:, t, :], ALU.mult, ALU.add).then_inc(o_ready, 1)

        @block.tensor
        def _(pe):
            def turn_weight(k):
                at_least(pe, w_copied[k % 2], k // 2)
                for c in range(DC):
                    if k < FT:
                        src = qk[:, 4 * (k % 4) + c, k // 4 * P:(k // 4 + 1) * P]
                    else:
                        t = 4 + (k - FT) // 4
                        pe.wait_ge(ffw.clipped, 4 * t + 4)
                        src = qk[:, 4 * c + k % 4, t * P:(t + 1) * P]
                    mm = pe.transpose(W_ps[k % 2][:, c * P:(c + 1) * P], src, ident[:])
                mm.then_inc(w_turned, 1)

            def turn_small():
                pe.wait_ge(a_loaded, 2 * DMA)
                pe.wait_ge(w_copied[0], FT // 2)
                pe.wait_ge(w_copied[1], FT // 2)
                for c in range(DC + FT):
                    mm = pe.transpose(W_ps[0][:, c * R:(c + 1) * R], a_raw[:, c * P:(c + 1) * P], ident[0:R, 0:R])
                mm.then_inc(small_turned, 1)
                pe.wait_ge(b_split, 1)
                for k in range(1, SMALL):
                    if k == 2:
                        pe.wait_ge(a_split, 1)
                    at_least(pe, small_copied, k - 2)
                    for i in range(4):
                        mm = pe.transpose(W_ps[k % 2][0:PACK, i * P:(i + 1) * P], b_pack[:, 4 * (k - 1) + i, :].bitcast(F32), ident[:])
                    mm.then_inc(small_turned, 1)

            for k in range(FT):
                turn_weight(k)
            turn_small()
            pe.wait_ge(small_copied, SMALL - 1)

            def turn_norm(t):
                pe.wait_ge(xn_ready, t + 1)
                at_least(pe, xt_low, t - 1)
                for c in range(DC):
                    mm = pe.transpose(N_ps[t % 2][:, c * P:(c + 1) * P], xn[t % 2][:, c * P:(c + 1) * P], ident[:])
                mm.then_inc(xn_turned, 1)

            for t in range(TILES):
                turn_weight(FT + 2 * t)
                turn_weight(FT + 2 * t + 1)
                turn_norm(t)

            def lora(k, chunks, first, high, low):
                at_least(pe, u_packed, k)
                for i, part in enumerate((high, low)):
                    for c in range(chunks):
                        mm = pe.matmul(U_ps[0:2 * R, :], aT[:, first + c, :], part(c), start=(i == 0 and c == 0), stop=(i == 1 and c == chunks - 1))
                mm.then_inc(u_ready, 1)

            def hidden(n):
                h, ft = n // FT, n % FT
                toks, cols = slice(h * HALF, (h + 1) * HALF), slice(ft * P, (ft + 1) * P)
                at_least(pe, gelu_done, n - 1)
                for c in range(DC):
                    for k, part in enumerate((xh, xl)):
                        pe.matmul(H_ps[n % 2][:], wfT[:, c, cols], part[:, c, toks], start=(c == 0 and k == 0), stop=False)
                if ft == 0:
                    pe.wait_ge(u_packed, 2 * h + 1)
                pe.matmul(H_ps[n % 2][:], bfP[:, cols], upack[0][:], start=False, stop=True).then_inc(h_ready, 1)

            def project(t):
                h = t // HT
                toks = slice((t % HT) * P, (t % HT + 1) * P)
                at_least(pe, o_ready, t - 1)
                for ft in range(FT):
                    for k, part in enumerate((hh, hl)):
                        pe.matmul(W_ps[t % 2][:], part[:, ft, toks], wpT[:, ft, :], start=(ft == 0 and k == 0), stop=False)
                if t % HT == 0:
                    pe.wait_ge(u_packed, 2 * h + 2)
                pe.matmul(W_ps[t % 2][:], upack[1][:, toks], bpP[:], start=False, stop=True).then_inc(z_ready, 1)

            for i in range(2):
                pe.wait_ge(w_copied[i], FT)
            pe.wait_ge(xt_low, TILES)
            for h in range(2):
                toks = slice(h * HALF, (h + 1) * HALF)
                lora(2 * h, DC, 0, lambda c: xh[:, c, toks], lambda c: xl[:, c, toks])
                for ft in range(FT):
                    hidden(h * FT + ft)
                pe.wait_ge(h_low, (h + 1) * FT)
                lora(2 * h + 1, FT, DC, lambda c: hh[:, c, :], lambda c: hl[:, c, :])
                for i in range(HT):
                    project(h * HT + i)


def perceiver(nc, args, out):
    sh = Shapes(args["x"], args["ctx_768"], args["L0_attn_w_qkv"], args["L0_ffn_W_fc"])
    with ExitStack() as st:
        arena = Arena(nc, 16512)
        resid = arena.place("resid", [P, sh.TILES, sh.D], F32)
        ident = arena.place("ident", [P, P], F32)
        ctxsum = arena.place("ctxsum", [P, sh.B, sh.SC, sh.CC], F32)
        nansum = arena.place("nansum", [P, sh.B * 8], F32)
        a = args
        later = CrossWeights(nc, sh, st, arena, a["L0_xattn_Wv"], a["L0_xattn_bv"], a["L0_xattn_Wo"], a["L0_xattn_bo"])
        ffw = FeedForwardWeights(nc, sh, st, arena, a["L0_ffn_W_fc"], a["L0_ffn_W_proj"])
        O_at = arena.at
        O_all = (arena.place("O_all", [P, sh.B, 256], F32), O_at)
        ident_ready = st.enter_context(nc.semaphore("ident_ready"))
        nc.gpsimd.memset(ident[:], 0.0).then_inc(ident_ready, 1)
        nc.gpsimd.wait_ge(ident_ready, 1)
        nc.gpsimd.affine_select(out=ident[:], in_=ident[:], compare_op=ALU.not_equal, fill=1.0, base=0,
                                pattern=[[-1, P]], channel_multiplier=1).then_inc(ident_ready, 1)
        cross_attention_block(nc, sh, later, arena, resid, ident, ident_ready, ctxsum, nansum, O_all, a["x"], a["ctx_768"], a["L0_xattn_Wq"], a["L0_xattn_bq"],
                              a["L0_xattn_Wk"], a["L0_xattn_bk"], a["L0_xattn_Wv"])
        qk, vals, taken = latent_block(nc, sh, later, ffw, arena, resid, ident, ctxsum, nansum, O_all, a["L0_attn_w_qkv"], a["L0_attn_ln_beta"])
        self_attention_block(nc, sh, ffw, later.bo_rows, O_at, resid, ident, qk, vals, taken, a["L0_attn_w_out"], a["L0_attn_b_out"],
                             a["L0_attn_ln_gamma"])
        feed_forward_block(nc, sh, ffw, O_at, resid, ident, qk, a["L0_ffn_b_fc"], a["L0_ffn_A_fc"], a["L0_ffn_B_fc"],
                           a["L0_ffn_b_proj"], a["L0_ffn_A_proj"], a["L0_ffn_B_proj"], out)


_INS = ['x', 'ctx_768', 'L0_xattn_Wq', 'L0_xattn_bq', 'L0_xattn_Wk', 'L0_xattn_bk', 'L0_xattn_Wv', 'L0_xattn_bv',
        'L0_xattn_Wo', 'L0_xattn_bo', 'L0_attn_w_qkv', 'L0_attn_w_out', 'L0_attn_b_out', 'L0_attn_ln_gamma',
        'L0_attn_ln_beta', 'L0_ffn_W_fc', 'L0_ffn_b_fc', 'L0_ffn_A_fc', 'L0_ffn_B_fc', 'L0_ffn_W_proj',
        'L0_ffn_b_proj', 'L0_ffn_A_proj', 'L0_ffn_B_proj']


def kernel(**inputs):
    import numpy as _np
    import concourse.bacc as _bacc
    from concourse import mybir as _mybir
    from concourse.bass_utils import run_bass_kernel_spmd as _run

    nc = _bacc.Bacc("TRN2", target_bir_lowering=False, num_devices=1)
    arrays, args = {}, {}
    for name in _INS:
        a = _np.ascontiguousarray(inputs[name])
        arrays[f"in_{name}_dram"] = a
        args[name] = nc.dram_tensor(f"in_{name}_dram", a.shape, _mybir.dt.from_np(a.dtype), kind="ExternalInput").ap()
    out = nc.dram_tensor("out_0_dram", (16, 64, 512), _mybir.dt.float32, kind="ExternalOutput").ap()
    perceiver(nc, args, out)
    r = _run(nc, [arrays], core_ids=[0])
    return r.results[0]["out_0_dram"]
```

```python
from contextlib import ExitStack

import concourse.bass as bass
from concourse import mybir
from concourse.alu_op_type import AluOpType as ALU

ACT = mybir.ActivationFunctionType
F32 = mybir.dt.float32
F32R = mybir.dt.float32r
I32 = mybir.dt.int32
X = mybir.AxisListType.X
MAX = bass.bass_isa.ReduceOp.max

P = 128
DMA = 16
BANK = 512


def at_least(eng, sem, value):
    if isinstance(value, int) and value <= 0:
        return
    eng.wait_ge(sem, value)


class Shapes:

    def __init__(self, x, ctx, w_qkv, w_fc):
        self.B, self.Q, self.D = x.shape
        _, self.S, self.C = ctx.shape
        self.TOK = self.B * self.Q
        self.TILES = self.TOK // P
        self.DC = self.D // P
        self.CC = self.C // P
        self.SC = self.S // P
        self.F = w_fc.shape[0]
        self.INNER = w_qkv.shape[1] // 3


class Arena:

    def __init__(self, nc, base):
        self.nc, self.at = nc, base

    def place(self, name, shape, dtype, at=None):
        size = 1
        for n in shape[1:]:
            size *= n
        size *= 4
        offset = self.at if at is None else at
        t = self.nc.alloc_sbuf_tensor_at(name, shape, dtype, offset=offset)
        if at is None:
            self.at += -(-size // 32) * 32
        return t


def three_products(pe, out, high_l, low_l, high_r, low_r, chunks):
    last = None
    n = 0
    for c in range(chunks):
        for l, r in ((high_l, high_r), (high_l, low_r), (low_l, high_r)):
            last = pe.matmul(out, l(c), r(c), start=(n == 0), stop=(n == 3 * chunks - 1))
            n += 1
    return last


def by_pair_group(w):
    return w.rearrange("(g p e d) n -> p d g e n", g=2, p=4, e=2)


def cross_attention_block(nc, sh, later, arena, resid, ident, ident_ready, ctxsum, nansum, O_all, x, ctx_in, Wq, bq, Wk, bk, Wv):
    B, Q, S, D, TOK = sh.B, sh.Q, sh.S, sh.D, sh.TOK
    DC, CC, SC, TILES = sh.DC, sh.CC, sh.SC, sh.TILES
    HEADS = 16
    DH = D // HEADS
    SCALE = DH ** -0.5
    CLAMP = 10000.0
    PAIRS = HEADS // 2
    UNITS = DC + SC
    VW = 2 * DH + 2
    HALF = TOK // 2
    base = arena.at
    with ExitStack() as st:
        def sem(name):
            return st.enter_context(nc.semaphore(name))

        def psum(name):
            return st.enter_context(nc.psum_tensor(name, [P, BANK], F32))

        place = arena.place
        wkh, wkl = place("wkh", [P, CC, D], F32R), place("wkl", [P, CC, D], F32R)
        wvh, wvl = place("wvh", [P, CC, D], F32R), place("wvl", [P, CC, D], F32R)
        qT = place("qT", [P, DC, TOK], F32)
        qdh = [place(f"qdh{i}", [P, PAIRS, P], F32R) for i in range(2)]
        qdl = [place(f"qdl{i}", [P, DC, P], F32R) for i in range(2)]
        ctx_rows = [place(f"ctx_rows{i}", [P, SC, sh.C], F32) for i in range(2)]
        cth = [place(f"cth{i}", [P, CC, S], F32R) for i in range(2)]
        ctl = [place(f"ctl{i}", [P, CC, S], F32R) for i in range(2)]
        keys0 = place("keys0", [P, PAIRS, S], F32R)
        k1 = arena.at
        keys = [keys0, place("keys1", [P, PAIRS, S], F32R)]
        vals = [place(f"vals{i}", [P, SC, PAIRS, VW], F32) for i in range(2)]
        p1 = arena.at
        probs = [place(f"probs{i}", [P, S], F32) for i in range(2)]
        probsT = [place(f"probsT{i}", [P, S], F32) for i in range(2)]
        later.at = arena.at
        later.place(arena)
        later.woh, later.wol = place("woh", [P, DC, D], F32R, at=base), place("wol", [P, DC, D], F32R, at=base + 4 * DC * D)
        xth = [place("xth0", [P, DC, HALF], F32R), place("xth1", [P, DC, HALF], F32R, at=k1)]
        xtl = [place("xtl0", [P, DC, HALF], F32R), place("xtl1", [P, DC, HALF], F32R, at=k1 + 4 * DC * HALF)]
        wk_raw = place("wk_raw", [P, CC, D], F32, at=k1)
        wv_raw = place("wv_raw", [P, CC, D], F32, at=k1 + 4 * CC * D)
        wq_raw = place("wq_raw", [P, DC, D], F32, at=p1)
        wqh = place("wqh", [P, DC, D], F32R, at=O_all[1])
        wql = place("wql", [P, DC, D], F32R, at=O_all[1] + 4 * DC * D)
        outs = O_all[0]
        xn = [place(f"xn{i}", [P, D], F32) for i in range(2)]
        stats = place("stats", [P, TILES, 6], F32)
        moments = place("moments", [P, TILES, 2], F32)
        std = place("std", [P, TILES], F32)
        rstd = place("rstd", [P, TILES], F32)
        bqT, bkT = place("bqT", [P, DC], F32), place("bkT", [P, DC], F32)
        bqs = place("bqs", [P, DC], F32)
        lowest = place("lowest", [P, 1], F32)
        bounds = [place(f"bounds{i}", [P, 1], F32) for i in range(2)]
        rawmax = [place(f"rawmax{i}", [P, 1], F32) for i in range(2)]
        negmax = [place(f"negmax{i}", [P, 1], F32) for i in range(2)]
        rsum = place("rsum", [P, 4], F32)
        zero = place("zero", [P, 1], F32)
        q_here = place("q_here", [P, DC, Q], F32)

        S_ps = [psum(f"S_ps{i}") for i in range(2)]
        T_ps = [psum(f"T_ps{i}") for i in range(2)]
        U_ps = [psum(f"U_ps{i}") for i in range(2)]
        O_ps, C_ps = psum("O_ps"), psum("C_ps")

        x_loaded, wk_loaded, wv_loaded, wq_loaded = sem("x_loaded"), sem("wk_loaded"), sem("wv_loaded"), sem("wq_loaded")
        bias_loaded = sem("bias_loaded")
        ctx_loaded = [sem(f"ctx_loaded{i}") for i in range(2)]
        consts_set = sem("consts_set")
        w_high, w_split = sem("xw_high"), sem("xw_split")
        bq_scaled = sem("bq_scaled")
        stat_step, var_ready, std_ready, xn_ready = sem("stat_step"), sem("var_ready"), sem("std_ready"), sem("xn_ready")
        xn_turned, xt_high, xt_low = sem("xn_turned"), sem("xt_high"), sem("xt_low")
        q_ready, q_copied = sem("q_ready"), sem("q_copied")
        ctx_turned, ctx_high, ctx_low = sem("ctx_turned"), sem("ctx_high"), sem("ctx_low")
        unit_ready, k_high, k_low, v_ready = sem("unit_ready"), sem("k_high"), sem("k_low"), sem("v_ready")
        q_taken, q_high, q_spread, q_doubled = sem("xq_taken"), sem("q_high"), sem("q_spread"), sem("q_doubled")
        scores_ready, rawmax_ready, max_ready = sem("scores_ready"), sem("rawmax_ready"), sem("max_ready")
        exp_done, clipped = sem("exp_done"), sem("clipped")
        turned, turned_copied, pv_ready = sem("turned"), sem("turned_copied"), sem("pv_ready")
        sum_inverted, out_taken = sem("sum_inverted"), sem("out_taken")
        wo_high = sem("wo_high")

        x_rows = x.rearrange("b q d -> (b q) d").rearrange("(t p) d -> t p d", p=P)

        def chunk_bank(b, c):
            return (C_ps, T_ps[0], O_ps, T_ps[1])[c] if isinstance(b, int) and b < 2 else C_ps

        def own(e):
            return slice(64 * e, 64 * e + 64)

        def high_queries(par, r, rows):
            by_group = qdh[par][rows].rearrange("p (g e) n -> p g e n", e=2)
            return by_group[:, :, r // 2, 64 * (r % 2):64 * (r % 2) + Q]

        def steps(eng, step):
            step(0, 0, True, True)
            step(1, 1, True, True)
            with eng.Fori(1, B // 2 - 1) as i:
                step(i * 2, 0, True, True)
                step(i * 2 + 1, 1, True, True)
            step(B - 2, 0, True, False)
            step(B - 1, 1, False, False)

        block = st.enter_context(nc.Block())

        @block.sync
        def _(sp):
            for b in range(2):
                sp.dma_start(ctx_rows[b][:], ctx_in[b].rearrange("(c p) d -> p c d", p=P)).then_inc(ctx_loaded[b], DMA)
                if b == 0:
                    sp.dma_start(wk_raw[:], Wk.rearrange("(c p) n -> p c n", p=P)).then_inc(wk_loaded, DMA)
                    with nc.allow_non_contiguous_dma(reason="two biases of 512 values, turned"):
                        sp.dma_start(bqT[:], bq.rearrange("(c p) -> p c", p=P)).then_inc(bias_loaded, DMA)
                        sp.dma_start(bkT[:], bk.rearrange("(c p) -> p c", p=P)).then_inc(bias_loaded, DMA)
                    sp.dma_start(wv_raw[:], Wv.rearrange("(c p) n -> p c n", p=P)).then_inc(wv_loaded, DMA)
            for t in range(TILES):
                sp.dma_start(resid[:, t, :], x_rows[t]).then_inc(x_loaded, DMA)
            sp.dma_start(wq_raw[:], Wq.rearrange("(c p) n -> p c n", p=P)).then_inc(wq_loaded, DMA)

            def fetch(b, par):
                sp.wait_ge(ctx_turned, (b - 1) * SC)
                sp.dma_start(ctx_rows[par][:], ctx_in[b].rearrange("(c p) d -> p c d", p=P)).then_inc(ctx_loaded[par], DMA)

            with sp.Fori(1, B // 2) as i:
                fetch(i * 2, 0)
                fetch(i * 2 + 1, 1)
            sp.wait_ge(q_copied, 2 * DC)
            later.fetch(sp)

        @block.gpsimd
        def _(pool):
            pool.memset(lowest[:], -CLAMP).then_inc(consts_set, 1)
            pool.memset(zero[:], 0.0).then_inc(consts_set, 1)
            for i in range(2):
                pool.memset(vals[i][:, :, :, 2 * DH:VW], 1.0).then_inc(consts_set, 1)
                pool.memset(qdh[i][:].bitcast(F32), 0.0).then_inc(consts_set, 1)
                pool.memset(qdl[i][:].bitcast(F32), 0.0).then_inc(consts_set, 1)
            pool.wait_ge(consts_set, 8)

            def step(b, par, more, turn):
                if isinstance(b, int) and b < 2:
                    pool.wait_ge(q_copied, DC)
                at_least(pool, scores_ready, (b - 1) * PAIRS)
                at_least(pool, q_spread, b * 4)
                pool.tensor_copy(q_here[:], qT[:, :, bass.ds(b * Q, Q)]).then_inc(q_taken, 1)
                pool.wait_ge(q_taken, b + 1)
                for r in range(4):
                    rows = slice(32 * r, 32 * r + 32)
                    cols = slice(64 * (r % 2), 64 * (r % 2) + Q)
                    src = q_here[rows, :, :]
                    if r > 0:
                        pool.wait_ge(q_spread, b * 4 + r)
                    pool.tensor_tensor(high_queries(par, r, rows), src, zero[rows].unsqueeze(2).to_broadcast((32, DC, Q)), ALU.add).then_inc(q_high, 1)
                    pool.wait_ge(q_high, b * 4 + r + 1)
                    pool.tensor_tensor(qdl[par][rows, :, cols], src, high_queries(par, r, rows).bitcast(F32), ALU.subtract).then_inc(q_spread, 1)
                pool.wait_ge(q_spread, b * 4 + 4)

            steps(pool, step)
            pool.wait_ge(later.bo_loaded, DMA)
            for t in range(TILES):
                pool.tensor_tensor(resid[:, t, :], resid[:, t, :], later.bo_rows[:], ALU.add)
            pool.wait_ge(wo_high, 1)
            pool.tensor_tensor(later.wol[:], later.wo_raw[:], later.woh[:].bitcast(F32), ALU.subtract)

        @block.scalar
        def _(act):
            def split(raw, high, loaded):
                act.wait_ge(loaded, DMA)
                act.copy(high[:], raw[:]).then_inc(w_high, 1)

            def ctx_chunk(b, par, c):
                act.wait_ge(ctx_turned, b * SC + c + 1)
                act.copy(cth[par][:, :, c * P:(c + 1) * P], chunk_bank(b, c)[:, 0:CC * P].rearrange("p (c t) -> p c t", c=CC)).then_inc(ctx_high, 1)

            def unit(b, par, u):
                act.wait_ge(unit_ready, b * UNITS + u + 1)
                if u < DC:
                    for e in range(2):
                        act.activation(keys[par][own(e), 2 * u + e, :], U_ps[u % 2][own(e), :], ACT.Identity, bias=bkT[own(e), u:u + 1]).then_inc(k_high, 1)
                else:
                    act.copy(vals[par][:, u - DC, :, 0:2 * DH], U_ps[u % 2][:].rearrange("p (h e) -> p h e", h=PAIRS)).then_inc(v_ready, 1)

            split(wk_raw, wkh, wk_loaded)
            for c in range(SC):
                ctx_chunk(0, 0, c)
            split(wv_raw, wvh, wv_loaded)
            act.wait_ge(bias_loaded, 2 * DMA)
            act.wait_ge(consts_set, 8)
            for u in range(UNITS):
                unit(0, 0, u)
                if u == DC:
                    act.wait_ge(var_ready, 1)
                    act.activation(std[:], moments[:, :, 1], ACT.Sqrt).then_inc(std_ready, 1)
                if u == DC + 1:
                    split(wq_raw, wqh, wq_loaded)
            act.wait_ge(bq_scaled, 1)

            def high(n):
                h, t = n // (TILES // 2), n % (TILES // 2)
                act.wait_ge(xn_turned, n + 1)
                act.copy(xth[h][:, :, t * P:(t + 1) * P], S_ps[n % 2][:].rearrange("p (c t) -> p c t", c=DC)).then_inc(xt_high, 1)

            for n in range(TILES // 2):
                high(n)
                if n > 0:
                    ctx_chunk(1, 1, n - 1)
            ctx_chunk(1, 1, SC - 1)
            def double_queries(b, par):
                act.wait_ge(q_spread, b * 4 + 4)
                for r in range(4):
                    rows, other = slice(32 * r, 32 * r + 32), slice(32 * (r ^ 2), 32 * (r ^ 2) + 32)
                    act.copy(high_queries(par, r, other), high_queries(par, r, rows).bitcast(F32)).then_inc(q_doubled, 1)

            for k in range(2 * DC):
                h, m = k // DC, k % DC
                if k < TILES // 2:
                    high(TILES // 2 + k)
                if k == 2 * DC - 1:
                    double_queries(0, 0)
                act.wait_ge(q_ready, k + 1)
                act.activation(qT[:, m, h * HALF:(h + 1) * HALF], U_ps[m % 2][:], ACT.Identity, bias=bqs[:, m:m + 1], scale=SCALE).then_inc(q_copied, 1)

            def step(b, par, more, turn):
                first = isinstance(b, int) and b == 0
                for j in range(PAIRS):
                    n = b * PAIRS + j
                    if j == 0 and not first:
                        unit(b, par, UNITS - 1)
                    if j > 0 and more:
                        unit(b + 1, 1 - par, j - 1)
                    if turn and j >= PAIRS - SC:
                        ctx_chunk(b + 2, par, j - PAIRS + SC)
                    act.wait_ge(max_ready, n + 1)
                    at_least(act, turned, n - 1)
                    act.activation(bounds[j % 2][:], lowest[:], ACT.Exp, bias=negmax[j % 2][:])
                    act.activation(probs[j % 2][:], S_ps[j % 2][:], ACT.Exp, bias=negmax[j % 2][:],
                                   accum_out=nansum[:, bass.ds(n, 1)]).then_inc(exp_done, 1)
                    if j == 6 and more:
                        double_queries(b + 1, 1 - par)
                    if j == 2 and not more:
                        act.wait_ge(later.wo_loaded, 8 * DMA)
                        act.copy(later.woh[:], later.wo_raw[:]).then_inc(wo_high, 1)

            steps(act, step)

        @block.vector
        def _(dve):
            def split(raw, high, low, n):
                dve.wait_ge(w_high, n)
                dve.tensor_tensor(low[:], raw[:], high[:].bitcast(F32), ALU.subtract).then_inc(w_split, 1)

            def turned_ctx(b, c):
                return chunk_bank(b, c)[:, 0:CC * P].rearrange("p (c t) -> p c t", c=CC)

            def ctx_low_part(b, par, c):
                dve.wait_ge(ctx_high, b * SC + c + 1)
                dve.tensor_tensor(ctl[par][:, :, c * P:(c + 1) * P], turned_ctx(b, c), cth[par][:, :, c * P:(c + 1) * P].bitcast(F32), ALU.subtract).then_inc(ctx_low, 1)

            def ctx_sum(b, c):
                dve.tensor_reduce(ctxsum[:, bass.ds(b, 1), c, :].rearrange("p b c -> p (b c)"), turned_ctx(b, c), X, ALU.add).then_inc(ctx_low, 1)

            def ctx_chunk(b, par, c):
                ctx_low_part(b, par, c)
                ctx_sum(b, c)

            def unit(b, par, u):
                if u < DC:
                    dve.wait_ge(k_high, (b * DC + u + 1) * 2)
                    for e in range(2):
                        dve.scalar_tensor_tensor(keys[par][own(1 - e), 2 * u + e, :], U_ps[u % 2][own(e), :], bkT[own(e), u:u + 1],
                                                 keys[par][own(e), 2 * u + e, :].bitcast(F32), ALU.add, ALU.subtract).then_inc(k_low, 1)

            for c in range(SC):
                ctx_low_part(0, 0, c)
            split(wk_raw, wkh, wkl, 1)
            split(wv_raw, wvh, wvl, 2)
            for u in range(DC):
                unit(0, 0, u)
                if u == 1:
                    dve.wait_ge(x_loaded, DMA * TILES)
                for t in ((), (0, 1, 2), (3,), range(4, TILES))[u]:
                    dve.bn_stats(stats[:, t, :], resid[:, t, :]).then_inc(stat_step, 1)
            for t in range(TILES):
                dve.wait_ge(stat_step, t + 1)
                dve.bn_aggr(moments[:, t, :], stats[:, t, :]).then_inc(stat_step, 1)
            dve.wait_ge(stat_step, 2 * TILES)
            dve.tensor_scalar(moments[:, :, 1], moments[:, :, 1], 1e-5, None, ALU.add).then_inc(var_ready, 1)
            dve.wait_ge(bias_loaded, 2 * DMA)
            dve.tensor_scalar(bqs[:], bqT[:], SCALE, None, ALU.mult).then_inc(bq_scaled, 1)
            dve.wait_ge(std_ready, 1)
            dve.reciprocal(rstd[:], std[:]).then_inc(stat_step, 1)
            dve.wait_ge(stat_step, 2 * TILES + 1)

            def norm(n):
                at_least(dve, xn_turned, n - 1)
                dve.tensor_scalar(xn[n % 2][:], resid[:, n, :], moments[:, n, 0:1], rstd[:, n:n + 1], ALU.subtract, ALU.mult).then_inc(xn_ready, 1)

            norm(0)
            norm(1)
            for c in range(SC):
                ctx_sum(0, c)
            split(wq_raw, wqh, wql, 3)
            for n in range(TILES):
                h, t = n // (TILES // 2), n % (TILES // 2)
                dve.wait_ge(xt_high, n + 1)
                dve.tensor_tensor(xtl[h][:, :, t * P:(t + 1) * P], S_ps[n % 2][:].rearrange("p (c t) -> p c t", c=DC),
                                  xth[h][:, :, t * P:(t + 1) * P].bitcast(F32), ALU.subtract).then_inc(xt_low, 1)
                if n + 2 < TILES:
                    norm(n + 2)
                if n >= TILES - SC:
                    ctx_chunk(1, 1, n - TILES + SC)

            def clamp(n, par):
                dve.wait_ge(exp_done, n + 1)
                dve.tensor_scalar(probs[par][:], probs[par][:], 1.0, bounds[par][:], ALU.min, ALU.max).then_inc(clipped, 1)

            def copy_turned(n, par):
                dve.wait_ge(turned, n + 1)
                dve.tensor_copy(probsT[par][:], T_ps[par][:]).then_inc(turned_copied, 1)

            def take_outputs(b, half):
                g = b * 2 + half
                dve.wait_ge(pv_ready, g * 4 + 4)
                o = O_ps[:, 0:4 * (VW - 1)].rearrange("p (h e) -> p h e", h=4)
                dve.reciprocal(rsum[:], o[:, :, 2 * DH]).then_inc(sum_inverted, 1)
                dve.wait_ge(sum_inverted, g + 1)
                for e in range(2):
                    rows = slice(64 * e, 64 * e + 64)
                    dst = outs[rows, bass.ds(b, 1), half * P:(half + 1) * P].rearrange("p b (h e) -> p (b h) e", h=4)
                    dve.tensor_tensor(dst, o[rows, :, e * DH:(e + 1) * DH],
                                      rsum[rows].unsqueeze(2).to_broadcast((64, 4, DH)), ALU.mult).then_inc(out_taken, 1)

            def step(b, par, more, turn):
                first = isinstance(b, int) and b == 0
                for j in range(PAIRS):
                    n = b * PAIRS + j
                    if more and not (first and j == 0):
                        clamp(n - 1, (j - 1) % 2)
                    dve.wait_ge(scores_ready, n + 1)
                    dve.tensor_reduce(rawmax[j % 2][:], S_ps[j % 2][:], X, ALU.max, negate=True).then_inc(rawmax_ready, 1)
                    dve.wait_ge(rawmax_ready, n + 1)
                    dve.tensor_scalar(negmax[j % 2][:], rawmax[j % 2][:], CLAMP, -CLAMP, ALU.min, ALU.max).then_inc(max_ready, 1)
                    if j > 0 and more:
                        unit(b + 1, 1 - par, j - 1)
                    if turn and j >= PAIRS - SC:
                        ctx_chunk(b + 2, par, j - PAIRS + SC)
                    if not more:
                        clamp(n - 1, (j - 1) % 2)
                        if j > 0:
                            copy_turned(n - 2, j % 2)
                    elif not (first and j == 0):
                        copy_turned(n - 1, (j - 1) % 2)
                    if j == (1 if more else 2) and not first:
                        take_outputs(b - 1, 1)
                    if j == (5 if more else 6):
                        take_outputs(b, 0)

            steps(dve, step)
            clamp(B * PAIRS - 1, 1)
            copy_turned(B * PAIRS - 2, 0)
            copy_turned(B * PAIRS - 1, 1)
            take_outputs(B - 1, 1)

        @block.tensor
        def _(pe):
            def ctx_chunk(b, par, c):
                if c == 0:
                    if par == 0:
                        pe.wait_ge(ctx_loaded[0], (b // 2 + 1) * DMA if isinstance(b, int) else b * (DMA // 2) + DMA)
                    else:
                        pe.wait_ge(ctx_loaded[1], (b // 2 + 1) * DMA if isinstance(b, int) else b * (DMA // 2) + DMA // 2)
                if isinstance(b, int) and b < 2:
                    at_least(pe, ctx_low, b * (SC + c + 1))
                else:
                    pe.wait_ge(ctx_low, (b * SC + c) * 2)
                for d in range(CC):
                    mm = pe.transpose(chunk_bank(b, c)[:, d * P:(d + 1) * P], ctx_rows[par][:, c, d * P:(d + 1) * P], ident[:])
                mm.then_inc(ctx_turned, 1)

            def unit(b, par, u, part):
                first = isinstance(b, int) and b == 0
                out = U_ps[u % 2][:]
                if part == 0:
                    if u == 0 and not first:
                        pe.wait_ge(ctx_low, (b * SC + SC) * 2)
                    if u in (0, 1):
                        at_least(pe, v_ready, b * SC - 1 + u)
                        if isinstance(b, int) and b == 1:
                            pe.wait_ge(q_copied, 2 * DC - 1 + u)
                    elif u - 2 < DC:
                        pe.wait_ge(k_low, (b * DC + u - 1) * 2)
                    else:
                        pe.wait_ge(v_ready, b * SC + u - 1 - DC)
                if u < DC:
                    cols = slice(u * P, (u + 1) * P)
                    ops = [(wkh[:, c, cols], cth[par][:, c, :]) for c in range(CC)]
                    ops += [(wkh[:, c, cols], ctl[par][:, c, :]) for c in range(CC)]
                    ops += [(wkl[:, c, cols], cth[par][:, c, :]) for c in range(CC)]
                else:
                    cols = slice((u - DC) * P, (u - DC + 1) * P)
                    ops = [(cth[par][:, c, cols], wvh[:, c, :]) for c in range(CC)]
                    ops += [(cth[par][:, c, cols], wvl[:, c, :]) for c in range(CC)]
                    ops += [(ctl[par][:, c, cols], wvh[:, c, :]) for c in range(CC)]
                cut = 5
                for k in range(cut) if part == 0 else range(cut, len(ops)):
                    if first and u == 0 and k % CC == 0:
                        if k == 0:
                            pe.wait_ge(ctx_high, SC)
                        else:
                            pe.wait_ge((ctx_low, w_split)[k // CC - 1], (SC, 1)[k // CC - 1])
                    mm = pe.matmul(out, ops[k][0], ops[k][1], start=(k == 0), stop=(k == len(ops) - 1))
                if part == 1:
                    mm.then_inc(unit_ready, 1)

            pe.wait_ge(ident_ready, 2)
            for c in range(SC):
                ctx_chunk(0, 0, c)
            for u in range(UNITS):
                if u == DC:
                    pe.wait_ge(w_split, 2)
                unit(0, 0, u, 0)
                unit(0, 0, u, 1)

            def turn_norm(n):
                pe.wait_ge(xn_ready, n + 1)
                at_least(pe, xt_low, n - 1)
                for c in range(DC):
                    mm = pe.transpose(S_ps[n % 2][:, c * P:(c + 1) * P], xn[n % 2][:, c * P:(c + 1) * P], ident[:])
                mm.then_inc(xn_turned, 1)

            for n in range(TILES // 2):
                turn_norm(n)
                if n > 0:
                    ctx_chunk(1, 1, n - 1)
            ctx_chunk(1, 1, SC - 1)
            pe.wait_ge(w_split, 3)
            for k in range(2 * DC):
                h, m = k // DC, k % DC
                if k < TILES // 2:
                    turn_norm(TILES // 2 + k)
                pe.wait_ge(xt_low, (h + 1) * (TILES // 2))
                if k < 2:
                    pe.wait_ge(v_ready, SC)
                else:
                    pe.wait_ge(q_copied, k - 1)
                three_products(pe, U_ps[m % 2][:], lambda c: wqh[:, c, m * P:(m + 1) * P], lambda c: wql[:, c, m * P:(m + 1) * P],
                               lambda c: xth[h][:, c, :], lambda c: xtl[h][:, c, :], DC).then_inc(q_ready, 1)

            def scores(b, par, j):
                n = b * PAIRS + j
                g, rows = j // 2, slice(64 * (j % 2), 64 * (j % 2) + 64)
                if j == 0:
                    pe.wait_ge(q_spread, b * 4 + 4)
                    pe.wait_ge(q_doubled, b * 4 + 4)
                if j % 2 == 0:
                    pe.wait_ge(k_low, (b * DC + g + 1) * 2)
                at_least(pe, exp_done, n - 1)
                out = S_ps[j % 2][:]
                pe.matmul(out, qdh[par][:, j, :], keys[par][:, j, :], start=True, stop=False)
                pe.matmul(out, qdl[par][rows, g, :], keys[par][rows, j, :], start=False, stop=True).then_inc(scores_ready, 1)

            def turn_probs(n, par):
                pe.wait_ge(clipped, n + 1)
                at_least(pe, turned_copied, n - 1)
                for c in range(SC):
                    mm = pe.transpose(T_ps[par][:, c * P:(c + 1) * P], probs[par][:, c * P:(c + 1) * P], ident[:])
                mm.then_inc(turned, 1)

            def weighted_values(b, vpar, j):
                n = b * PAIRS + j
                pe.wait_ge(turned_copied, n + 1)
                if j == 0:
                    pe.wait_ge(v_ready, b * SC + SC)
                if j % 4 == 0:
                    at_least(pe, out_taken, b * 4 + j // 2)
                w = VW - 1
                for c in range(SC):
                    mm = pe.matmul(O_ps[:, (j % 4) * w:(j % 4 + 1) * w], probsT[j % 2][:, c * P:(c + 1) * P], vals[vpar][:, c, j, 0:w],
                                   start=(c == 0), stop=(c == SC - 1))
                mm.then_inc(pv_ready, 1)

            def step(b, par, more, turn):
                first = isinstance(b, int) and b == 0
                for j in range(PAIRS):
                    n = b * PAIRS + j
                    scores(b, par, j)
                    if more:
                        unit(b + 1, 1 - par, j, 0)
                    if not more:
                        if j > 0:
                            turn_probs(n - 2, j % 2)
                        if j >= 3:
                            weighted_values(b, par, j - 3)
                        elif j > 0:
                            weighted_values(b - 1, 1 - par, PAIRS + j - 3)
                        continue
                    if not (first and j < 1):
                        turn_probs(n - 1, (j - 1) % 2)
                    if j >= 2:
                        weighted_values(b, par, j - 2)
                    elif not first:
                        weighted_values(b - 1, 1 - par, PAIRS + j - 2)
                    if more:
                        unit(b + 1, 1 - par, j, 1)
                    if turn and PAIRS - SC - 1 <= j < PAIRS - 1:
                        ctx_chunk(b + 2, par, j - PAIRS + SC + 1)

            steps(pe, step)
            turn_probs(B * PAIRS - 2, 0)
            weighted_values(B - 1, 1, PAIRS - 3)
            turn_probs(B * PAIRS - 1, 1)
            weighted_values(B - 1, 1, PAIRS - 2)
            weighted_values(B - 1, 1, PAIRS - 1)
    arena.at = base


class CrossWeights:

    def __init__(self, nc, sh, st, arena, Wv, bv, Wo, bo):
        self.nc, self.sh, self.Wv, self.bv, self.Wo, self.bo = nc, sh, Wv, bv, Wo, bo
        self.bvT = arena.place("bvT", [P, sh.DC], F32)
        self.bo_rows = arena.place("bo_rows", [P, sh.D], F32)
        self.wo_loaded = st.enter_context(nc.semaphore("wo_loaded"))
        self.wv_loaded = st.enter_context(nc.semaphore("wv_again"))
        self.bv_loaded = st.enter_context(nc.semaphore("bv_loaded"))
        self.bo_loaded = st.enter_context(nc.semaphore("bo_loaded"))

    def place(self, arena):
        sh = self.sh
        self.wo_raw = arena.place("wo_raw", [P, sh.DC, sh.D], F32, at=self.at)
        self.wv = arena.place("wv_all", [P, sh.CC, sh.D], F32, at=self.at + 4 * sh.DC * sh.D)

    def fetch(self, sp):
        wo = by_pair_group(self.Wo)
        bv = by_pair_group(self.bv.rearrange("(n o) -> n o", o=1))
        for p in range(4):
            rows = slice(32 * p, 32 * p + 32)
            for g in range(2):
                sp.dma_start(self.wo_raw[rows, 2 * g:2 * g + 2, :], wo[p][:, g]).then_inc(self.wo_loaded, DMA)
        sp.dma_start(self.wv[:], self.Wv.rearrange("(c p) n -> p c n", p=P)).then_inc(self.wv_loaded, DMA)
        with self.nc.allow_non_contiguous_dma(reason="a bias of 512 values, turned"):
            for p in range(4):
                rows = slice(32 * p, 32 * p + 32)
                for g in range(2):
                    sp.dma_start(self.bvT[rows, 2 * g:2 * g + 2], bv[p][:, g, :, 0]).then_inc(self.bv_loaded, DMA)
        sp.dma_start(self.bo_rows[:], self.bo.partition_broadcast(P)).then_inc(self.bo_loaded, DMA)


class FeedForwardWeights:
    QMAX = 127.0
    MAGIC = 1.5 * 2.0 ** 23
    LORA = 2.0
    PARTS = 8

    def __init__(self, nc, sh, st, arena, W_fc, W_proj, lora):
        self.sh, self.W_fc, self.W_proj = sh, W_fc, W_proj
        self.lora = lora
        self.R = lora[0].shape[0]
        self.scale, self.inv, self.twice = (arena.place(name, [P, 2], F32) for name in ("wscale", "winv", "wtwice"))
        self.absmax = arena.place("absmax", [P, 2, self.PARTS], F32)
        self.wmax, self.allmax = arena.place("wmax", [P, 2], F32), arena.place("allmax", [P, 2], F32)
        self.fc_tiles = sh.TILES // 2
        self.late = sh.TILES - 3
        self.early = 8
        self.loaded = [st.enter_context(nc.semaphore(f"ffw_loaded{i}")) for i in range(2)]
        self.loaded_late = st.enter_context(nc.semaphore("ffw_loaded_late"))
        self.lora_loaded = st.enter_context(nc.semaphore("ffw_lora_loaded"))
        self.rounded = st.enter_context(nc.semaphore("ffw_rounded"))
        self.clipped = st.enter_context(nc.semaphore("ffw_clipped"))
        self.clipped_last = st.enter_context(nc.semaphore("ffw_clipped_last"))

    def part(self, n):
        if n < self.PARTS:
            return self.W_fc.rearrange("(k p a) d -> k p (a d)", k=self.PARTS, p=P)[n]
        n -= self.PARTS
        half = self.sh.F // 2
        return self.W_proj[(n // 2) * P:(n // 2 + 1) * P, (n % 2) * half:(n % 2 + 1) * half]

    def fetch(self, sp, qk, t):
        done = self.loaded_late if t >= self.late else self.loaded[t % 2]
        for i in range(4):
            if t < 4:
                src = self.W_fc[(4 * t + i) * P:(4 * t + i + 1) * P, :]
            else:
                src = self.W_proj[i * P:(i + 1) * P, (t - 4) * BANK:(t - 3) * BANK]
            sp.dma_start(qk[:, 4 * i:4 * i + 4, t * P:(t + 1) * P], src.rearrange("p (c n) -> p c n", c=4)).then_inc(done, DMA)

    def round(self, act, qk, t, i, w):
        piece = qk[:, 4 * i:4 * i + 4, bass.ds(t * P, P)]
        act.activation(piece, piece, ACT.Copy, scale=self.inv[:, w:w + 1], bias=self.MAGIC).then_inc(self.rounded, 1)

    def place_lora(self, nc, at):
        sh, R = self.sh, self.R
        self.a_raw = nc.alloc_sbuf_tensor_at("a_raw", [R, sh.D + sh.F], F32, offset=at)
        b_at = at + 4 * (sh.D + sh.F)
        self.b_raw = nc.alloc_sbuf_tensor_at("b_raw", [P, sh.F // P + sh.DC, R], F32, offset=b_at)
        return b_at + 4 * (sh.F // P + sh.DC) * R

    def fetch_lora(self, sp):
        A_fc, B_fc, A_proj, B_proj = self.lora
        D, FT = self.sh.D, self.sh.F // P
        for dst, src in ((self.b_raw[:, 0:FT, :], B_fc.rearrange("(t p) r -> p t r", p=P)), (self.b_raw[:, FT:, :], B_proj.rearrange("(t p) r -> p t r", p=P)),
                         (self.a_raw[:, 0:D], A_fc), (self.a_raw[:, D:], A_proj)):
            sp.dma_start(dst, src).then_inc(self.lora_loaded, DMA)

    def turn_fc(self, pe, qk, ident, bank, k):
        for c in range(self.sh.DC):
            mm = pe.transpose(bank[:, c * P:(c + 1) * P], qk[:, 4 * (k % 4) + c, k // 4 * P:(k // 4 + 1) * P], ident[:])
        return mm

    def clip(self, eng, qk, t, i, done):
        piece = qk[:, 4 * i:4 * i + 4, bass.ds(t * P, P)]
        eng.tensor_scalar(piece, piece, self.MAGIC + self.QMAX, self.MAGIC - self.QMAX - 1, ALU.min, ALU.max).then_inc(done, 1)


def latent_block(nc, sh, later, ffw, arena, resid, ident, ctxsum, nansum, O_all, w_qkv, ln_beta):
    D, TOK, TILES, DC, CC, B, Q = sh.D, sh.TOK, sh.TILES, sh.DC, sh.CC, sh.B, sh.Q
    INNER = sh.INNER
    COLS = 512
    WBLOCKS = 3 * INNER // COLS
    QK = 2 * INNER // COLS
    G = INNER // P
    HEADS = INNER // 32
    VW = 33
    HALF = TOK // 2
    base = arena.at
    with ExitStack() as st:
        def sem(name):
            return st.enter_context(nc.semaphore(name))

        def psum(name):
            return st.enter_context(nc.psum_tensor(name, [P, BANK], F32))

        place = arena.place
        region = O_all[1]
        arena.at = region
        qk = place("qk", [P, 2 * G, TOK], F32)
        woh, wol = later.woh, later.wol
        early = Arena(nc, region + 32 * 1024)
        at = [early.place(f"at{i}", [P, D], F32) for i in range(2)]
        ath = [early.place(f"ath{i}", [P, DC, P], F32R) for i in range(2)]
        atl = [early.place(f"atl{i}", [P, DC, P], F32R) for i in range(2)]
        xn = [early.place(f"lxn{i}", [P, D], F32) for i in range(2)]
        ctxmean = early.place("ctxmean", [P, B, CC], F32)
        uniform = early.place("uniform", [P, DC, B], F32)
        isnan = early.place("isnan", [P, nansum.shape[1]], F32)
        anynan = early.place("anynan", [P, 1], F32)
        flag = early.place("flag", [P, 1], F32)
        assert early.at <= region + 64 * 1024
        xnh, xnl = place("xnh", [P, DC, TOK], F32R), place("xnl", [P, DC, TOK], F32R)
        w_at = arena.at
        w_raw = [place(f"w_raw{i}", [P, DC, COLS], F32) for i in range(2)]
        wh = [place(f"wh{i}", [P, DC, COLS], F32R) for i in range(2)]
        wl = [place(f"wl{i}", [P, DC, COLS], F32R) for i in range(2)]
        vals = place("lvals", [P, TILES, HEADS, VW], F32)
        stats = place("lstats", [P, TILES, 6], F32)
        moments = place("lmoments", [P, TILES, 2], F32)
        std = place("lstd", [P, TILES], F32)
        rstd = place("lrstd", [P, TILES], F32)
        beta_rows = place("beta_rows", [P, D], F32)
        part = [place(f"ffw_part{i}", [P, 1024], F32) for i in range(2)]
        kbd = [place(f"kbd{i}", [P, G // 2, 2, 4, Q], F32, at=w_at + 8 * 1024 * i) for i in range(2)]
        qt = [place(f"qt{i}", [P, G // 2, P], F32, at=w_at + 16 * 1024 + 2 * 1024 * i) for i in range(2)]
        assert arena.at <= 229368, arena.at

        A_ps = [psum(f"A_ps{i}") for i in range(2)]
        Y_ps = [psum(f"Y_ps{i}") for i in range(2)]
        N_ps = [psum(f"N_ps{i}") for i in range(2)]
        U_ps = [psum(f"LU_ps{i}") for i in range(2)]

        w_loaded = [sem(f"w_loaded{i}") for i in range(2)]
        w_high, w_split_early, w_split = sem("w_high"), sem("w_split_early"), sem("w_split")
        ones_set = sem("ones_set")
        any_ready, flag_ready = sem("any_ready"), sem("flag_ready")
        mean_step, uniform_turned, uniform_ready = sem("mean_step"), sem("uniform_turned"), sem("uniform_ready")
        out_turned, at_biased, at_chosen, at_high, at_low = sem("out_turned"), sem("at_biased"), sem("at_chosen"), sem("at_high"), sem("at_low")
        y_ready, x_ready = sem("y_ready"), sem("x_ready")
        ln_step, var_ready, std_ready, rstd_ready, xn_ready = sem("ln_step"), sem("lvar_ready"), sem("lstd_ready"), sem("lrstd_ready"), sem("lxn_ready")
        xn_turned, xt_high, xt_low = sem("lxn_turned"), sem("lxt_high"), sem("lxt_low")
        unit_ready, unit_copied = sem("lunit_ready"), sem("lunit_copied")
        beta_loaded, beta_added, kbd_step = sem("beta_loaded"), sem("beta_added"), sem("kbd_step")
        part_loaded, part_seen = [sem(f"part_loaded{i}") for i in range(2)], sem("part_seen")
        wmax_ready, allmax_ready, scale_step = sem("wmax_ready"), sem("allmax_ready"), sem("scale_step")

        UNITS = 8
        block = st.enter_context(nc.Block())

        @block.sync
        def _(sp):
            for k in range(WBLOCKS):
                if 2 <= k < 4:
                    sp.wait_ge(w_split_early, 4 * (k - 1))
                at_least(sp, w_split, k - 3)
                src = w_qkv[:, k * COLS:(k + 1) * COLS].rearrange("(c p) n -> p c n", p=P)
                sp.dma_start(w_raw[k % 2][:], src).then_inc(w_loaded[k % 2], DMA)
                if k == 0:
                    sp.dma_start(beta_rows[:], ln_beta.partition_broadcast(P)).then_inc(beta_loaded, DMA)
                for n in range(*{WBLOCKS - 3: (0, 5), WBLOCKS - 2: (5, 10), WBLOCKS - 1: (10, 2 * ffw.PARTS)}.get(k, (0, 0))):
                    at_least(sp, part_seen, n - 1)
                    sp.dma_start(part[n % 2][:], ffw.part(n)).then_inc(part_loaded[n % 2], DMA)

        @block.gpsimd
        def _(pool):
            def split_piece(n):
                k, c = n // 4, n % 4
                pool.wait_ge(w_high, n + 1)
                pool.tensor_tensor(wl[k][:, c, :], w_raw[k][:, c, :], wh[k][:, c, :].bitcast(F32), ALU.subtract).then_inc(w_split_early, 1)

            for t in range(TILES):
                if t == 0:
                    pool.wait_ge(any_ready, 1)
                    pool.partition_all_reduce(flag[:], anynan[:], P, MAX).then_inc(flag_ready, 1)
                pool.wait_ge(at_high, t + 1)
                at_least(pool, y_ready, t - 1)
                pool.tensor_tensor(atl[t % 2][:].rearrange("p k (b q) -> p b k q", b=2), at[t % 2][:].rearrange("p (b k q) -> p b k q", b=2, k=DC),
                                   ath[t % 2][:].bitcast(F32).rearrange("p k (b q) -> p b k q", b=2), ALU.subtract).then_inc(at_low, 1)
                if t >= 1:
                    split_piece(t - 1)
            split_piece(2 * DC - 1)
            pool.wait_ge(beta_loaded, DMA)
            pool.wait_ge(xn_ready, TILES)
            for t in range(TILES):
                pool.tensor_tensor(resid[:, t, :], resid[:, t, :], beta_rows[:], ALU.add).then_inc(beta_added, 1)
            pool.wait_ge(w_split, WBLOCKS - 2)
            for i in range(2):
                pool.memset(kbd[i][:], 0.0).then_inc(kbd_step, 1)
            pool.wait_ge(unit_copied, QK * UNITS)
            for f in range(2):
                for r in range(4):
                    pool.wait_ge(kbd_step, 2 + 4 * f + r)
                    spread(pool.tensor_copy, qk, kbd, 0, f, r).then_inc(kbd_step, 1)
            pool.wait_ge(kbd_step, 10)
            pool.wait_ge(unit_ready, (WBLOCKS - 1) * UNITS)
            for f in range(2):
                pool.tensor_copy(qt[f][:], qk[:, f * (G // 2):(f + 1) * (G // 2), 0:P]).then_inc(kbd_step, 1)
            for w in range(2):
                pool.wait_ge(wmax_ready, w + 1)
                pool.partition_all_reduce(ffw.allmax[:, w:w + 1], ffw.wmax[:, w:w + 1], P, MAX).then_inc(allmax_ready, 1)

        @block.scalar
        def _(act):
            def root(t):
                act.wait_ge(var_ready, t + 1)
                act.activation(std[:, t:t + 1], moments[:, t, 1:2], ACT.Sqrt).then_inc(std_ready, 1)

            def high(t):
                act.wait_ge(xn_turned, t + 1)
                act.copy(xnh[:, :, t * P:(t + 1) * P], N_ps[t % 2][:].rearrange("p (c t) -> p c t", c=DC)).then_inc(xt_high, 1)

            def split_high(k):
                act.wait_ge(w_loaded[k % 2], (k // 2 + 1) * DMA)
                at_least(act, unit_ready, (k - 1) * UNITS)
                act.copy(wh[k % 2][:], w_raw[k % 2][:]).then_inc(w_high, DC)

            def outputs_biased(t):
                act.wait_ge(out_turned, t + 1)
                at_least(act, at_low, t - 1)
                for k in range(DC):
                    src, dst = (bank[:].rearrange("p (b k q) -> p b k q", b=2, k=DC)[:, :, k, :] for bank in (A_ps[t % 2], at[t % 2]))
                    act.activation(dst, src, ACT.Identity, bias=later.bvT[:, k:k + 1]).then_inc(at_biased, 1)

            def outputs_high(t):
                act.wait_ge(at_chosen, t + 1)
                at_least(act, y_ready, t - 1)
                act.copy(ath[t % 2][:].rearrange("p k (b q) -> p b k q", b=2), at[t % 2][:].rearrange("p (b k q) -> p b k q", b=2, k=DC)).then_inc(at_high, 1)

            act.wait_ge(later.bv_loaded, 8 * DMA)
            for t in range(2):
                outputs_biased(t)
                outputs_high(t)
            for t in range(TILES):
                if t + 2 < TILES:
                    outputs_biased(t + 2)
                k, c = t // 4, t % 4
                act.wait_ge(w_loaded[k], DMA)
                act.copy(wh[k][:, c, :], w_raw[k][:, c, :]).then_inc(w_high, 1)
                if t >= 1:
                    root(t - 1)
                if t >= 2:
                    high(t - 2)
                if t + 2 < TILES:
                    outputs_high(t + 2)
            root(TILES - 1)

            def unit(n):
                act.wait_ge(unit_ready, n + 1)
                if n < QK * UNITS:
                    m, h = n // UNITS * 4 + n % 4, n % UNITS // 4
                    act.copy(qk[:, m, h * HALF:(h + 1) * HALF], U_ps[n % 2][:]).then_inc(unit_copied, 1)
                else:
                    if n == QK * UNITS:
                        act.wait_ge(ones_set, 1)
                    vb, t = (n - QK * UNITS) // UNITS, n % UNITS
                    act.copy(vals[:, t, vb * 16:(vb + 1) * 16, 0:32], U_ps[n % 2][:].rearrange("p (h e) -> p h e", h=16)).then_inc(unit_copied, 1)

            high(TILES - 2)
            unit(0)
            high(TILES - 1)
            for n in range(1, WBLOCKS * UNITS):
                if n % UNITS == 0 and n < (WBLOCKS - 1) * UNITS:
                    split_high(n // UNITS + 1)
                unit(n)

        @block.vector
        def _(dve):
            dve.tensor_tensor(isnan[:], nansum[:], nansum[:], ALU.not_equal).then_inc(mean_step, 1)
            dve.tensor_reduce(ctxmean[:], ctxsum[:].rearrange("p b s c -> p b c s"), X, ALU.add).then_inc(mean_step, 1)
            dve.wait_ge(mean_step, 1)
            dve.tensor_reduce(anynan[:], isnan[:], X, ALU.max).then_inc(any_ready, 1)
            dve.wait_ge(mean_step, 2)
            dve.tensor_scalar(ctxmean[:], ctxmean[:], 1.0 / sh.S, None, ALU.mult).then_inc(mean_step, 1)
            dve.wait_ge(uniform_turned, 1)
            dve.wait_ge(later.bv_loaded, 8 * DMA)
            dve.tensor_tensor(uniform[:], Y_ps[1][:, 0:DC * B].rearrange("p (k b) -> p k b", k=DC),
                              later.bvT[:].unsqueeze(2).to_broadcast((P, DC, B)), ALU.add).then_inc(uniform_ready, 1)
            dve.wait_ge(uniform_ready, 1)
            dve.wait_ge(flag_ready, 1)

            def outputs(t):
                dve.wait_ge(at_biased, DC * (t + 1))
                dve.copy_predicated(at[t % 2][:].rearrange("p (b k q) -> p b k q", b=2, k=DC),
                                    flag[:].bitcast(I32).unsqueeze(1).unsqueeze(2).to_broadcast((P, 2, DC, Q)),
                                    uniform[:, :, 2 * t:2 * t + 2].rearrange("p k b -> p b k").unsqueeze(3).to_broadcast((P, 2, DC, Q))).then_inc(at_chosen, 1)

            def residual(t):
                dve.wait_ge(y_ready, t + 1)
                dve.tensor_tensor(resid[:, t, :], Y_ps[t % 2][:], resid[:, t, :], ALU.add).then_inc(x_ready, 1)
                dve.wait_ge(x_ready, t + 1)
                dve.bn_stats(stats[:, t, :], resid[:, t, :]).then_inc(ln_step, 1)
                dve.wait_ge(ln_step, 2 * t + 1)
                dve.bn_aggr(moments[:, t, :], stats[:, t, :]).then_inc(ln_step, 1)
                dve.wait_ge(ln_step, 2 * t + 2)
                dve.tensor_scalar(moments[:, t, 1:2], moments[:, t, 1:2], 1e-5, None, ALU.add).then_inc(var_ready, 1)

            def norm(t):
                dve.wait_ge(std_ready, t + 1)
                dve.reciprocal(rstd[:, t:t + 1], std[:, t:t + 1]).then_inc(rstd_ready, 1)
                dve.wait_ge(rstd_ready, t + 1)
                at_least(dve, xn_turned, t - 1)
                dve.tensor_scalar(xn[t % 2][:], resid[:, t, :], moments[:, t, 0:1], rstd[:, t:t + 1], ALU.subtract, ALU.mult).then_inc(xn_ready, 1)

            def low(t):
                dve.wait_ge(xt_high, t + 1)
                dve.tensor_tensor(xnl[:, :, t * P:(t + 1) * P], N_ps[t % 2][:].rearrange("p (c t) -> p c t", c=DC),
                                  xnh[:, :, t * P:(t + 1) * P].bitcast(F32), ALU.subtract).then_inc(xt_low, 1)

            def split_low(k):
                dve.wait_ge(w_high, (k + 1) * DC)
                at_least(dve, unit_ready, (k - 1) * UNITS)
                dve.tensor_tensor(wl[k % 2][:], w_raw[k % 2][:], wh[k % 2][:].bitcast(F32), ALU.subtract).then_inc(w_split, 1)

            outputs(0)
            outputs(1)
            for t in range(TILES + 3):
                if 3 <= t < TILES:
                    low(t - 3)
                if t == TILES:
                    residual(t - 1)
                if 2 <= t <= TILES + 1:
                    norm(t - 2)
                if 1 <= t < TILES:
                    residual(t - 1)
                if t + 2 < TILES:
                    outputs(t + 2)
                if t >= TILES:
                    low(t - 3)
            dve.memset(vals[:, :, :, VW - 1:VW], 1.0).then_inc(ones_set, 1)
            for n in range(2 * ffw.PARTS):
                w, k = n // ffw.PARTS, n % ffw.PARTS
                if n in (0, 5, 10):
                    split_low(2 + n // 5)
                dve.wait_ge(part_loaded[n % 2], (n // 2 + 1) * DMA)
                dve.tensor_reduce(ffw.absmax[:, w, k:k + 1], part[n % 2][:], X, ALU.max, apply_absolute_value=True).then_inc(part_seen, 1)
            split_low(WBLOCKS - 1)
            dve.wait_ge(part_seen, 2 * ffw.PARTS)
            for w in range(2):
                dve.tensor_reduce(ffw.wmax[:, w:w + 1], ffw.absmax[:, w, :], X, ALU.max).then_inc(wmax_ready, 1)
            dve.wait_ge(allmax_ready, 2)
            dve.tensor_scalar(ffw.scale[:], ffw.allmax[:], 1.0 / ffw.QMAX, None, ALU.mult).then_inc(scale_step, 1)
            dve.wait_ge(scale_step, 1)
            dve.reciprocal(ffw.inv[:], ffw.scale[:]).then_inc(scale_step, 1)
            dve.wait_ge(scale_step, 2)
            dve.tensor_scalar(ffw.twice[:], ffw.inv[:], ffw.LORA, None, ALU.mult).then_inc(scale_step, 1)

        @block.tensor
        def _(pe):
            def turn_outputs(t):
                at_least(pe, at_biased, DC * (t - 1))
                for b in range(2):
                    for g in range(2):
                        mm = pe.transpose(A_ps[t % 2][:, (2 * b + g) * P:(2 * b + g + 1) * P], O_all[0][:, 2 * t + b, g * P:(g + 1) * P], ident[:])
                mm.then_inc(out_turned, 1)

            def project(t):
                pe.wait_ge(at_low, t + 1)
                if t == 1:
                    pe.wait_ge(uniform_ready, 1)
                at_least(pe, x_ready, t - 1)
                three_products(pe, Y_ps[t % 2][:], lambda c: ath[t % 2][:, c, :], lambda c: atl[t % 2][:, c, :],
                               lambda c: woh[:, c, :], lambda c: wol[:, c, :], DC).then_inc(y_ready, 1)

            def turn_norm(t):
                pe.wait_ge(xn_ready, t + 1)
                at_least(pe, xt_low, t - 1)
                for c in range(DC):
                    mm = pe.transpose(N_ps[t % 2][:, c * P:(c + 1) * P], xn[t % 2][:, c * P:(c + 1) * P], ident[:])
                mm.then_inc(xn_turned, 1)

            def unit(n):
                k, u = n // UNITS, n % UNITS
                par = k % 2
                if u == 0:
                    if k < 2:
                        pe.wait_ge(w_split_early, (k + 1) * DC)
                    else:
                        pe.wait_ge(w_split, k - 1)
                if n in (0, 4):
                    pe.wait_ge(xt_low, TILES // 2 * (n // 4 + 1))
                at_least(pe, unit_copied, n - 1)
                if k < QK:
                    cols, toks = slice(u % 4 * P, (u % 4 + 1) * P), slice(u // 4 * HALF, (u // 4 + 1) * HALF)
                    mm = three_products(pe, U_ps[n % 2][:], lambda c: wh[par][:, c, cols], lambda c: wl[par][:, c, cols],
                                        lambda c: xnh[:, c, toks], lambda c: xnl[:, c, toks], DC)
                else:
                    toks = slice(u * P, (u + 1) * P)
                    mm = three_products(pe, U_ps[n % 2][:], lambda c: xnh[:, c, toks], lambda c: xnl[:, c, toks],
                                        lambda c: wh[par][:, c, :], lambda c: wl[par][:, c, :], DC)
                mm.then_inc(unit_ready, 1)

            turn_outputs(0)
            turn_outputs(1)
            pe.wait_ge(mean_step, 3)
            pe.wait_ge(later.wv_loaded, DMA)
            for k in range(DC):
                for p in range(4):
                    head = 8 * (k // 2) + 2 * p + k % 2
                    for c in range(CC):
                        mm = pe.matmul(Y_ps[1][32 * p:32 * p + 32, k * B:(k + 1) * B], later.wv[:, c, 32 * head:32 * head + 32],
                                       ctxmean[:, :, c], start=(c == 0), stop=(c == CC - 1))
            mm.then_inc(uniform_turned, 1)
            for t in range(TILES + 2):
                if t + 2 < TILES:
                    turn_outputs(t + 2)
                if t < TILES:
                    project(t)
                if t >= TILES:
                    unit(t - TILES)
                if t >= 2:
                    turn_norm(t - 2)
            for n in range(2, WBLOCKS * UNITS):
                unit(n)
    arena.at = base
    return qk, vals, (kbd, qt)


def spread(copy, qk, kbd, t, f, r):
    G = qk.shape[1] // 2
    rows = slice(32 * r, 32 * r + 32)
    g0 = G + f * (G // 2)
    src = qk[rows, g0:g0 + G // 2, bass.ds(t * P, P)].rearrange("d g (b k) -> d g b k", b=2)
    return copy(kbd[f][rows, :, :, r, :], src)


def self_attention_block(nc, sh, ffw, bout_rows, region, resid, ident, qk, vals, taken, w_out, b_out, ln_gamma, x_stats):
    D, TILES, Q = sh.D, sh.TILES, sh.Q
    INNER = sh.INNER
    G = INNER // P
    KC = INNER // P
    OCTETS = INNER // 32 // 8
    SCALE = 32 ** -0.5
    VW = 33
    with ExitStack() as st:
        def sem(name):
            return st.enter_context(nc.semaphore(name))

        def psum(name):
            return st.enter_context(nc.psum_tensor(name, [P, BANK], F32))

        mid = Arena(nc, region + 64 * 1024)
        woh = mid.place("owh", [P, KC, D], F32R)
        wol_at = mid.at
        wol = mid.place("owl", [P, KC, D], F32R)
        wo_raw = mid.place("ow_raw", [P, KC, D], F32, at=wol_at)
        kbd, qt = taken
        mid.at += 20 * 1024
        shifted = [mid.place(f"shifted{i}", [P, BANK], F32) for i in range(2)]
        probs_at = mid.at
        probs = [mid.place(f"sprobs{i}", [P, 8, P], F32) for i in range(2)]
        last_oth = mid.place("last_oth", [P, KC, P], F32R, at=probs_at)
        last_otl = mid.place("last_otl", [P, KC, P], F32R, at=probs_at + 8 * P * 4)
        outs = mid.place("souts", [P, INNER], F32)
        oth, otl = mid.place("oth", [P, KC, P], F32R), mid.place("otl", [P, KC, P], F32R)
        y_rows = [mid.place(f"y_rows{i}", [P, D], F32) for i in range(2)]
        wfT = nc.alloc_sbuf_tensor_at("wfT", [P, sh.DC, sh.F], F32R, offset=region + 64 * 1024)
        assert mid.at <= region + 144 * 1024
        assert ffw.place_lora(nc, region + 144 * 1024) <= region + 144 * 1024 + 4 * 4 * VW * (INNER // 32)
        end = Arena(nc, region + 177 * 1024)
        probsT = [end.place(f"sprobsT{i}", [P, 8, P], F32) for i in range(2)]
        gamma_rows = end.place("gamma_rows", [P, D], F32)
        y_stats = [end.place(f"y_stats{i}", [P, 6], F32) for i in range(2)]
        y_moments = end.place("y_moments", [P, 2, 2], F32)
        y_std, y_rstd = end.place("y_std", [P, 2], F32), end.place("y_rstd", [P, 2], F32)
        rsum = end.place("srsum", [P, 8], F32)
        no_use = end.place("no_use", [P, 1], F32)
        rowmax = [end.place(f"rowmax{i}", [P, 8], F32) for i in range(2)]

        S_ps = [psum(f"SS_ps{i}") for i in range(2)]
        T_ps = [psum(f"ST_ps{i}") for i in range(2)]
        A_ps = [psum(f"SA_ps{i}") for i in range(2)]
        O_ps, Y_ps = psum("SO_ps"), psum("SY_ps")
        turned_fc = A_ps + T_ps + S_ps

        w_loaded, b_loaded = sem("ow_loaded"), sem("ob_loaded")
        w_high, w_split = sem("ow_high"), sem("ow_split")
        zeroed = sem("zeroed")
        q_taken, k_spread = sem("q_taken"), [sem(f"k_spread{i}") for i in range(2)]
        scores_ready, max_ready, shifted_ready = sem("sscores_ready"), sem("smax_ready"), sem("shifted_ready")
        exp_done = sem("sexp_done")
        turned, turned_copied = sem("sturned"), [sem(f"sturned_copied{i}") for i in range(2)]
        pv_ready, sum_inverted, out_taken = sem("spv_ready"), sem("ssum_inverted"), sem("sout_taken")
        outs_turned, ot_high, ot_low = sem("outs_turned"), sem("ot_high"), sem("ot_low")
        y_ready, y_copied, stat_step = sem("sy_ready"), sem("sy_copied"), sem("sstat_step")
        y_moved, y_var_ready, y_std_ready, y_inverted = sem("y_moved"), sem("y_var_ready"), sem("y_std_ready"), sem("y_inverted")
        y_normed, y_scaled, x_ready = sem("y_normed"), sem("y_scaled"), sem("sx_ready")
        y_added, x_seen = sem("y_added"), sem("sx_seen")
        fc_turned, fc_copied = sem("fc_turned"), sem("fc_copied")

        def steps(eng, step):
            step(0, 0, 0)
            step(1, 1, 0)
            step(2, 0, 0)
            with eng.Fori(1, TILES // 2 - 1) as i:
                step(i * 2 + 1, 1, i)
                step(i * 2 + 2, 0, i)
            step(TILES - 1, 1, 0)

        block = st.enter_context(nc.Block())

        @block.sync
        def _(sp):
            sp.dma_start(wo_raw[:], w_out.rearrange("(c p) n -> p c n", p=P)).then_inc(w_loaded, DMA)
            sp.dma_start(bout_rows[:], b_out.partition_broadcast(P)).then_inc(b_loaded, DMA)
            sp.dma_start(gamma_rows[:], ln_gamma.partition_broadcast(P)).then_inc(b_loaded, DMA)
            for t in range(TILES):
                at_least(sp, q_taken, 2 * t)
                at_least(sp, k_spread[0], 4 * t)
                at_least(sp, k_spread[1], 4 * t)
                if t < ffw.late:
                    at_least(sp, ffw.rounded, 4 * (t - 1))
                ffw.fetch(sp, qk, t)
                if t == 5:
                    sp.wait_ge(pv_ready, 4 * OCTETS)
                    ffw.fetch_lora(sp)

        def spread_keys(eng, copy, t, f, r):
            spread(copy, qk, kbd, t, f, r).then_inc(k_spread[f], 1)

        @block.gpsimd
        def _(pool):
            for i in range(2):
                pool.memset(probs[i][:], 0.0).then_inc(zeroed, 1)
            pool.wait_ge(zeroed, 2)

            def take(t):
                for f in range(2):
                    at_least(pool, scores_ready, (t - 1) * OCTETS + 2 * f + 2)
                    at_least(pool, k_spread[0], (t - 1) * 4 + 4 * f)
                    pool.tensor_copy(qt[f][:], qk[:, f * (G // 2):(f + 1) * (G // 2), bass.ds(t * P, P)]).then_inc(q_taken, 1)
                    if f == 0:
                        pool.wait_ge(q_taken, 2 * (t - 1) + 1)
                        for r in range(4):
                            if r > 0:
                                pool.wait_ge(k_spread[0], (t - 1) * 4 + r)
                            spread_keys(pool, pool.tensor_copy, t, 0, r)

            def add_pair(t):
                for p in range(2):
                    m = t + p
                    x = resid[:, bass.ds(m, 1), :].rearrange("p o d -> p (o d)")
                    pool.wait_ge(y_normed, m + 1)
                    pool.tensor_tensor(y_rows[p][:], y_rows[p][:], gamma_rows[:], ALU.mult).then_inc(y_scaled, 1)
                    pool.wait_ge(y_scaled, m + 1)
                    pool.tensor_tensor(x, x, y_rows[p][:], ALU.add).then_inc(x_ready, 1)

            def step(t, par, i):
                if not (isinstance(t, int) and t == TILES - 1):
                    take(t + 1)
                if par == 0 and not (isinstance(t, int) and t < 4):
                    add_pair(t - 4)

            steps(pool, step)
            add_pair(TILES - 4)
            for n in range(4):
                pool.wait_ge(ffw.rounded, 4 * (TILES - 2) + n + 1)
                ffw.clip(pool, qk, TILES - 2, n, ffw.clipped_last)
            pool.wait_ge(q_taken, 2 * (TILES - 1))

        @block.scalar
        def _(act):
            act.activation(no_use[:], ident[:, 0:1], ACT.Exp, scale=0.0)
            act.wait_ge(zeroed, 2)

            def copy_turned(n, par):
                act.wait_ge(turned, 2 * n + 1)
                act.copy(probsT[par][:, 0:4, :], T_ps[0][:].rearrange("p (h q) -> p h q", h=4)).then_inc(turned_copied[0], 1)

            def outs_high(t, oth=oth):
                for f in range(2):
                    act.wait_ge(outs_turned, 2 * t + f + 1)
                    if oth is not last_oth:
                        at_least(act, y_ready, t)
                    act.copy(oth[:, 4 * f:4 * f + 4, :], A_ps[f][:].rearrange("p (c q) -> p c q", c=4)).then_inc(ot_high, 1)

            def root():
                act.activation(y_std[:], y_moments[:, :, 1], ACT.Sqrt).then_inc(y_std_ready, 1)

            def step(t, par, i):
                static = isinstance(t, int)
                first = static and t == 0
                pair = par == 0 and not (static and t < 4)
                for k in range(OCTETS):
                    n = t * OCTETS + k
                    if not (first and k == 0):
                        copy_turned(n - 1, (k - 1) % 2)
                    act.wait_ge(shifted_ready, n + 1)
                    at_least(act, turned, 2 * (n - 1))
                    for b in range(2):
                        rows = slice(64 * b, 64 * b + 64)
                        act.activation(probs[k % 2][rows, :, 64 * b:64 * b + Q], shifted[k % 2][rows].rearrange("p (h k) -> p h k", h=8),
                                       ACT.Exp, scale=SCALE).then_inc(exp_done, 1)
                    if static and t == 1:
                        act.wait_ge(w_loaded, DMA)
                        act.copy(woh[:, 2 * k:2 * k + 2, :], wo_raw[:, 2 * k:2 * k + 2, :]).then_inc(w_high, 1)
                    if k == 0 and not first:
                        at_least(act, scores_ready, t * OCTETS)
                        for r in range(4):
                            spread_keys(act, act.copy, t, 1, r)
                    if k in (1, 2) and not (static and t < 3):
                        if k == 1:
                            act.wait_ge(ffw.loaded[1 - par], (t - 2 + par) * (4 * DMA // 2))
                        for piece in ((0, 1), (2, 3))[k - 1]:
                            ffw.round(act, qk, t - 3, piece, 1 if static and t - 3 >= ffw.fc_tiles else 0)
                    if pair and k == 2:
                        act.wait_ge(y_var_ready, i)
                        root()
                        act.activation(no_use[:], y_moments[:, 0, 0:1], ACT.Exp, scale=0.0)
                    if k == 3 and not first:
                        outs_high(t - 1)

            steps(act, step)
            copy_turned(TILES * OCTETS - 1, 1)
            act.wait_ge(ffw.loaded_late, (TILES - ffw.late) * 4 * DMA)
            for n in range(4):
                ffw.round(act, qk, ffw.late + n // 4, n % 4, 1)
            act.wait_ge(y_var_ready, TILES // 2 - 1)
            root()
            outs_high(TILES - 1, last_oth)
            for n in range(4, 4 * (TILES - ffw.late)):
                ffw.round(act, qk, ffw.late + n // 4, n % 4, 1)

            def root_last(p):
                act.wait_ge(y_var_ready, TILES // 2 + p)
                act.activation(y_std[:, p:p + 1], y_moments[:, p, 1:2], ACT.Sqrt).then_inc(y_std_ready, 1)

            root_last(0)
            act.wait_ge(y_ready, TILES)
            for k in range(ffw.early):
                act.wait_ge(fc_turned, k + 1)
                act.activation(wfT[:, :, k * P:(k + 1) * P], turned_fc[k % 6][:].rearrange("p (c n) -> p c n", c=sh.DC),
                               ACT.Copy, bias=-ffw.MAGIC).then_inc(fc_copied, 1)
                if k == 2:
                    root_last(1)

        @block.vector
        def _(dve):

            def copy_turned(n, par):
                dve.wait_ge(turned, 2 * n + 2)
                dve.tensor_copy(probsT[par][:, 4:8, :], T_ps[1][:].rearrange("p (h q) -> p h q", h=4)).then_inc(turned_copied[1], 1)

            def take_outputs(n, t, k):
                dve.wait_ge(pv_ready, n + 1)
                o = O_ps[:, 0:8 * VW].rearrange("p (h e) -> p h e", h=8)
                dve.reciprocal(rsum[:], o[:, :, 32]).then_inc(sum_inverted, 1)
                dve.wait_ge(sum_inverted, n + 1)
                if k == 0:
                    at_least(dve, outs_turned, 2 * t)
                dve.tensor_tensor(outs[:, k * 256:(k + 1) * 256].rearrange("p (h e) -> p h e", h=8), o[:, :, 0:32],
                                  rsum[:].unsqueeze(2).to_broadcast((P, 8, 32)), ALU.mult).then_inc(out_taken, 1)

            def outs_low(t, oth=oth, otl=otl):
                for f in range(2):
                    dve.wait_ge(ot_high, 2 * t + f + 1)
                    dve.tensor_tensor(otl[:, 4 * f:4 * f + 4, :], A_ps[f][:].rearrange("p (c q) -> p c q", c=4),
                                      oth[:, 4 * f:4 * f + 4, :].bitcast(F32), ALU.subtract).then_inc(ot_low, 1)

            def w_out_low(k):
                dve.wait_ge(w_high, k + 1)
                chunks = slice(2 * k, 2 * k + 2)
                dve.tensor_tensor(wol[:, chunks, :], wo_raw[:, chunks, :], woh[:, chunks, :].bitcast(F32), ALU.subtract).then_inc(w_split, 1)

            def take_y(t, par):
                dve.wait_ge(y_ready, t + 1)
                at_least(dve, x_ready, t - par)
                dve.tensor_tensor(y_rows[par][:], Y_ps[:], bout_rows[:], ALU.add).then_inc(y_copied, 1)

            def see_y(t, par):
                dve.wait_ge(y_copied, t + 1)
                dve.bn_stats(y_stats[par][:], y_rows[par][:]).then_inc(stat_step, 1)

            def y_means(i):
                for p in range(2):
                    dve.bn_aggr(y_moments[:, p, :], y_stats[p][:]).then_inc(y_moved, 1)
                dve.wait_ge(y_moved, i * 2)
                dve.tensor_scalar(y_moments[:, :, 1], y_moments[:, :, 1], 1e-6, None, ALU.add).then_inc(y_var_ready, 1)

            def normalise(p):
                dve.tensor_scalar(y_rows[p][:], y_rows[p][:], y_moments[:, p, 0:1], y_rstd[:, p:p + 1], ALU.subtract, ALU.mult).then_inc(y_normed, 1)

            def norm_y(t, i):
                dve.wait_ge(y_std_ready, i)
                dve.reciprocal(y_rstd[:], y_std[:]).then_inc(y_inverted, 1)
                dve.wait_ge(y_inverted, i)
                for p in range(2):
                    normalise(p)

            def step(t, par, i):
                static = isinstance(t, int)
                first = static and t == 0
                pair = par == 0 and not (static and t < 4)
                for k in range(OCTETS):
                    n = t * OCTETS + k
                    dve.wait_ge(scores_ready, n + 1)
                    s = S_ps[k % 2][:].rearrange("p (h k) -> p h k", h=8)
                    dve.tensor_reduce(rowmax[k % 2][:], s, X, ALU.max).then_inc(max_ready, 1)
                    dve.wait_ge(max_ready, n + 1)
                    at_least(dve, exp_done, 2 * (n - 1))
                    dve.tensor_tensor(shifted[k % 2][:].rearrange("p (h k) -> p h k", h=8), s,
                                      rowmax[k % 2][:].unsqueeze(2).to_broadcast((P, 8, Q)), ALU.subtract).then_inc(shifted_ready, 1)
                    if static and t == 1 and k >= 1:
                        w_out_low(k - 1)
                        if k == 3:
                            w_out_low(3)
                            dve.wait_ge(b_loaded, 2 * DMA)
                    if k == 0 and not (static and t < 3):
                        take_y(t - 3, 1 - par)
                    if pair and k == 3:
                        norm_y(t - 4, i)
                    if not (first and k == 0):
                        copy_turned(n - 1, (k - 1) % 2)
                    if k == 0 and not (static and t < 2):
                        outs_low(t - 2)
                    if k == 1 and not (static and t < 3):
                        see_y(t - 3, 1 - par)
                    if k >= 2 and not (static and t < 3):
                        for piece in ((0, 1), (2, 3))[k - 2]:
                            dve.wait_ge(ffw.rounded, (t - 3) * 4 + piece + 1)
                            if k == 2 and piece == 1:
                                dve.wait_ge(stat_step, t - 2)
                            ffw.clip(dve, qk, t - 3, piece, ffw.clipped)
                            if pair and k == 2 and piece == 1:
                                y_means(i)
                    if k >= 2:
                        take_outputs(n - 2, t, k - 2)
                    elif not first:
                        take_outputs(n - 2, t - 1, k + 2)

            steps(dve, step)
            last = TILES * OCTETS
            take_y(TILES - 3, 1)
            outs_low(TILES - 2)
            copy_turned(last - 1, 1)
            take_outputs(last - 2, TILES - 1, 2)
            for n in range(4):
                dve.wait_ge(ffw.rounded, 4 * ffw.late + n + 1)
                ffw.clip(dve, qk, ffw.late, n, ffw.clipped)
            take_outputs(last - 1, TILES - 1, 3)
            see_y(TILES - 3, 1)
            dve.wait_ge(stat_step, TILES - 2)
            y_means(TILES // 2 - 1)

            def see_x(t):
                dve.bn_stats(x_stats[:, t, :], resid[:, t, :]).then_inc(x_seen, 1)

            def add_y(t, p):
                dve.wait_ge(y_normed, t + 1)
                dve.tensor_tensor(y_rows[p][:], y_rows[p][:], gamma_rows[:], ALU.mult).then_inc(y_added, 1)
                dve.wait_ge(y_added, 2 * (t - TILES) + 5)
                dve.tensor_tensor(resid[:, t, :], resid[:, t, :], y_rows[p][:], ALU.add).then_inc(y_added, 1)

            norm_y(TILES - 4, TILES // 2 - 1)
            dve.wait_ge(x_ready, TILES - 4)
            for t in range(TILES - 4):
                see_x(t)
            outs_low(TILES - 1, last_oth, last_otl)
            for p in range(2):
                t = TILES - 2 + p
                dve.wait_ge(x_ready, TILES - 3 + p)
                see_x(TILES - 4 + p)
                dve.wait_ge(y_ready, t + 1)
                dve.tensor_tensor(y_rows[p][:], (Y_ps, O_ps)[p][:], bout_rows[:], ALU.add).then_inc(y_copied, 1)
                see_y(t, p)
                dve.wait_ge(stat_step, t + 1)
                dve.bn_aggr(y_moments[:, p, :], y_stats[p][:]).then_inc(y_moved, 1)
                dve.wait_ge(y_moved, t + 1)
                dve.tensor_scalar(y_moments[:, p, 1:2], y_moments[:, p, 1:2], 1e-6, None, ALU.add).then_inc(y_var_ready, 1)
                dve.wait_ge(y_std_ready, TILES // 2 + p)
                dve.reciprocal(y_rstd[:, p:p + 1], y_std[:, p:p + 1]).then_inc(y_inverted, 1)
                dve.wait_ge(y_inverted, TILES // 2 + p)
                normalise(p)
                add_y(t, p)
                dve.wait_ge(y_added, 2 + 2 * p)
                see_x(t)
            dve.wait_ge(x_seen, TILES)

        @block.tensor
        def _(pe):
            def scores(n, t, par, k):
                if k % 2 == 0:
                    at_least(pe, q_taken, (t - 1) * 2 + k // 2 + 1)
                    at_least(pe, k_spread[k // 2], t * 4)
                at_least(pe, shifted_ready, n - 1)
                for g in range(2):
                    for b in range(2):
                        keys = kbd[k // 2][:, (2 * k + g) % 4, b].rearrange("p r k -> p (r k)")
                        mm = pe.matmul(S_ps[k % 2][64 * b:64 * b + 64, g * 256:(g + 1) * 256], qt[k // 2][:, (2 * k + g) % 4, 64 * b:64 * b + Q],
                                       keys, start=True, stop=True)
                mm.then_inc(scores_ready, 1)

            def turn_probs(n, par):
                pe.wait_ge(exp_done, 2 * n + 2)
                for f in range(2):
                    at_least(pe, turned_copied[f], n)
                    for h in range(4):
                        mm = pe.transpose(T_ps[f][:, h * P:(h + 1) * P], probs[par][:, 4 * f + h, :], ident[:])
                    mm.then_inc(turned, 1)

            def weighted_values(n, t, k):
                for f in range(2):
                    pe.wait_ge(turned_copied[f], n + 1)
                at_least(pe, out_taken, n)
                for h in range(8):
                    v = vals[:, bass.ds(t, 1), 8 * k + h, 0:VW].rearrange("p t e -> p (t e)")
                    mm = pe.matmul(O_ps[:, h * VW:(h + 1) * VW], probsT[k % 2][:, h, :], v, start=True, stop=True)
                mm.then_inc(pv_ready, 1)

            def turn_outs(t):
                pe.wait_ge(out_taken, (t + 1) * OCTETS)
                for f in range(2):
                    at_least(pe, ot_low, 2 * t - 1 + f)
                    for c in range(4):
                        mm = pe.transpose(A_ps[f][:, c * P:(c + 1) * P], outs[:, (4 * f + c) * P:(4 * f + c + 1) * P], ident[:])
                    mm.then_inc(outs_turned, 1)

            def project(t, part, bank=Y_ps, oth=oth, otl=otl):
                if part == 0:
                    if isinstance(t, int) and t == 0:
                        pe.wait_ge(w_split, KC // 2)
                    pe.wait_ge(ot_low, 2 * t + 2)
                    if bank is Y_ps:
                        at_least(pe, y_copied, t)
                for c in ((0, 1, 2), (3, 4), (5, 6, 7))[part]:
                    for l, r in ((oth, woh), (oth, wol), (otl, woh)):
                        mm = pe.matmul(bank[:], l[:, c, :], r[:, c, :], start=(c == 0 and l is oth and r is woh), stop=(c == KC - 1 and l is otl))
                if part == 2:
                    mm.then_inc(y_ready, 1)

            def step(t, par, i):
                first = isinstance(t, int) and t == 0
                for k in range(OCTETS):
                    n = t * OCTETS + k
                    scores(n, t, par, k)
                    if k == 2 and not first:
                        turn_outs(t - 1)
                    if k >= 2 and not (isinstance(t, int) and t < 2):
                        project(t - 2, k - 1)
                    if not (first and k == 0):
                        turn_probs(n - 1, (k - 1) % 2)
                    if k == 1 and not (isinstance(t, int) and t < 2):
                        project(t - 2, 0)
                    if k >= 2:
                        weighted_values(n - 2, t, k - 2)
                    elif not first:
                        weighted_values(n - 2, t - 1, k + 2)

            steps(pe, step)
            last = TILES * OCTETS
            turn_probs(last - 1, 1)
            weighted_values(last - 2, TILES - 1, 2)
            weighted_values(last - 1, TILES - 1, 3)
            for part in range(3):
                if part == 1:
                    turn_outs(TILES - 1)
                project(TILES - 2, part)
            for part in range(3):
                if part == 0:
                    pe.wait_ge(out_taken, last)
                project(TILES - 1, part, O_ps, last_oth, last_otl)
            pe.wait_ge(ffw.clipped, 4 * (ffw.early // 4))
            for k in range(ffw.early):
                at_least(pe, fc_copied, k - 5)
                ffw.turn_fc(pe, qk, ident, turned_fc[k % 6], k).then_inc(fc_turned, 1)
    return wfT


def feed_forward_block(nc, sh, ffw, region, resid, ident, qk, wfT, stats, b_fc, b_proj, out):
    D, TOK, TILES, DC, F = sh.D, sh.TOK, sh.TILES, sh.DC, sh.F
    FT = F // P
    R = ffw.R
    MAGIC = ffw.MAGIC
    HALF = TOK // 2
    HT = TILES // 2
    PACK = 6 * R
    K = 1024
    with ExitStack() as st:
        def sem(name):
            return st.enter_context(nc.semaphore(name))

        def psum(name):
            return st.enter_context(nc.psum_tensor(name, [P, BANK], F32))

        def at(name, shape, dtype, kib):
            return nc.alloc_sbuf_tensor_at(name, shape, dtype, offset=region + kib * K)

        hh, hl = at("hh", [P, FT, HALF], F32R, 0), at("hl", [P, FT, HALF], F32R, 32)
        wpT = at("wpT", [P, FT, D], F32R, 96)
        xh, xl = at("fxh", [P, DC, TOK], F32R, 128), at("fxl", [P, DC, TOK], F32R, 144)
        a_raw, b_raw = ffw.a_raw, ffw.b_raw
        b_pack = at("b_pack", [P, FT + DC, PACK], F32R, 156)
        tail = Arena(nc, region + 160 * K)
        xn = [tail.place(f"fxn{i}", [P, D], F32) for i in range(2)]
        bp_rows = tail.place("bp_rows", [P, D], F32)
        aT = tail.place("aT", [P, DC + FT, 2 * R], F32R)
        bfP, bpP = tail.place("bfP", [PACK, F], F32R), tail.place("bpP", [PACK, D], F32R)
        upack = [tail.place(f"upack{i}", [PACK, HALF], F32R) for i in range(2)]
        o_rows = [tail.place(f"o_rows{i}", [P, D], F32) for i in range(2)]
        bf_bias = tail.place("bf_bias", [P, FT], F32)
        moments = tail.place("fmoments", [P, TILES, 2], F32)
        std, rstd = tail.place("fstd", [P, TILES], F32), tail.place("frstd", [P, TILES], F32)
        wscale, twice = ffw.scale, ffw.twice
        assert tail.at <= 229368 - 224, tail.at

        N_ps = [psum(f"FN_ps{i}") for i in range(2)]
        W_ps = [psum(f"FW_ps{i}") for i in range(2)]
        H_ps = [psum(f"FH_ps{i}") for i in range(2)]
        U_ps = psum("FU_ps")
        turned_weights = W_ps + H_ps

        bias_loaded = sem("fbias_loaded")
        small_turned, small_copied = sem("small_turned"), sem("small_copied")
        small_high, small_split = sem("small_high"), sem("small_split")
        w_turned, w_copied = sem("w_turned"), [sem(f"w_copied{i}") for i in range(2)]
        ln_step, var_ready, std_ready, rstd_ready, xn_ready = sem("fln_step"), sem("fvar_ready"), sem("fstd_ready"), sem("frstd_ready"), sem("fxn_ready")
        xn_turned, xt_high, xt_low = sem("fxn_turned"), sem("fxt_high"), sem("fxt_low")
        u_ready, u_high, u_packed = sem("u_ready"), sem("u_high"), sem("u_packed")
        h_ready, gelu_done, h_high, h_low = sem("h_ready"), sem("gelu_done"), sem("h_high"), sem("h_low")
        bias_added, z_ready, o_ready, o_stored = sem("bias_added"), sem("z_ready"), sem("o_ready"), [sem("o_stored0"), sem("o_stored1")]

        SMALL = 1 + (FT + DC) // 4
        out_rows = out.rearrange("b q d -> (b q) d").rearrange("(t p) d -> t p d", p=P)
        block = st.enter_context(nc.Block())

        def as_chunks(ap):
            return ap.rearrange("p (c n) -> p c n", c=DC)

        @block.sync
        def _(sp):
            sp.dma_start(bp_rows[:], b_proj.partition_broadcast(P)).then_inc(bias_loaded, DMA)
            with nc.allow_non_contiguous_dma(reason="a bias of 2048 values, turned"):
                sp.dma_start(bf_bias[:], b_fc.rearrange("(t p) -> p t", p=P)).then_inc(bias_loaded, DMA)
            for t in range(TILES):
                sp.wait_ge(o_ready, t + 1)
                sp.dma_start(out_rows[t], o_rows[t % 2][:]).then_inc(o_stored[t % 2], DMA)
            for i in range(2):
                sp.wait_ge(o_stored[i], TILES // 2 * DMA)

        @block.gpsimd
        def _(pool):
            pool.wait_ge(ffw.rounded, 4 * TILES)
            for n in range(4):
                ffw.clip(pool, qk, TILES - 1, n, ffw.clipped_last)
            pool.wait_ge(bias_loaded, 2 * DMA)
            for t in range(TILES):
                pool.wait_ge(xn_ready, t + 1)
                pool.tensor_tensor(resid[:, t, :], resid[:, t, :], bp_rows[:], ALU.add).then_inc(bias_added, 1)
            for n in range(2 * FT):
                h, ft = n // FT, n % FT
                pool.wait_ge(h_high, n + 1)
                pool.tensor_tensor(hl[:, ft, :], xn[n % 2][:], hh[:, ft, :].bitcast(F32), ALU.subtract).then_inc(h_low, 1)

        EARLY = ffw.early

        def copy_weight(eng, k):
            eng.wait_ge(w_turned, k - EARLY + 1)
            bank = turned_weights[k % 4][:]
            if k < FT:
                dst, src = wfT[:, :, k * P:(k + 1) * P], as_chunks(bank)
            else:
                dst, src = wpT[:, k - FT, :], bank
            if k % 2 == 0 or k >= FT:
                eng.activation(dst, src, ACT.Copy, bias=-MAGIC).then_inc(w_copied[k % 2], 1)
            else:
                eng.tensor_scalar(dst, src, MAGIC, None, ALU.subtract).then_inc(w_copied[1], 1)

        @block.scalar
        def _(act):
            for k in range(EARLY, FT, 2):
                copy_weight(act, k)
                if k == EARLY:
                    act.wait_ge(ffw.lora_loaded, 4 * DMA)
                    act.copy(b_pack[:, :, 0:4 * R].rearrange("p t (k r) -> p t k r", k=4), b_raw[:].unsqueeze(2).to_broadcast((P, FT + DC, 4, R))).then_inc(small_high, 1)
            act.wait_ge(small_turned, 1)
            act.copy(aT[:, :, 0:R], W_ps[0][:, 0:(DC + FT) * R].rearrange("p (t r) -> p t r", r=R)).then_inc(small_high, 1)
            for k in range(1, SMALL):
                act.wait_ge(small_turned, k + 1)
                dst = bfP[:, (k - 1) * BANK:k * BANK] if k < SMALL - 1 else bpP[:]
                act.copy(dst, turned_weights[k % 4][0:PACK, :]).then_inc(small_copied, 1)

            act.wait_ge(var_ready, 1)
            act.activation(std[:], moments[:, :, 1], ACT.Sqrt).then_inc(std_ready, 1)

            def high(t):
                act.wait_ge(xn_turned, t + 1)
                act.copy(xh[:, :, t * P:(t + 1) * P], as_chunks(N_ps[t % 2][:])).then_inc(xt_high, 1)

            for t in range(TILES):
                copy_weight(act, FT + 2 * t)
                high(t)
                copy_weight(act, FT + 2 * t + 1)

            def pack(k):
                act.wait_ge(u_ready, k + 1)
                w, h = k % 2, k // 2
                rows = slice(0, 2 * R)
                at_least(act, z_ready if w else h_ready, (HT * h if w else FT * h))
                act.activation(upack[w][rows, :], U_ps[rows, :], ACT.Copy, scale=twice[rows, w:w + 1]).then_inc(u_high, 1)
                act.activation(upack[w][4 * R:6 * R, :], U_ps[rows, :], ACT.Copy, scale=twice[rows, w:w + 1]).then_inc(u_high, 1)

            act.wait_ge(bias_loaded, 2 * DMA)
            for h in range(2):
                pack(2 * h)
                for ft in range(FT):
                    n = h * FT + ft
                    act.wait_ge(h_ready, n + 1)
                    at_least(act, h_low, n - 1)
                    act.activation(xn[n % 2][:], H_ps[n % 2][:], ACT.Gelu, bias=bf_bias[:, ft:ft + 1], scale=wscale[:, 0:1]).then_inc(gelu_done, 1)
                pack(2 * h + 1)

        @block.vector
        def _(dve):
            for t in range(TILES):
                dve.bn_aggr(moments[:, t, :], stats[:, t, :]).then_inc(ln_step, 1)
            dve.wait_ge(ln_step, TILES)
            dve.tensor_scalar(moments[:, :, 1], moments[:, :, 1], 1e-5, None, ALU.add).then_inc(var_ready, 1)

            def norm(t):
                at_least(dve, xn_turned, t - 1)
                dve.tensor_scalar(xn[t % 2][:], resid[:, t, :], moments[:, t, 0:1], rstd[:, t:t + 1], ALU.subtract, ALU.mult).then_inc(xn_ready, 1)

            def low(t):
                dve.wait_ge(xt_high, t + 1)
                dve.tensor_tensor(xl[:, :, t * P:(t + 1) * P], as_chunks(N_ps[t % 2][:]), xh[:, :, t * P:(t + 1) * P].bitcast(F32), ALU.subtract).then_inc(xt_low, 1)

            for k in range(EARLY + 1, FT, 2):
                copy_weight(dve, k)
                if k == EARLY + 3:
                    dve.wait_ge(small_high, 1)
                    dve.tensor_tensor(b_pack[:, :, 4 * R:6 * R].rearrange("p t (k r) -> p t k r", k=2), b_raw[:].unsqueeze(2).to_broadcast((P, FT + DC, 2, R)),
                                      b_pack[:, :, 0:2 * R].bitcast(F32).rearrange("p t (k r) -> p t k r", k=2), ALU.subtract).then_inc(small_split, 1)
            dve.wait_ge(small_high, 2)
            dve.tensor_tensor(aT[:, :, R:2 * R], W_ps[0][:, 0:(DC + FT) * R].rearrange("p (t r) -> p t r", r=R),
                              aT[:, :, 0:R].bitcast(F32), ALU.subtract).then_inc(small_split, 1)
            dve.wait_ge(std_ready, 1)
            dve.reciprocal(rstd[:], std[:]).then_inc(rstd_ready, 1)
            dve.wait_ge(rstd_ready, 1)
            norm(0)
            norm(1)
            for t in range(TILES):
                low(t)
                if t + 2 < TILES:
                    norm(t + 2)

            def pack(k):
                dve.wait_ge(u_high, 2 * k + 2)
                w, rows = k % 2, slice(0, 2 * R)
                dve.scalar_tensor_tensor(upack[w][2 * R:4 * R, :], U_ps[rows, :], twice[rows, w:w + 1], upack[w][rows, :].bitcast(F32),
                                         ALU.mult, ALU.subtract).then_inc(u_packed, 1)

            for h in range(2):
                pack(2 * h)
                for ft in range(FT):
                    n = h * FT + ft
                    dve.wait_ge(gelu_done, n + 1)
                    dve.tensor_copy(hh[:, ft, :], xn[n % 2][:]).then_inc(h_high, 1)
                pack(2 * h + 1)
                for i in range(HT):
                    t = h * HT + i
                    dve.wait_ge(z_ready, t + 1)
                    dve.wait_ge(bias_added, t + 1)
                    at_least(dve, o_stored[t % 2], t // 2 * DMA)
                    dve.scalar_tensor_tensor(o_rows[t % 2][:], W_ps[t % 2][:], wscale[:, 1:2], resid[:, t, :], ALU.mult, ALU.add).then_inc(o_ready, 1)

        @block.tensor
        def _(pe):
            def turn_weight(k):
                at_least(pe, w_copied[k % 2], (k - EARLY) // 2 - 1)
                bank = turned_weights[k % 4]
                if k < FT:
                    mm = ffw.turn_fc(pe, qk, ident, bank, k)
                else:
                    t = 4 + (k - FT) // 4
                    if t == TILES - 1:
                        pe.wait_ge(ffw.clipped_last, 8)
                    for c in range(DC):
                        mm = pe.transpose(bank[:, c * P:(c + 1) * P], qk[:, 4 * c + k % 4, t * P:(t + 1) * P], ident[:])
                mm.then_inc(w_turned, 1)

            def turn_small():
                pe.wait_ge(ffw.lora_loaded, 4 * DMA)
                pe.wait_ge(w_copied[0], (FT - EARLY) // 2)
                pe.wait_ge(w_copied[1], (FT - EARLY) // 2)
                for c in range(DC + FT):
                    mm = pe.transpose(W_ps[0][:, c * R:(c + 1) * R], a_raw[:, c * P:(c + 1) * P], ident[0:R, 0:R])
                mm.then_inc(small_turned, 1)
                pe.wait_ge(small_split, 1)
                for k in range(1, SMALL):
                    if k == 2:
                        pe.wait_ge(small_split, 2)
                    at_least(pe, small_copied, k - 4)
                    for i in range(4):
                        mm = pe.transpose(turned_weights[k % 4][0:PACK, i * P:(i + 1) * P], b_pack[:, 4 * (k - 1) + i, :].bitcast(F32), ident[:])
                    mm.then_inc(small_turned, 1)

            for k in range(EARLY, FT):
                turn_weight(k)
            turn_small()
            pe.wait_ge(small_copied, SMALL - 1)

            def turn_norm(t):
                pe.wait_ge(xn_ready, t + 1)
                at_least(pe, xt_low, t - 1)
                for c in range(DC):
                    mm = pe.transpose(N_ps[t % 2][:, c * P:(c + 1) * P], xn[t % 2][:, c * P:(c + 1) * P], ident[:])
                mm.then_inc(xn_turned, 1)

            for t in range(TILES):
                turn_weight(FT + 2 * t)
                turn_weight(FT + 2 * t + 1)
                turn_norm(t)

            def lora(k, chunks, first, high, low, lows=0):
                at_least(pe, u_packed, k)
                for i, part in enumerate((high, low)):
                    for c in range(chunks):
                        if lows and c in (0, chunks - 1):
                            pe.wait_ge((h_high, h_low)[i], lows - (c == 0))
                        mm = pe.matmul(U_ps[0:2 * R, :], aT[:, first + c, :], part(c), start=(i == 0 and c == 0), stop=(i == 1 and c == chunks - 1))
                mm.then_inc(u_ready, 1)

            def hidden(n):
                h, ft = n // FT, n % FT
                toks, cols = slice(h * HALF, (h + 1) * HALF), slice(ft * P, (ft + 1) * P)
                at_least(pe, gelu_done, n - 1)
                for c in range(DC):
                    for k, part in enumerate((xh, xl)):
                        pe.matmul(H_ps[n % 2][:], wfT[:, c, cols], part[:, c, toks], start=(c == 0 and k == 0), stop=False)
                if ft == 0:
                    pe.wait_ge(u_packed, 2 * h + 1)
                pe.matmul(H_ps[n % 2][:], bfP[:, cols], upack[0][:], start=False, stop=True).then_inc(h_ready, 1)

            def project(t):
                h = t // HT
                toks = slice((t % HT) * P, (t % HT + 1) * P)
                at_least(pe, o_ready, t - 1)
                for ft in range(FT):
                    for k, part in enumerate((hh, hl)):
                        pe.matmul(W_ps[t % 2][:], part[:, ft, toks], wpT[:, ft, :], start=(ft == 0 and k == 0), stop=False)
                if t % HT == 0:
                    pe.wait_ge(u_packed, 2 * h + 2)
                pe.matmul(W_ps[t % 2][:], upack[1][:, toks], bpP[:], start=False, stop=True).then_inc(z_ready, 1)

            for h in range(2):
                toks = slice(h * HALF, (h + 1) * HALF)
                pe.wait_ge(xt_low, (h + 1) * HT)
                lora(2 * h, DC, 0, lambda c: xh[:, c, toks], lambda c: xl[:, c, toks])
                if h == 0:
                    for i in range(2):
                        pe.wait_ge(w_copied[i], (2 * FT - EARLY) // 2)
                for ft in range(FT):
                    hidden(h * FT + ft)
                lora(2 * h + 1, FT, DC, lambda c: hh[:, c, :], lambda c: hl[:, c, :], (h + 1) * FT)
                for i in range(HT):
                    project(h * HT + i)


def perceiver(nc, args, out):
    sh = Shapes(args["x"], args["ctx_768"], args["L0_attn_w_qkv"], args["L0_ffn_W_fc"])
    with ExitStack() as st:
        arena = Arena(nc, 16512)
        resid = arena.place("resid", [P, sh.TILES, sh.D], F32)
        ident = arena.place("ident", [P, P], F32)
        ctxsum = arena.place("ctxsum", [P, sh.B, sh.SC, sh.CC], F32)
        nansum = arena.place("nansum", [P, sh.B * 8], F32)
        a = args
        later = CrossWeights(nc, sh, st, arena, a["L0_xattn_Wv"], a["L0_xattn_bv"], a["L0_xattn_Wo"], a["L0_xattn_bo"])
        ffw = FeedForwardWeights(nc, sh, st, arena, a["L0_ffn_W_fc"], a["L0_ffn_W_proj"],
                                 (a["L0_ffn_A_fc"], a["L0_ffn_B_fc"], a["L0_ffn_A_proj"], a["L0_ffn_B_proj"]))
        x_stats = arena.place("x_stats", [P, sh.TILES, 6], F32)
        O_at = arena.at
        O_all = (arena.place("O_all", [P, sh.B, 256], F32), O_at)
        ident_ready = st.enter_context(nc.semaphore("ident_ready"))
        nc.gpsimd.memset(ident[:], 0.0).then_inc(ident_ready, 1)
        nc.gpsimd.wait_ge(ident_ready, 1)
        nc.gpsimd.affine_select(out=ident[:], in_=ident[:], compare_op=ALU.not_equal, fill=1.0, base=0,
                                pattern=[[-1, P]], channel_multiplier=1).then_inc(ident_ready, 1)
        cross_attention_block(nc, sh, later, arena, resid, ident, ident_ready, ctxsum, nansum, O_all, a["x"], a["ctx_768"], a["L0_xattn_Wq"], a["L0_xattn_bq"],
                              a["L0_xattn_Wk"], a["L0_xattn_bk"], a["L0_xattn_Wv"])
        qk, vals, taken = latent_block(nc, sh, later, ffw, arena, resid, ident, ctxsum, nansum, O_all, a["L0_attn_w_qkv"], a["L0_attn_ln_beta"])
        wfT = self_attention_block(nc, sh, ffw, later.bo_rows, O_at, resid, ident, qk, vals, taken, a["L0_attn_w_out"], a["L0_attn_b_out"],
                                   a["L0_attn_ln_gamma"], x_stats)
        feed_forward_block(nc, sh, ffw, O_at, resid, ident, qk, wfT, x_stats, a["L0_ffn_b_fc"], a["L0_ffn_b_proj"], out)


_INS = ['x', 'ctx_768', 'L0_xattn_Wq', 'L0_xattn_bq', 'L0_xattn_Wk', 'L0_xattn_bk', 'L0_xattn_Wv', 'L0_xattn_bv',
        'L0_xattn_Wo', 'L0_xattn_bo', 'L0_attn_w_qkv', 'L0_attn_w_out', 'L0_attn_b_out', 'L0_attn_ln_gamma',
        'L0_attn_ln_beta', 'L0_ffn_W_fc', 'L0_ffn_b_fc', 'L0_ffn_A_fc', 'L0_ffn_B_fc', 'L0_ffn_W_proj',
        'L0_ffn_b_proj', 'L0_ffn_A_proj', 'L0_ffn_B_proj']


def kernel(**inputs):
    import numpy as _np
    import concourse.bacc as _bacc
    from concourse import mybir as _mybir
    from concourse.bass_utils import run_bass_kernel_spmd as _run

    nc = _bacc.Bacc("TRN2", target_bir_lowering=False, num_devices=1)
    arrays, args = {}, {}
    for name in _INS:
        a = _np.ascontiguousarray(inputs[name])
        arrays[f"in_{name}_dram"] = a
        args[name] = nc.dram_tensor(f"in_{name}_dram", a.shape, _mybir.dt.from_np(a.dtype), kind="ExternalInput").ap()
    out = nc.dram_tensor("out_0_dram", (16, 64, 512), _mybir.dt.float32, kind="ExternalOutput").ap()
    perceiver(nc, args, out)
    r = _run(nc, [arrays], core_ids=[0])
    return r.results[0]["out_0_dram"]
```
